# Optimizing a Trainium2 kernel written in Bass

```python
import numpy as np
import jax
import jax.numpy as jnp

def _softmax(x, axis=-1):
    return jax.nn.softmax(x, axis=axis)

def _gelu(x):
    return jax.nn.gelu(x, approximate=True)

def _silu(x):
    return jax.nn.silu(x)

def _sigmoid(x):
    return jax.nn.sigmoid(x)

def _layernorm(x, axis=-1, eps=1e-05):
    m = jnp.mean(x, axis=axis, keepdims=True)
    v = jnp.var(x, axis=axis, keepdims=True)
    return (x - m) / jnp.sqrt(v + eps)

def _scatter_add(tgt, idx, src, axis=0):
    return tgt.at[idx].add(src)

def _segment_sum(src, seg, n):
    return jax.ops.segment_sum(src, seg, n)
kernel_name = 'mk_gnn_preln_d2_gnn_r64_9794ef'

def setup_inputs(seed: int=0):
    np.random.seed(seed)
    _w = jnp.asarray

    def _rec_inputs():
        import jax
        import jax.numpy as jnp
        _gk = jax.random.key(seed)
        x = -0.0009044 + 1 * jax.random.normal(jax.random.fold_in(_gk, 1), (100000, 32), jnp.float32)
        src = jax.random.randint(jax.random.fold_in(_gk, 2), (25000,), 0, 100000, jnp.int32)
        dst = jnp.minimum((100000 * jax.random.uniform(jax.random.fold_in(_gk, 3), (25000,)) ** 2.0).astype(jnp.int32), 99999)
        _o = jnp.argsort(dst, stable=True)
        src = src[_o]
        dst = dst[_o]
        edge_attr_10 = jax.random.uniform(jax.random.fold_in(_gk, 12), (25000, 10), jnp.float32, 0.0, 1)
        edge_attr_3 = 0.00109039 + 0.999626 * jax.random.normal(jax.random.fold_in(_gk, 13), (25000, 3), jnp.float32)
        edge_weight = jax.random.uniform(jax.random.fold_in(_gk, 15), (25000,), jnp.float32, 0.0, 0.999997)
        return (x, src, dst, edge_attr_10, edge_attr_3, edge_weight)
    x, src, dst, edge_attr_10, edge_attr_3, edge_weight = _rec_inputs()

    def _L0_gnn_setup():
        import jax, jax.numpy as jnp
        import numpy as np
        MUL = 16
        MOUT = 8
        TANH_GAIN = 1.593
        INV_SQRT3 = 0.5773502691896258
        PW_S = 0.17677669529663687
        PW_V = 0.25

        def _w3j_121():
            s2, s6 = (2 ** 0.5, 6 ** 0.5)
            M = np.zeros((5, 3, 3))
            M[0, 0, 1] = M[0, 1, 0] = 1 / s2
            M[1, 1, 2] = M[1, 2, 1] = 1 / s2
            M[2] = np.diag([-1.0, -1.0, 2.0]) / s6
            M[3, 0, 2] = M[3, 2, 0] = 1 / s2
            M[4] = np.diag([1.0, -1.0, 0.0]) / s2
            return jnp.asarray(np.transpose(M, (1, 0, 2)) / 5 ** 0.5, jnp.float32)
        W3J121 = _w3j_121()

        def _sph(edge_vec):
            n = edge_vec / jnp.linalg.norm(edge_vec, axis=1, keepdims=True)
            x, y, z = (n[:, 0], n[:, 1], n[:, 2])
            y1 = 3.0 ** 0.5 * n
            s15 = 15.0 ** 0.5
            y2 = jnp.stack([s15 * x * y, s15 * y * z, 5.0 ** 0.5 / 2 * (3 * z * z - 1), s15 * x * z, s15 / 2 * (x * x - y * y)], axis=1)
            return (y1, y2)

        def _forward(x, edge_src, edge_dst, edge_vec, emb, norm, W1, W2):
            N, E = (x.shape[0], edge_src.shape[0])
            xs = jnp.concatenate([x[edge_src, :8], x[edge_dst, :8]], axis=1)
            xv = jnp.concatenate([x[edge_src, 8:].reshape(E, 8, 3), x[edge_dst, 8:].reshape(E, 8, 3)], axis=1)
            y1, y2 = _sph(edge_vec)
            h = 2.0 ** 0.5 * jax.nn.relu(emb @ W1 / 10.0 ** 0.5)
            w = (h @ W2 / 16.0 ** 0.5).reshape(E, 7, MUL, MOUT)
            wa_s, wb_s, wa_g, wb_g, wc, wd, we = [w[:, i] for i in range(7)]
            s_out = PW_S * (jnp.einsum('eu,euw->ew', xs, wa_s) + INV_SQRT3 * jnp.einsum('eui,ei,euw->ew', xv, y1, wb_s))
            g_out = PW_S * (jnp.einsum('eu,euw->ew', xs, wa_g) + INV_SQRT3 * jnp.einsum('eui,ei,euw->ew', xv, y1, wb_g))
            v_out = PW_V * (INV_SQRT3 * jnp.einsum('eu,ek,euw->ewk', xs, y1, wc) + INV_SQRT3 * jnp.einsum('eui,euw->ewi', xv, wd) + jnp.einsum('eui,ea,iak,euw->ewk', xv, y2, W3J121, we))
            s_act = TANH_GAIN * jnp.tanh(s_out)
            gates = TANH_GAIN * jnp.tanh(g_out)
            edge_ftr = jnp.concatenate([s_act, (gates[:, :, None] * v_out).reshape(E, 24)], axis=1) * norm[:, None]
            return jax.ops.segment_sum(edge_ftr, edge_dst, num_segments=N)
        key = jax.random.key(seed)
        ks = jax.random.split(key, 8)
        N, E = (50000, 300000)
        return {'x': jax.random.normal(ks[0], (N, 32), jnp.float32), 'edge_src': jax.random.randint(ks[1], (E,), 0, N), 'edge_dst': jax.random.randint(ks[2], (E,), 0, N), 'edge_vec': jax.random.normal(ks[3], (E, 3), jnp.float32), 'emb': jax.random.uniform(ks[4], (E, 10), jnp.float32), 'norm': jax.random.uniform(ks[5], (E,), jnp.float32), 'W1': jax.random.normal(ks[6], (10, 16), jnp.float32), 'W2': jax.random.normal(ks[7], (16, 896), jnp.float32)}
    _L0_gnn_all = _L0_gnn_setup()
    _L0_gnn_in = {k: v for k, v in _L0_gnn_all.items() if k in ('W1', 'W2')}
    del _L0_gnn_all

    def _L1_gnn_setup():
        import jax, jax.numpy as jnp
        import numpy as np
        N_NODES = 50000
        N_EDGES = 12500
        FEAT = 32
        HEADS = 4
        key = jax.random.key(seed)
        ks = jax.random.split(key, 6)
        s = 1.0 / np.sqrt(FEAT)
        x = jax.random.normal(ks[0], (N_NODES, FEAT), dtype=jnp.float32)
        edge_index = jax.random.randint(ks[1], (2, N_EDGES), 0, N_NODES, dtype=jnp.int32)
        Wq = jax.random.normal(ks[2], (HEADS, FEAT, FEAT), dtype=jnp.float32) * s
        Wk = jax.random.normal(ks[3], (HEADS, FEAT, FEAT), dtype=jnp.float32) * s
        Wv = jax.random.normal(ks[4], (HEADS, FEAT, FEAT), dtype=jnp.float32) * s
        Wout = jax.random.normal(ks[5], (FEAT, FEAT), dtype=jnp.float32) * s
        return {'x': x, 'edge_index': edge_index, 'Wq': Wq, 'Wk': Wk, 'Wv': Wv, 'Wout': Wout}
    _L1_gnn_all = _L1_gnn_setup()
    _L1_gnn_in = {k: v for k, v in _L1_gnn_all.items() if k in ('Wq', 'Wk', 'Wv', 'Wout')}
    del _L1_gnn_all
    return {'x': x, 'src': src, 'dst': dst, 'edge_attr_10': edge_attr_10, 'edge_attr_3': edge_attr_3, 'edge_weight': edge_weight, 'L0_gnn_W1': _L0_gnn_in['W1'], 'L0_gnn_W2': _L0_gnn_in['W2'], 'L1_gnn_Wq': _L1_gnn_in['Wq'], 'L1_gnn_Wk': _L1_gnn_in['Wk'], 'L1_gnn_Wv': _L1_gnn_in['Wv'], 'L1_gnn_Wout': _L1_gnn_in['Wout']}

def reference(x, src, dst, edge_attr_10, edge_attr_3, edge_weight, L0_gnn_W1, L0_gnn_W2, L1_gnn_Wq, L1_gnn_Wk, L1_gnn_Wv, L1_gnn_Wout):
    import jax
    import jax.numpy as jnp

    def _L0_gnn_ref(x, edge_src, edge_dst, edge_vec, emb, norm, W1, W2):
        import jax, jax.numpy as jnp
        import numpy as np
        MUL = 16
        MOUT = 8
        TANH_GAIN = 1.593
        INV_SQRT3 = 0.5773502691896258
        PW_S = 0.17677669529663687
        PW_V = 0.25

        def _w3j_121():
            s2, s6 = (2 ** 0.5, 6 ** 0.5)
            M = np.zeros((5, 3, 3))
            M[0, 0, 1] = M[0, 1, 0] = 1 / s2
            M[1, 1, 2] = M[1, 2, 1] = 1 / s2
            M[2] = np.diag([-1.0, -1.0, 2.0]) / s6
            M[3, 0, 2] = M[3, 2, 0] = 1 / s2
            M[4] = np.diag([1.0, -1.0, 0.0]) / s2
            return jnp.asarray(np.transpose(M, (1, 0, 2)) / 5 ** 0.5, jnp.float32)
        W3J121 = _w3j_121()

        def _sph(edge_vec):
            n = edge_vec / jnp.linalg.norm(edge_vec, axis=1, keepdims=True)
            x, y, z = (n[:, 0], n[:, 1], n[:, 2])
            y1 = 3.0 ** 0.5 * n
            s15 = 15.0 ** 0.5
            y2 = jnp.stack([s15 * x * y, s15 * y * z, 5.0 ** 0.5 / 2 * (3 * z * z - 1), s15 * x * z, s15 / 2 * (x * x - y * y)], axis=1)
            return (y1, y2)

        def _forward(x, edge_src, edge_dst, edge_vec, emb, norm, W1, W2):
            N, E = (x.shape[0], edge_src.shape[0])
            xs = jnp.concatenate([x[edge_src, :8], x[edge_dst, :8]], axis=1)
            xv = jnp.concatenate([x[edge_src, 8:].reshape(E, 8, 3), x[edge_dst, 8:].reshape(E, 8, 3)], axis=1)
            y1, y2 = _sph(edge_vec)
            h = 2.0 ** 0.5 * jax.nn.relu(emb @ W1 / 10.0 ** 0.5)
            w = (h @ W2 / 16.0 ** 0.5).reshape(E, 7, MUL, MOUT)
            wa_s, wb_s, wa_g, wb_g, wc, wd, we = [w[:, i] for i in range(7)]
            s_out = PW_S * (jnp.einsum('eu,euw->ew', xs, wa_s) + INV_SQRT3 * jnp.einsum('eui,ei,euw->ew', xv, y1, wb_s))
            g_out = PW_S * (jnp.einsum('eu,euw->ew', xs, wa_g) + INV_SQRT3 * jnp.einsum('eui,ei,euw->ew', xv, y1, wb_g))
            v_out = PW_V * (INV_SQRT3 * jnp.einsum('eu,ek,euw->ewk', xs, y1, wc) + INV_SQRT3 * jnp.einsum('eui,euw->ewi', xv, wd) + jnp.einsum('eui,ea,iak,euw->ewk', xv, y2, W3J121, we))
            s_act = TANH_GAIN * jnp.tanh(s_out)
            gates = TANH_GAIN * jnp.tanh(g_out)
            edge_ftr = jnp.concatenate([s_act, (gates[:, :, None] * v_out).reshape(E, 24)], axis=1) * norm[:, None]
            return jax.ops.segment_sum(edge_ftr, edge_dst, num_segments=N)
        return _forward(x, edge_src, edge_dst, edge_vec, emb, norm, W1, W2)

    def _L1_gnn_ref(x, edge_index, Wq, Wk, Wv, Wout):
        import jax, jax.numpy as jnp
        import numpy as np
        N_NODES = 50000
        N_EDGES = 12500
        FEAT = 32
        HEADS = 4
        sender, receiver = (edge_index[0], edge_index[1])
        n, f = x.shape
        scale = f ** (-0.5)
        Q = jnp.einsum('nf,hfo->hno', x, Wq)
        K = jnp.einsum('nf,hfo->hno', x, Wk)
        V = jnp.einsum('nf,hfo->hno', x, Wv)
        s = jnp.einsum('hef,hef->eh', Q[:, receiver], K[:, sender]) * scale
        m = jax.ops.segment_max(s, receiver, num_segments=n)
        m = jnp.where(jnp.isfinite(m), m, 0.0)
        e = jnp.exp(s - m[receiver])
        denom = jax.ops.segment_sum(e, receiver, num_segments=n)
        Vs = jnp.transpose(V[:, sender], (1, 0, 2))
        num = jax.ops.segment_sum(e[..., None] * Vs, receiver, num_segments=n)
        denom_safe = jnp.where(denom > 0, denom, 1.0)
        attn = jnp.where(denom[..., None] > 0, num / denom_safe[..., None], 0.0)
        out = attn.mean(axis=1)
        return x + out @ Wout
    edge_index = jnp.stack([src, dst])
    h = jnp.maximum(_layernorm(x, axis=-1), 0.0)
    x = x + _L0_gnn_ref(h, src, dst, edge_attr_3, edge_attr_10, edge_weight, L0_gnn_W1, L0_gnn_W2)
    h = jnp.maximum(_layernorm(x, axis=-1), 0.0)
    x = x + _L1_gnn_ref(h, edge_index, L1_gnn_Wq, L1_gnn_Wk, L1_gnn_Wv, L1_gnn_Wout)
    return x

_drawn_inputs = setup_inputs


def setup_inputs(seed=0):
    import zlib

    import numpy as np

    out = dict(_drawn_inputs(seed))
    spreads = {}
    factors = {'L1_gnn_Wq': 8.0, 'L1_gnn_Wk': 8.0}
    for name, (base, spread) in spreads.items():
        noise = np.random.default_rng([zlib.crc32(name.encode()), seed]).standard_normal(out[name].shape)
        drawn = base * np.exp(spread * noise) if base else spread * noise
        out[name] = jnp.asarray(drawn.astype(out[name].dtype))
    for name, factor in factors.items():
        out[name] = (out[name] * factor).astype(out[name].dtype)
    return out
```

```python
import numpy as np
import concourse.bass as bass
from concourse import mybir
from contextlib import ExitStack

F32 = mybir.dt.float32
I32 = mybir.dt.int32
ALU = mybir.AluOpType
ACT = mybir.ActivationFunctionType
AX = mybir.AxisListType.X

P = 128
FEAT = 32
EMB = 10
HID = 16
MOUT = 8
HEADS = 4
EPS = 1e-5
TANH_GAIN = 1.593
PW_S = 0.17677669529663687
PW_V = 0.25
BIG = float(1 << 20)
FAR = 1.0e30


def build_gnn(nc, x, src, dst, attr10, attr3, weight, W1, W2, Wq, Wk, Wv, Wout, out):
    N = x.shape[0]
    E = src.shape[0]
    T = -(-E // P)
    T = -(-T // 28) * 28
    TAIL = E - (P - 1) * T
    assert 0 < TAIL <= T and T % 28 == 0

    GA = 7
    NGA = T // GA
    ITA = NGA // 2
    GB = 4
    NSB = 7
    NGB = T // GB
    ITB = NGB // NSB
    CH = 2 * FEAT + 2 * MOUT
    OUTS = 6 * MOUT
    HALF = HID // 2 * OUTS
    RPP = N // P
    DR = -(-RPP // NGA)
    DLAST = RPP - (NGA - 1) * DR
    DREM = N - P * RPP
    assert 0 < DLAST < DR and DREM <= P and NGA % 2 == 0

    agg = nc.dram_tensor("agg_rows", [N, FEAT], F32, kind="Internal").ap()

    ctx = ExitStack()
    with ctx:
        def sb(name, shape, dt=F32):
            return ctx.enter_context(nc.sbuf_tensor(name, shape, dt))

        def pb(name, cols=512):
            return ctx.enter_context(nc.psum_tensor(name, [P, cols], F32))

        def sem(name):
            return ctx.enter_context(nc.semaphore(name))

        idx = sb("idx", [P, 2, T + 28], I32)
        sidx = sb("sidx", [P, T], I32)
        fixidx = sb("fixidx", [P, 1], I32)
        dst_i = sb("dst_i", [P, T], I32)
        edge_i = sb("edge_i", [P, 2], I32)
        edge_f = sb("edge_f", [P, 2])
        dstf = sb("dstf", [P, T])
        same = sb("same", [P, T + 1])
        first_run = sb("first_run", [P, T])
        last_run = sb("last_run", [P, T])
        crossing = sb("crossing", [P, 3, FEAT])
        xsd = sb("xsd", [P, T, 2, FEAT])
        msg = sb("msg", [P, T, FEAT])
        run = sb("run", [P, T + 1, FEAT])
        back = sb("back", [P, T, FEAT])
        x1d = xsd[:, :, 1, :]
        h1d = msg
        base = run
        h1sT = back[:, :, :].rearrange("p t f -> p (t f)").rearrange("p (k e) -> p k e", e=P)
        prod = back[:, :, :].rearrange("p t f -> p (t f)")[:, 0:GA * HID * OUTS].rearrange(
            "p (t j o) -> p t j o", t=GA, o=OUTS)

        ident = sb("ident", [P, P])
        eps = sb("eps", [P, 1])
        wscale = sb("wscale", [P, 1])
        w1bd = sb("w1bd", [GA * EMB, GA * HID])
        w2r = sb("w2r", [CH, HID, OUTS])
        gbd = sb("gbd", [P, GB, P])
        ubd = sb("ubd", [P, GB, P])

        area_a = sb("features_or_scores", [P, 4 * HEADS * T])
        taken_a = {0: 0, 1: 0}

        def in_a(layer, *dims):
            n, at = int(np.prod(dims)), taken_a[layer]
            taken_a[layer] += n
            assert taken_a[layer] <= 4 * HEADS * T
            v = area_a[:, at:at + n]
            names = "abc"[:len(dims)]
            return v.rearrange(f"p ({' '.join(names)}) -> p {' '.join(names)}", **dict(zip(names, dims))) \
                if len(dims) > 1 else v

        emb = in_a(0, T, EMB)
        unit = in_a(0, T, 3)
        wn = in_a(0, T)
        score = in_a(1, HEADS, T)
        seg_f = in_a(1, HEADS, T)
        seg_b = in_a(1, HEADS, T)
        seg_m = in_a(1, HEADS, T)

        AREA = 5920
        area_b = sb("working_buffers", [P, AREA])
        taken_b = {0: 0, 1: 0}

        def in_b(layer, *dims, parts=P):
            n, at = int(np.prod(dims)), taken_b[layer]
            taken_b[layer] += n
            assert taken_b[layer] <= AREA, taken_b
            v = area_b[0:parts, at:at + n]
            names = "abcd"[:len(dims)]
            return v.rearrange(f"p ({' '.join(names)}) -> p {' '.join(names)}", **dict(zip(names, dims))) \
                if len(dims) > 1 else v

        raw = in_b(0, 2, GA, 2, FEAT)
        cen = in_b(0, GA * 2, FEAT)
        sqr = in_b(0, GA * 2, FEAT)
        pos = in_b(0, GA, 2, FEAT)
        chan = in_b(0, GA, CH)
        vprod = in_b(0, GA, 2 * MOUT, 3)
        emb_blk = in_b(0, 2, GA * EMB)
        embT = in_b(0, P, parts=GA * EMB)
        hid = in_b(0, 2, GA, HID)
        chanT = in_b(0, GA, P, parts=CH)
        outs = in_b(0, GA, OUTS)
        gate = in_b(0, 2, GA, 2 * MOUT)
        vmix = in_b(0, GA, MOUT, 3)

        agg_ring = in_b(1, NSB, GB, FEAT)
        x1s = in_b(1, NSB, GB, FEAT)
        c1s = in_b(1, NSB, GB, FEAT)
        q1s = in_b(1, NSB, GB, FEAT)
        h1s = in_b(1, NSB, GB, FEAT)
        hprod = in_b(1, GB, HEADS, FEAT)
        h1d_blk = in_b(1, P)
        h1dT = in_b(1, P)
        ytmp = in_b(1, GB, FEAT)
        yfirst = in_b(1, GB, FEAT)
        first_far = in_b(1, T)
        last_far = in_b(1, T)
        out_ring = agg_ring
        h1sT_ring = q1s
        yrow = x1s
        yrun = c1s

        idx_ring = sb("idx_ring", [P, 2, 2, GA], I32)
        sidx_ring = sb("sidx_ring", [P, 2, GA], I32)
        idx_ring_b = sb("idx_ring_b", [P, NSB, GB], I32)
        sidx_ring_b = sb("sidx_ring_b", [P, NSB, GB], I32)
        row_ring = sb("row_ring", [P, 2, GA, FEAT])
        NST = 2 * GA + DR
        stat = sb("stat", [P, 4, NST])
        stat_b = sb("stat_b", [P, NSB, 4, GB])
        xin = sb("xin", [P, 2, DR, FEAT])
        dcen = sb("dcen", [P, DR, FEAT])
        dsqr = sb("dsqr", [P, DR, FEAT])
        fixrow = sb("fixrow", [P, FEAT])
        same_far = sb("same_far", [P, T + 1])

        flagT = sb("flagT", [FEAT, 3, P])
        keepT = sb("keepT", [FEAT, 2, P])
        farT = sb("farT", [FEAT, 4, P])
        ends = sb("ends", [P, 2, FEAT])
        endT = sb("endT", [FEAT, 2, P])
        carryT = sb("carryT", [FEAT, 2, P])
        carry = sb("carry", [P, 2, FEAT])

        back_flat = back[:, :, :].rearrange("p t f -> p (t f)")
        w2a = back_flat[0:CH, 0:HID * OUTS].rearrange("p (j o) -> p j o", o=OUTS)
        w2b = back_flat[0:CH, HID * OUTS:HID * OUTS * 3 // 2].rearrange("p (j o) -> p j o", o=OUTS // 2)
        msg_flat = msg[:, :, :].rearrange("p t f -> p (t f)")
        ZR = 28
        zeros = xsd[:, T - ZR // 2:T, :, :].rearrange("p t s f -> p (t s f)")
        wtop = T * FEAT
        wqk = msg_flat[:, wtop - 96:wtop].rearrange("p (a f) -> p a f", a=3)
        wqkvT = msg_flat[0:FEAT, wtop - 512:wtop - 128].rearrange("p (a e) -> p a e", a=3)
        wout = msg_flat[0:FEAT, wtop - 128:wtop - 96]
        gu = msg_flat[0:FEAT, wtop - 768:wtop - 512].rearrange("p (a e) -> p a e", a=2)

        small = pb("small")
        turnA = pb("turnA")
        turnB = pb("turnB")
        tens = [pb("tens0", 1024), pb("tens1", 1024)]
        spare = pb("spare")

        s_pad = sem("pads_set")
        s_edges = sem("edges_loaded")
        s_feat = sem("edge_features_loaded")
        s_wz = sem("weight_buffers_zeroed")
        s_wl = sem("weights_loaded")
        s_w2 = sem("w2_built")
        s_wT = sem("attention_weights_turned")
        s_wTs = sem("turned_weights_on_sbuf")
        s_gps = sem("folded_weights_ready")
        s_gsb = sem("folded_weights_on_sbuf")
        s_gbd = sem("block_weights_loaded")
        s_flags = sem("partition_flags_ready")
        s_id0 = sem("identity_zeroed")
        s_id = sem("identity_ready")
        s_zset = sem("zeros_set")
        s_zfill = sem("agg_rows_zeroed")
        s_idx = sem("indices_ready")
        s_const = sem("act_constants_ready")
        s_vsq = sem("vector_norms_summed")
        s_vstd = sem("vector_norms_ready")
        s_cross = sem("crossing_flags_ready")
        s_crossT = sem("crossing_flags_turned")
        s_istg = sem("indices_staged")
        s_pool = sem("pool_steps")
        s_gath = [sem("rows_gathered0"), sem("rows_gathered1")]
        s_rawd = sem("raw_read_by_vector")
        s_rawa = sem("raw_read_by_scalar")
        s_cen = sem("centred")
        s_sq = sem("squared")
        s_var = sem("variance_summed")
        s_std = sem("deviation_ready")
        s_chan = sem("channels_ready")
        s_embB = sem("emb_block_staged")
        s_embT = sem("emb_turned")
        s_embS = sem("emb_on_sbuf")
        s_hps = sem("hidden_product_ready")
        s_hid = sem("hidden_ready")
        s_turn = sem("channels_turned")
        s_turned = sem("turned_channels_on_sbuf")
        s_tens = sem("tensor_product_ready")
        s_tfree = sem("tensor_product_read")
        s_outs = sem("outputs_summed")
        s_tanh = sem("gates_ready")
        s_run = sem("running_sums_ready")
        s_rows = sem("scatter_rows_staged")
        s_rfree = sem("scatter_ring_free")
        s_scat = sem("agg_rows_scattered")
        s_xl = [sem("dense_rows_loaded0"), sem("dense_rows_loaded1")]
        s_ddone = sem("dense_rows_ready")
        s_dst = sem("dense_rows_stored")
        s_ends = sem("segment_ends_ready")
        s_endT = sem("segment_ends_turned")
        s_carT = sem("carries_scanned")
        s_car = sem("carries_ready")
        s_fix = sem("fix_rows_ready")
        s_fixd = sem("fix_rows_scattered")
        s_hdB = sem("dst_block_staged")
        s_hvB = sem("values_block_staged")
        s_hdT = sem("dst_rows_turned")
        s_hdS = sem("turned_dst_rows_on_sbuf")
        s_h1d = sem("dst_h_ready")
        s_dc = sem("dst_centred")
        s_dq = sem("dst_squared")
        s_dv = sem("dst_variance_summed")
        s_dd = sem("dst_deviation_ready")
        s_istgb = sem("src_indices_staged")
        s_gb = [sem(f"agg_gathered{s}") for s in range(NSB)]
        s_agread = sem("agg_ring_read")
        s_bc = sem("src_centred")
        s_bq = sem("src_squared")
        s_bv = sem("src_variance_summed")
        s_bd = sem("src_deviation_ready")
        s_bh = sem("src_h_ready")
        s_hsT = sem("src_rows_turned")
        s_hsS = sem("turned_src_rows_on_sbuf")
        s_q = sem("query_ready")
        s_qfree = sem("query_read")
        s_sm = sem("max_subtracted")
        s_e = sem("exponentials_ready")
        s_attn = sem("attention_ready")
        s_v = sem("values_ready")
        s_vfree = sem("values_read")
        s_vused = sem("value_blocks_used")
        s_orow = sem("output_rows_ready")
        s_sstg = sem("output_indices_staged")
        s_ofree = sem("output_ring_free")
        s_osc = [sem(f"output_rows_scattered{s}") for s in range(NSB)]
        s_last = sem("last_rows_scattered")
        s_hold = {e: sem(f"held_{e}") for e in ("act", "dve", "pe", "pool", "sp")}

        def hold(eng, name, *waits):
            for s, v in waits:
                eng.wait_ge(s, v)
            eng.sem_inc(s_hold[name], 1)

        def full(ap, dims):
            return ap.to_broadcast(dims)

        block = ctx.enter_context(nc.Block())

        def edge_loads(eng, dest, source, s):
            w = 1 if len(source.shape) == 1 else source.shape[1]
            flat = source if w == 1 else source.rearrange("e c -> (e c)")
            for a, b in ((0, 112), (112, P - 1)):
                v = flat[a * T * w:b * T * w].rearrange("(p n) -> p n", p=b - a)
                eng.dma_start(dest[a:b, 0:T * w], v).then_inc(s, 16)
            v = flat[(P - 1) * T * w:E * w].rearrange("(p n) -> p n", p=1)
            eng.dma_start(dest[P - 1:P, 0:TAIL * w], v).then_inc(s, 16)
            return 48

        ZC = N // (P * ZR)
        ZREST = (N - ZC * P * ZR) // P
        ZREM = N - ZC * P * ZR - P * ZREST
        N_LOADS = GA + 2 * (3 + 2 * 3) + 3 + 3 + 1

        @block.sync
        def _(sp):
            sp.wait_ge(s_pad, 1)
            edge_loads(sp, dst_i[:, :], dst, s_edges)
            edge_loads(sp, idx[:, 0, :], src, s_edges)
            border = dst[0:(P - 1) * T].rearrange("(p n) -> p n", n=T)[:, T - 1:T]
            sp.dma_start(edge_i[1:P, 0:1], border, allow_slow_non_contiguous=True).then_inc(s_edges, 16)
            border = dst[T:(P - 1) * T].rearrange("(p n) -> p n", n=T)[:, 0:1]
            sp.dma_start(edge_i[0:P - 2, 1:2], border, allow_slow_non_contiguous=True).then_inc(s_edges, 16)
            sp.dma_start(edge_i[P - 2:P - 1, 1:2],
                         dst[(P - 1) * T:(P - 1) * T + 1].rearrange("(p n) -> p n", n=1)).then_inc(s_edges, 16)
            edge_loads(sp, unit[:, :, :].rearrange("p t c -> p (t c)"), attr3, s_feat)
            edge_loads(sp, wn, weight, s_feat)
            edge_loads(sp, emb[:, :, :].rearrange("p t c -> p (t c)"), attr10, s_feat)
            xrows = x[0:P * RPP, :].rearrange("(p r) f -> p (r f)", p=P)
            orows = out[0:P * RPP, :].rearrange("(p r) f -> p (r f)", p=P)

            def chunk(ap, g, n):
                if isinstance(g, int):
                    return ap[:, g * DR * FEAT:(g * DR + n) * FEAT]
                return ap[:, bass.ds(g * (DR * FEAT), n * FEAT)]

            def slot(b, n):
                return xin[:, b, 0:n, :].rearrange("p r f -> p (r f)")

            for b in range(2):
                sp.dma_start(slot(b, DR), chunk(xrows, b, DR)).then_inc(s_xl[b], 16)
            sp.wait_ge(s_zset, 1)
            sp.dma_start(agg[0:ZC * P * ZR, :].rearrange("(c p a) f -> p c (a f)", c=ZC, p=P),
                         zeros[:, None, :].to_broadcast([P, ZC, ZR * FEAT])).then_inc(s_zfill, 16)
            sp.dma_start(agg[ZC * P * ZR:ZC * P * ZR + P * ZREST, :].rearrange("(p a) f -> p (a f)", p=P),
                         zeros[:, 0:ZREST * FEAT]).then_inc(s_zfill, 16)
            sp.dma_start(agg[N - ZREM:N, :], zeros[0:ZREM, 0:FEAT]).then_inc(s_zfill, 16)

            def store(g, b, n):
                hold(sp, "sp", (s_ddone, g + 1))
                sp.dma_start(chunk(orows, g, n), slot(b, n)).then_inc(s_dst, 16)

            with sp.Fori(0, ITA - 2) as i:
                for b in range(2):
                    g = i * 2 + b
                    store(g, b, DR)
                    hold(sp, "sp", (s_dst, (g + 1) * 16))
                    sp.dma_start(slot(b, DR), chunk(xrows, g + 2, DR)).then_inc(s_xl[b], 16)
            store(NGA - 4, 0, DR)
            sp.wait_ge(s_dst, (NGA - 3) * 16)
            sp.dma_start(slot(0, DR), chunk(xrows, NGA - 2, DR)).then_inc(s_xl[0], 16)
            store(NGA - 3, 1, DR)
            sp.wait_ge(s_dst, (NGA - 2) * 16)
            sp.dma_start(slot(1, DLAST), chunk(xrows, NGA - 1, DLAST)).then_inc(s_xl[1], 16)
            sp.dma_start(xin[0:DREM, 1, DLAST, :], x[P * RPP:N, :]).then_inc(s_xl[1], 16)
            store(NGA - 2, 0, DR)
            store(NGA - 1, 1, DLAST)
            sp.dma_start(out[P * RPP:N, :], xin[0:DREM, 1, DLAST, :]).then_inc(s_dst, 16)
            sp.wait_ge(s_dst, (NGA + 1) * 16)

        @block.gpsimd
        def _(pool):
            nc.gpsimd.memset(ident[:], 0.0).then_inc(s_id0, 1)
            pool.wait_ge(s_id0, 1)
            nc.gpsimd.affine_select(out=ident[:], in_=ident[:], compare_op=ALU.not_equal, fill=1.0, base=0,
                                    pattern=[[-1, P]], channel_multiplier=1).then_inc(s_id, 1)

            def gathers(g, b):
                hold(pool, "pool", (s_istg, g + 1), (s_rawd, g + 1), (s_rawa, g + 1))
                for t in range(GA):
                    for side in range(2):
                        nc.gpsimd.indirect_dma_start(
                            raw[:, b, t, side, :], None, x,
                            bass.IndirectOffsetOnAxis(ap=idx_ring[:, b, side, t:t + 1], axis=0)
                        ).then_inc(s_gath[b], 16)

            def scatters(g, b):
                hold(pool, "pool", (s_rows, g + 1))
                for t in range(GA):
                    nc.gpsimd.indirect_dma_start(
                        agg, bass.IndirectOffsetOnAxis(ap=sidx_ring[:, b, t:t + 1], axis=0),
                        row_ring[:, b, t, :], None, bounds_check=N - 1, oob_is_err=False
                    ).then_inc(s_scat, 16)

            def scattered(g):
                pool.wait_ge(s_scat, (g + 1) * (16 * GA))
                pool.sem_inc(s_rfree, 1)

            pool.sem_inc(s_rfree, 2)
            for g in range(4):
                gathers(g, g % 2)
            pool.wait_ge(s_zfill, 48)
            with pool.Fori(2, ITA) as i:
                for b in range(2):
                    g = i * 2 + b
                    gathers(g, b)
                    scatters(g - 4, b)
                    scattered(g - 4)
            for g in range(NGA - 4, NGA):
                scatters(g, g % 2)
                scattered(g)
            pool.wait_ge(s_fix, 1)
            nc.gpsimd.indirect_dma_start(agg, bass.IndirectOffsetOnAxis(ap=fixidx[:, 0:1], axis=0),
                                         fixrow[:], None, bounds_check=N - 1, oob_is_err=False
                                         ).then_inc(s_fixd, 16)
            pool.wait_ge(s_fixd, 16)

            with pool.Fori(0, ITB) as i:
                for s in range(NSB):
                    k = i * NSB + s
                    hold(pool, "pool", (s_istgb, k + 1), (s_agread, k + 1))
                    for t in range(GB):
                        nc.gpsimd.indirect_dma_start(
                            agg_ring[:, s, t, :], None, agg,
                            bass.IndirectOffsetOnAxis(ap=idx_ring_b[:, s, t:t + 1], axis=0)
                        ).then_inc(s_gb[s], 16)

            pool.wait_ge(s_dst, (NGA + 1) * 16)
            pool.sem_inc(s_ofree, NSB)

            def out_scatters(i, first):
                for s in range(NSB):
                    k = i * NSB + s
                    if not first:
                        pool.wait_ge(s_osc[s], i * (16 * GB))
                        pool.sem_inc(s_ofree, 1)
                    hold(pool, "pool", (s_orow, k + 1), (s_sstg, k + 1))
                    for t in range(GB):
                        nc.gpsimd.indirect_dma_start(
                            out, bass.IndirectOffsetOnAxis(ap=sidx_ring_b[:, s, t:t + 1], axis=0),
                            out_ring[:, s, t, :], None, bounds_check=N - 1, oob_is_err=False
                        ).then_inc(s_osc[s], 16)

            out_scatters(0, True)
            with pool.Fori(1, ITB) as i:
                out_scatters(i, False)
            pool.wait_ge(s_fix, 2)
            nc.gpsimd.indirect_dma_start(out, bass.IndirectOffsetOnAxis(ap=fixidx[:, 0:1], axis=0),
                                         fixrow[:], None, bounds_check=N - 1, oob_is_err=False
                                         ).then_inc(s_last, 16)
            for s in range(NSB):
                pool.wait_ge(s_osc[s], ITB * 16 * GB)
            pool.wait_ge(s_last, 16)

        @block.scalar
        def _(act):
            act.wait_ge(s_wz, 1)
            loads = []

            def load(dest, source):
                act.dma_start(dest, source).then_inc(s_wl, 16)
                loads.append(1)

            for t in range(GA):
                load(w1bd[t * EMB:(t + 1) * EMB, t * HID:(t + 1) * HID], W1)
            w2v = W2.rearrange("j (i u w) -> i u j w", i=7, w=MOUT)
            WA_S, WB_S, WA_G, WB_G, WC, WD, WE = range(7)
            for side in range(2):
                u = slice(side * MOUT, (side + 1) * MOUT)
                at = side * FEAT
                for col, which in ((0, WA_S), (1, WA_G), (2, WC)):
                    load(w2a[at:at + MOUT, :, col * MOUT:(col + 1) * MOUT], w2v[which, u])
                for k in range(3):
                    rows = slice(at + MOUT + k, at + FEAT, 3)
                    load(w2a[rows, :, (3 + k) * MOUT:(4 + k) * MOUT], w2v[WD, u])
                    load(w2b[rows, :, k * MOUT:(k + 1) * MOUT], w2v[WE, u])
            for col, which in ((0, WB_S), (1, WB_G), (2, WE)):
                load(w2a[2 * FEAT:CH, :, col * MOUT:(col + 1) * MOUT], w2v[which])
            for a, w in enumerate((Wq, Wk, Wv)):
                load(wqk[:, a, :], w.rearrange("h f o -> (h f) o"))
            load(wout, Wout)
            assert len(loads) == N_LOADS

            def stage_indices(g, b):
                return nc.scalar.copy(idx_ring[:, b, :, :],
                                      idx[:, :, g * GA:(g + 1) * GA] if isinstance(g, int)
                                      else idx[:, :, bass.ds(g * GA, GA)]).then_inc(s_istg, 1)

            act.wait_ge(s_idx, 1)
            stage_indices(0, 0)
            stage_indices(1, 1)
            act.sem_inc(s_rawa, 2)

            act.wait_ge(s_vsq, 1)
            nc.scalar.activation(same_far[:, 0:T], dstf[:, :], ACT.Sqrt).then_inc(s_vstd, 1)

            act.wait_ge(s_wT, 1)
            nc.scalar.copy(wqkvT, turnA[0:FEAT, 0:3 * P].rearrange("p (a e) -> p a e", a=3)).then_inc(s_wTs, 1)
            act.wait_ge(s_gps, 1)
            nc.scalar.activation(gu[:, 0, :], turnB[0:FEAT, 0:P], ACT.Copy, scale=float(FEAT) ** -0.5)
            nc.scalar.activation(gu[:, 1, :], turnB[0:FEAT, P:2 * P], ACT.Copy,
                                 scale=1.0 / HEADS).then_inc(s_gsb, 1)
            act.wait_ge(s_gsb, 1)
            for t in range(GB):
                act.dma_start(gbd[t * FEAT:(t + 1) * FEAT, t, :], gu[:, 0, :]).then_inc(s_gbd, 16)
                act.dma_start(ubd[t * FEAT:(t + 1) * FEAT, t, :], gu[:, 1, :]).then_inc(s_gbd, 16)

            def cols(ap, start, n, axis_len=None):
                return ap[:, start:start + n] if isinstance(start, int) else ap[:, bass.ds(start, n)]

            def take_rows(g, b, turn):
                nc.scalar.copy(emb_blk[:, b].rearrange("p (t c) -> p t c", c=EMB),
                               cols(emb, g * GA, GA)).then_inc(s_embB, 1)
                hold(act, "act", (s_gath[b], turn * (16 * 2 * GA)))
                nc.scalar.copy(cols(xsd, g * GA, GA), raw[:, b]).then_inc(s_rawa, 1)
                stage_indices(g + 2, b)

            def squares(n, gathered, dense):
                act.wait_ge(s_cen, n)
                if gathered:
                    nc.scalar.activation(pos, cen.rearrange("p (t s) f -> p t s f", s=2), ACT.Relu)
                    last = nc.scalar.activation(sqr, cen, ACT.Square)
                if dense:
                    last = nc.scalar.activation(dsqr[:], dcen[:], ACT.Square)
                last.then_inc(s_sq, 1)

            def deviation(n):
                act.wait_ge(s_var, n)
                nc.scalar.activation(stat[:, 2, :], stat[:, 1, :], ACT.Sqrt, bias=eps[:, 0:1],
                                     scale=1.0 / FEAT).then_inc(s_std, 1)

            def hidden(g, b):
                act.wait_ge(s_embT, g + 1)
                nc.scalar.copy(embT, small[0:GA * EMB, 0:P]).then_inc(s_embS, 1)
                act.wait_ge(s_hps, g + 1)
                nc.scalar.activation(hid[:, b].rearrange("p t j -> p (t j)"), small[:, P:P + GA * HID], ACT.Relu,
                                     scale=2.0 ** 0.5 / (4 * EMB ** 0.5)).then_inc(s_hid, 1)
                act.wait_ge(s_turn, g * 2 + 1)
                nc.scalar.copy(chanT[:, 0:4, :].rearrange("c t e -> c (t e)"), turnA[0:CH, :]).then_inc(s_turned, 1)
                act.wait_ge(s_turn, g * 2 + 2)
                nc.scalar.copy(chanT[:, 4:GA, :].rearrange("c t e -> c (t e)"),
                               turnB[0:CH, 0:(GA - 4) * P]).then_inc(s_turned, 1)

            def gates(g):
                act.wait_ge(s_outs, g + 1)
                nc.scalar.activation(gate[:, 0], outs[:, :, 0:2 * MOUT], ACT.Tanh).then_inc(s_tanh, 1)

            def stage_rows(g, b):
                hold(act, "act", (s_run, g + 1), (s_rfree, g + 1))
                nc.scalar.copy(row_ring[:, b], cols(run, g * GA + 1, GA))
                nc.scalar.copy(sidx_ring[:, b], cols(sidx, g * GA, GA)).then_inc(s_rows, 1)

            take_rows(0, 0, 1)
            squares(1, True, False)
            deviation(1)
            hidden(0, 0)

            def layer0(i, b, last):
                g = i * 2 + b
                if not last:
                    take_rows(g + 1, 1 - b, i + 1 + b)
                squares(g + 2, not last, True)
                deviation(g + 2)
                if not last:
                    hidden(g + 1, 1 - b)
                gates(g)
                stage_rows(g, b)

            with act.Fori(0, ITA - 1) as i:
                for b in range(2):
                    layer0(i, b, False)
            layer0(ITA - 1, 0, False)
            layer0(ITA - 1, 1, True)

            act.wait_ge(s_dc, 1)
            nc.scalar.activation(back[:], msg[:], ACT.Square).then_inc(s_dq, 1)
            act.wait_ge(s_dv, 1)
            nc.scalar.activation(seg_f[:, 2, :], seg_f[:, 1, :], ACT.Sqrt, bias=eps[:, 0:1],
                                 scale=1.0 / FEAT).then_inc(s_dd, 1)

            def stage_src(k, s):
                return nc.scalar.copy(idx_ring_b[:, s, :],
                                      idx[:, 0, k * GB:(k + 1) * GB] if isinstance(k, int)
                                      else idx[:, 0, bass.ds(k * GB, GB)]).then_inc(s_istgb, 1)

            for s in range(NSB):
                stage_src(s, s)

            def sources(i, s, turn):
                k = i * NSB + s
                hold(act, "act", (s_gb[s], turn * (16 * GB)))
                stage_src(k + NSB, s)
                act.wait_ge(s_bc, k + 1)
                nc.scalar.activation(q1s[:, s], c1s[:, s], ACT.Square).then_inc(s_bq, 1)

            def stage_dst(k):
                return nc.scalar.copy(h1d_blk.rearrange("p (t f) -> p t f", f=FEAT),
                                      cols(h1d, k * GB, GB)).then_inc(s_hdB, 1)

            act.wait_ge(s_h1d, 1)
            stage_dst(0)
            sources(0, 0, 1)

            def layer1(i, s, last):
                k = i * NSB + s
                act.wait_ge(s_hdT, k + 1)
                nc.scalar.copy(h1dT, turnA[:, 0:P]).then_inc(s_hdS, 1)
                if not last:
                    stage_dst(k + 1)
                    if s + 1 < NSB:
                        sources(i, s + 1, i + 1)
                    else:
                        sources(i + 1, 0, i + 2)
                act.wait_ge(s_bv, k + 1)
                nc.scalar.activation(stat_b[:, s, 2, :], stat_b[:, s, 1, :], ACT.Sqrt, bias=eps[:, 0:1],
                                     scale=1.0 / FEAT).then_inc(s_bd, 1)
                hold(act, "act", (s_hsT, k + 1))
                nc.scalar.copy(h1sT[:, k, :] if isinstance(k, int) else h1sT[:, bass.ds(k, 1), :],
                               turnB[:, 0:P] if isinstance(k, int) else turnB[:, None, 0:P]).then_inc(s_hsS, 1)

            with act.Fori(0, ITB - 1) as i:
                for s in range(NSB):
                    layer1(i, s, False)
            for s in range(NSB):
                layer1(ITB - 1, s, s == NSB - 1)

            act.wait_ge(s_sm, 1)
            nc.scalar.activation(seg_m, seg_b, ACT.Exp).then_inc(s_e, 1)

            with act.Fori(0, ITB) as i:
                for s in range(NSB):
                    k = i * NSB + s
                    hold(act, "act", (s_vused, k + 1))
                    nc.scalar.copy(h1sT_ring[:, s:s + 1].rearrange("p s t f -> p s (t f)"),
                                   h1sT[:, bass.ds(k, 1), :]).then_inc(s_hvB, 1)
                    hold(act, "act", (s_ofree, k + 1))
                    nc.scalar.copy(sidx_ring_b[:, s, :], sidx[:, bass.ds(k * GB, GB)]).then_inc(s_sstg, 1)

        @block.tensor
        def _(pe):
            pe.wait_ge(s_id, 1)
            pe.wait_ge(s_wl, 16 * N_LOADS)
            for a in range(3):
                mm = nc.tensor.transpose(turnA[0:FEAT, a * P:(a + 1) * P], wqk[:, a, :], ident[:])
            mm.then_inc(s_wT, 1)
            pe.wait_ge(s_wTs, 1)
            for h in range(HEADS):
                w = slice(h * FEAT, (h + 1) * FEAT)
                nc.tensor.matmul(turnB[0:FEAT, w], wqkvT[:, 0, w], wqkvT[:, 1, w], start=True, stop=True)
                mm = nc.tensor.matmul(turnB[0:FEAT, P + h * FEAT:P + (h + 1) * FEAT], wqkvT[:, 2, w], wout,
                                      start=True, stop=True)
            mm.then_inc(s_gps, 1)
            pe.wait_ge(s_cross, 1)
            for a in range(3):
                mm = nc.tensor.transpose(small[0:FEAT, a * P:(a + 1) * P], crossing[:, a, :], ident[:])
            mm.then_inc(s_crossT, 1)
            pe.wait_ge(s_flags, 1)
            pe.wait_ge(s_gsb, 1)
            pe.wait_ge(s_feat, 16 * 9)
            pe.wait_ge(s_w2, 1)

            def prepare(g, b):
                if not (isinstance(g, int) and g == 0):
                    pe.wait_ge(s_hid, g)
                pe.wait_ge(s_embB, g + 1)
                nc.tensor.transpose(small[0:GA * EMB, 0:P], emb_blk[:, b], ident[:]).then_inc(s_embT, 1)
                pe.wait_ge(s_embS, g + 1)
                nc.tensor.matmul(small[:, P:P + GA * HID], embT, w1bd[:], start=True, stop=True).then_inc(s_hps, 1)
                pe.wait_ge(s_chan, g + 1)
                for t in range(GA):
                    bank = turnA if t < 4 else turnB
                    mm = nc.tensor.transpose(bank[0:CH, (t % 4) * P:(t % 4 + 1) * P], chan[:, t, :], ident[:])
                    if t in (3, GA - 1):
                        mm.then_inc(s_turn, 1)

            def products(g, b):
                for t in range(GA):
                    n = g * GA + t
                    if t == 0:
                        pe.wait_ge(s_turned, g * 2 + 1)
                    if t == 4:
                        pe.wait_ge(s_turned, g * 2 + 2)
                    pe.wait_ge(s_tfree, n + 1)
                    bank = tens[(b + t) % 2]
                    for half in range(2):
                        mm = nc.tensor.matmul(bank[:, half * 512:half * 512 + HALF], chanT[:, t, :],
                                              w2r[:, half * (HID // 2):(half + 1) * (HID // 2), :].rearrange(
                                                  "c j o -> c (j o)"), start=True, stop=True)
                    mm.then_inc(s_tens, 1)

            prepare(0, 0)
            with pe.Fori(0, ITA - 1) as i:
                for b in range(2):
                    products(i * 2 + b, b)
                    prepare(i * 2 + b + 1, 1 - b)
            products(NGA - 2, 0)
            prepare(NGA - 1, 1)
            products(NGA - 1, 1)

            def cross(n, done):
                pe.wait_ge(s_ends, done + 1)
                nc.tensor.transpose(small[0:n, 0:P], ends[:, 0, 0:n], ident[:])
                nc.tensor.transpose(small[0:n, P:2 * P], ends[:, 1, 0:n], ident[:]).then_inc(s_endT, 1)
                pe.wait_ge(s_carT, done + 1)
                nc.tensor.transpose(small[:, 2 * P:2 * P + n], carryT[0:n, 0, :], ident[0:n, 0:n])
                nc.tensor.transpose(small[:, 2 * P + FEAT:2 * P + FEAT + n], carryT[0:n, 1, :],
                                    ident[0:n, 0:n]).then_inc(s_car, 1)

            cross(FEAT, 0)

            pe.wait_ge(s_h1d, 1)
            pe.wait_ge(s_gbd, 16 * 2 * GB)
            pe.wait_ge(s_dd, 1)
            with pe.Fori(0, ITB) as i:
                for s in range(NSB):
                    k = i * NSB + s
                    hold(pe, "pe", (s_qfree, k + 1))
                    pe.wait_ge(s_hdB, k + 1)
                    nc.tensor.transpose(turnA[:, 0:P], h1d_blk, ident[:]).then_inc(s_hdT, 1)
                    pe.wait_ge(s_hdS, k + 1)
                    nc.tensor.matmul(tens[s % 2][:, 0:GB * P], h1dT, gbd[:, :, :].rearrange("p t e -> p (t e)"),
                                     start=True, stop=True).then_inc(s_q, 1)
                    pe.wait_ge(s_bh, k + 1)
                    nc.tensor.transpose(turnB[:, 0:P], h1s[:, s].rearrange("p t f -> p (t f)"),
                                        ident[:]).then_inc(s_hsT, 1)

            cross(HEADS, 1)
            cross(HEADS, 2)

            pe.wait_ge(s_hsS, NGB)
            with pe.Fori(0, ITB) as i:
                for s in range(NSB):
                    k = i * NSB + s
                    hold(pe, "pe", (s_vfree, k + 1), (s_hvB, k + 1))
                    nc.tensor.matmul(tens[s % 2][:, 0:GB * P], h1sT_ring[:, s].rearrange("p t f -> p (t f)"),
                                     ubd[:, :, :].rearrange("p t e -> p (t e)"),
                                     start=True, stop=True).then_inc(s_v, 1)
            cross(FEAT, 3)

        @block.vector
        def _(dve):
            v = nc.vector

            def cols(ap, start, n):
                return ap[:, start:start + n] if isinstance(start, int) else ap[:, bass.ds(start, n)]

            def spread(ap, axis, dims):
                full = [slice(None)] * (len(ap.shape) + 1)
                full[axis] = None
                return ap[tuple(full)].to_broadcast(dims)

            q = slice(96, P)
            v.memset(idx[:], 0)
            v.memset(edge_i[:], -1)
            v.memset(dst_i[q, TAIL:T], int(BIG))
            v.memset(unit[q, TAIL:T, :], 1.0)
            v.memset(wn[q, TAIL:T], 0.0)
            v.memset(emb[q, TAIL:T, :], 0.0).then_inc(s_pad, 1)
            v.memset(zeros, 0.0).then_inc(s_zset, 1)
            v.memset(w1bd[:], 0.0)
            v.memset(w2a, 0.0)
            v.memset(w2b, 0.0)
            v.memset(gbd[:], 0.0)
            v.memset(ubd[:], 0.0).then_inc(s_wz, 1)
            v.memset(run[:, 0, :], 0.0)
            v.memset(eps[:], EPS)
            v.memset(same[:], 0.0)
            v.memset(stat[:], 1.0)
            v.memset(keepT[:], 0.0)
            v.memset(endT[:], 0.0)
            v.memset(wscale[:], PW_V)
            v.drain()
            v.memset(wscale[2 * FEAT:CH], 1.5 ** 0.5 * PW_V)

            dve.wait_ge(s_edges, 16 * 9)
            v.tensor_copy(dstf[:], dst_i[:])
            v.tensor_copy(edge_f[:], edge_i[:])
            v.drain()
            v.tensor_scalar(idx[:, 1, 0:T], dstf[:], float(N - 1), None, ALU.min).then_inc(s_idx, 1)

            v.tensor_tensor(same[:, 1:T], dstf[:, 1:T], dstf[:, 0:T - 1], ALU.is_equal)
            v.tensor_scalar(first_run[:], dstf[:], dstf[:, 0:1], None, ALU.is_equal)
            v.tensor_scalar(last_run[:], dstf[:], dstf[:, T - 1:T], None, ALU.is_equal)
            v.tensor_tensor(crossing[:, 0, 0:1], edge_f[:, 0:1], dstf[:, 0:1], ALU.is_equal)
            v.tensor_tensor(crossing[:, 1, 0:1], dstf[:, T - 1:T], edge_f[:, 1:2], ALU.is_equal)
            v.drain()
            v.tensor_copy(crossing[:, 2, :], first_run[:, T - 1:T].to_broadcast([P, FEAT]))
            v.tensor_copy(crossing[:, 0, 1:FEAT], crossing[:, 0, 0:1].to_broadcast([P, FEAT - 1]))
            v.tensor_copy(crossing[:, 1, 1:FEAT], crossing[:, 1, 0:1].to_broadcast([P, FEAT - 1])).then_inc(s_cross, 1)
            goes_on = same_far
            v.tensor_copy(goes_on[:, 0:T - 1], same[:, 1:T])
            v.drain()
            v.tensor_copy(goes_on[:, T - 1:T], crossing[:, 1, 0:1])
            v.drain()
            v.tensor_tensor(goes_on[:, 0:T], goes_on[:, 0:T], first_run[:], ALU.max)
            v.tensor_tensor(fixrow[:, 0:1], crossing[:, 1, 0:1], crossing[:, 2, 0:1], ALU.mult)
            v.drain()
            v.scalar_tensor_tensor(sidx[:], goes_on[:, 0:T], BIG, dstf[:], ALU.mult, ALU.add)
            v.scalar_tensor_tensor(fixidx[:], fixrow[:, 0:1], BIG, dstf[:, 0:1], ALU.mult, ALU.add)

            dve.wait_ge(s_feat, 16 * 9)
            v3 = msg_flat[:, 0:3 * T].rearrange("p (t c) -> p t c", c=3)
            v.tensor_tensor(v3, unit, unit, ALU.mult)
            v.tensor_scalar(wn, wn, TANH_GAIN, None, ALU.mult)
            v.drain()
            v.tensor_reduce(dstf[:], v3, AX, ALU.add).then_inc(s_vsq, 1)

            dve.wait_ge(s_crossT, 1)
            v.tensor_copy(flagT[:], small[0:FEAT, 0:3 * P].rearrange("p (a e) -> p a e", a=3))
            v.drain()
            v.tensor_tensor(keepT[:, 0, 1:P], flagT[:, 0, 1:P], flagT[:, 2, 0:P - 1], ALU.mult)
            v.tensor_tensor(keepT[:, 1, 0:P - 1], flagT[:, 1, 0:P - 1], flagT[:, 2, 1:P], ALU.mult)
            v.drain()
            for a in range(2):
                v.tensor_scalar(farT[:, a, :], flagT[:, a, :], FAR, -FAR, ALU.mult, ALU.add)
                v.tensor_scalar(farT[:, 2 + a, :], keepT[:, a, :], FAR, -FAR, ALU.mult, ALU.add)
            v.drain().then_inc(s_flags, 1)

            dve.wait_ge(s_vstd, 1)
            v.reciprocal(dstf[:], same_far[:, 0:T])
            v.drain()
            v.tensor_tensor(unit, unit, spread(dstf[:], 2, [P, T, 3]), ALU.mult)

            dve.wait_ge(s_wl, 16 * N_LOADS)
            v.tensor_scalar(w2r[:, :, 0:2 * MOUT], w2a[:, :, 0:2 * MOUT], PW_S, None, ALU.mult)
            v.tensor_scalar(w2r[:, :, 2 * MOUT:3 * MOUT], w2a[:, :, 2 * MOUT:3 * MOUT], wscale[0:CH, 0:1], None,
                            ALU.mult)
            v.tensor_scalar(w2a[:, :, 3 * MOUT:], w2a[:, :, 3 * MOUT:], PW_V * 3.0 ** -0.5, None, ALU.mult)
            v.drain()
            v.scalar_tensor_tensor(w2r[:, :, 3 * MOUT:], w2b, -PW_V * 6.0 ** -0.5, w2a[:, :, 3 * MOUT:],
                                   ALU.mult, ALU.add).then_inc(s_w2, 1)

            dve.sem_inc(s_tfree, 2)
            dve.sem_inc(s_rawd, 2)
            NG2 = 2 * GA

            def centre(b_next, turn, g, b, dense_wait):
                if b_next is not None:
                    hold(dve, "dve", (s_gath[b_next], turn * (16 * 2 * GA)))
                    rows = raw[:, b_next].rearrange("p t s f -> p (t s) f")
                    v.tensor_reduce(stat[:, 0, 0:NG2], rows, AX, ALU.add)
                if g is not None:
                    hold(dve, "dve", (s_xl[b], dense_wait))
                    v.tensor_reduce(stat[:, 0, NG2:NST], xin[:, b], AX, ALU.add)
                v.drain()
                v.tensor_scalar(stat[:, 3, :], stat[:, 0, :], 1.0 / FEAT, None, ALU.mult)
                v.drain()
                if b_next is not None:
                    last = v.tensor_tensor(cen, rows, spread(stat[:, 3, 0:NG2], 2, [P, NG2, FEAT]), ALU.subtract)
                    last.then_inc(s_rawd, 1)
                if g is not None:
                    last = v.tensor_tensor(dcen[:], xin[:, b], spread(stat[:, 3, NG2:NST], 2, [P, DR, FEAT]),
                                           ALU.subtract)
                v.drain().then_inc(s_cen, 1)

            def variance(n, gathered, dense):
                dve.wait_ge(s_sq, n)
                if gathered:
                    last = v.tensor_reduce(stat[:, 1, 0:NG2], sqr, AX, ALU.add)
                if dense:
                    last = v.tensor_reduce(stat[:, 1, NG2:NST], dsqr[:], AX, ALU.add)
                v.drain().then_inc(s_var, 1)

            def channels(g):
                v.tensor_tensor(chan[:, :, 0:2 * FEAT].rearrange("p t (s f) -> p t s f", s=2), pos,
                                stat[:, 3, 0:NG2].rearrange("p (t s) -> p t s", s=2)[:, :, :, None].to_broadcast(
                                    [P, GA, 2, FEAT]), ALU.mult)
                v.drain()
                for side in range(2):
                    v.tensor_tensor(
                        vprod[:, :, side * MOUT:(side + 1) * MOUT, :],
                        chan[:, :, side * FEAT + MOUT:(side + 1) * FEAT].rearrange("p t (u k) -> p t u k", k=3),
                        spread(cols(unit, g * GA, GA), 2, [P, GA, MOUT, 3]), ALU.mult)
                v.drain()
                v.tensor_reduce(chan[:, :, 2 * FEAT:CH], vprod, AX, ALU.add).then_inc(s_chan, 1)

            def multiply(g, b, t):
                dve.wait_ge(s_tens, g * GA + (t + 1))
                v.tensor_tensor(
                    prod[:, t].rearrange("p (a j) o -> p a j o", a=2),
                    tens[(b + t) % 2][:, :].rearrange("p (a c) -> p a c", a=2)[:, :, 0:HALF].rearrange(
                        "p a (j o) -> p a j o", o=OUTS),
                    hid[:, b, t, :].rearrange("p (a j) -> p a j", a=2)[:, :, :, None].to_broadcast(
                        [P, 2, HID // 2, OUTS]), ALU.mult).then_inc(s_tfree, 1)

            def messages(g):
                v.drain()
                v.tensor_reduce(outs, prod.rearrange("p t j o -> p t o j"), AX, ALU.add).then_inc(s_outs, 1)
                v.drain()
                v.tensor_tensor(vmix, spread(outs[:, :, 2 * MOUT:3 * MOUT], 3, [P, GA, MOUT, 3]),
                                spread(cols(unit, g * GA, GA), 2, [P, GA, MOUT, 3]), ALU.mult)
                v.drain()
                v.tensor_tensor(vmix, vmix, outs[:, :, 3 * MOUT:].rearrange("p t (k w) -> p t w k", k=3), ALU.add)
                hold(dve, "dve", (s_tanh, g + 1))
                v.tensor_tensor(gate[:, 1], gate[:, 0], spread(cols(wn, g * GA, GA), 2, [P, GA, 2 * MOUT]), ALU.mult)
                v.drain()
                m = cols(msg, g * GA, GA)
                v.tensor_copy(m[:, :, 0:MOUT], gate[:, 1, :, 0:MOUT])
                v.tensor_tensor(m[:, :, MOUT:].rearrange("p t (w k) -> p t w k", k=3), vmix,
                                spread(gate[:, 1, :, MOUT:], 3, [P, GA, MOUT, 3]), ALU.mult)
                for t in range(GA):
                    n = g * GA + t
                    v.drain()
                    last = v.scalar_tensor_tensor(cols(run, n + 1, 1), cols(run, n, 1), cols(same, n, 1),
                                                  cols(msg, n, 1), ALU.mult, ALU.add)
                last.then_inc(s_run, 1)

            def invert(n):
                dve.wait_ge(s_std, n)
                v.reciprocal(stat[:, 3, :], stat[:, 2, :])
                v.drain()

            def layer0(i, b, last):
                g = i * 2 + b
                wait = (i + 1) * 16
                if last:
                    wait = (i + 2) * 16
                centre(None if last else 1 - b, i + 1 + b, g, b, wait)
                dve.wait_ge(s_hid, g + 1)
                for t in range(0, 4):
                    multiply(g, b, t)
                variance(g + 2, not last, True)
                for t in range(4, 6):
                    multiply(g, b, t)
                invert(g + 2)
                if not last:
                    channels(g + 1)
                v.scalar_tensor_tensor(dcen[:], dcen[:], 0.0, spread(stat[:, 3, NG2:NST], 2, [P, DR, FEAT]),
                                       ALU.max, ALU.mult)
                multiply(g, b, 6)
                v.drain()
                v.tensor_tensor(xin[:, b], xin[:, b], dcen[:], ALU.add).then_inc(s_ddone, 1)
                messages(g)

            centre(0, 1, None, None, None)
            dve.wait_ge(s_gbd, 16 * 2 * GB)
            variance(1, True, False)
            invert(1)
            channels(0)
            with dve.Fori(0, ITA - 1) as i:
                for b in range(2):
                    layer0(i, b, False)
            layer0(ITA - 1, 0, False)
            layer0(ITA - 1, 1, True)

            v.drain()
            for f in range(FEAT):
                v.tensor_tensor_scan(back[:, ::-1, f], same[:, T:0:-1], msg[:, ::-1, f], 0.0, ALU.mult, ALU.add)

            def cross(n, done, far):
                v.drain().then_inc(s_ends, 1)
                dve.wait_ge(s_endT, done + 1)
                if far:
                    v.memset(endT[0:n, 0, 0:1], -FAR)
                    v.memset(endT[0:n, 1, P - 1:P], -FAR)
                f0, f1 = (farT[0:n, 0], farT[0:n, 1]) if far else (flagT[0:n, 0], flagT[0:n, 1])
                k0, k1 = (farT[0:n, 2], farT[0:n, 3]) if far else (keepT[0:n, 0], keepT[0:n, 1])
                op = ALU.add if far else ALU.mult
                v.tensor_tensor(endT[0:n, 0, 1:P], f0[:, 1:P], small[0:n, 0:P - 1], op)
                v.tensor_tensor(endT[0:n, 1, 0:P - 1], f1[:, 0:P - 1], small[0:n, P + 1:2 * P], op)
                v.drain()
                init = -FAR if far else 0.0
                op1 = ALU.max if far else ALU.add
                v.tensor_tensor_scan(carryT[0:n, 0, :], k0, endT[0:n, 0, :], init, op, op1)
                v.tensor_tensor_scan(carryT[0:n, 1, ::-1], k1[:, ::-1], endT[0:n, 1, ::-1], init, op, op1)
                v.drain().then_inc(s_carT, 1)
                dve.wait_ge(s_car, done + 1)
                v.tensor_copy(carry[:, :, 0:n], small[:, 2 * P:2 * P + 2 * FEAT].rearrange(
                    "p (a n) -> p a n", a=2)[:, :, 0:n])
                if far:
                    v.memset(endT[0:n, 0, 0:1], 0.0)
                    v.memset(endT[0:n, 1, P - 1:P], 0.0)
                v.drain()

            v.drain()
            v.tensor_copy(ends[:, 0, :], run[:, T, :])
            v.tensor_copy(ends[:, 1, :], back[:, 0, :])
            cross(FEAT, 0, False)
            v.tensor_tensor(fixrow[:], back[:, 0, :], carry[:, 0, :], ALU.add).then_inc(s_fix, 1)

            v.drain()
            v.tensor_tensor(back[:], back[:], msg[:], ALU.subtract)
            v.drain()
            v.tensor_tensor(back[:], back[:], run[:, 1:, :], ALU.add)
            for a, at in ((0, first_run), (1, last_run)):
                v.drain()
                v.tensor_tensor(msg[:], spread(at[:], 2, [P, T, FEAT]), spread(carry[:, a, :], 1, [P, T, FEAT]),
                                ALU.mult)
                v.drain()
                v.tensor_tensor(back[:], back[:], msg[:], ALU.add)
            v.drain()
            v.tensor_tensor(x1d, x1d, back[:], ALU.add)
            v.drain()

            s0, s1, s2, s3 = (seg_f[:, a, :] for a in range(4))
            v.tensor_reduce(s0, x1d, AX, ALU.add)
            v.drain()
            v.tensor_scalar(s3, s0, 1.0 / FEAT, None, ALU.mult)
            v.drain()
            v.tensor_tensor(msg[:], x1d, spread(s3, 2, [P, T, FEAT]), ALU.subtract).then_inc(s_dc, 1)
            dve.wait_ge(s_dq, 1)
            v.tensor_reduce(s1, back[:], AX, ALU.add).then_inc(s_dv, 1)
            dve.wait_ge(s_dd, 1)
            v.reciprocal(s3, s2)
            v.drain()
            v.scalar_tensor_tensor(h1d[:], msg[:], 0.0, spread(s3, 2, [P, T, FEAT]), ALU.max,
                                   ALU.mult).then_inc(s_h1d, 1)
            v.drain()
            v.tensor_tensor(base[:, 0:T, :], x1d, h1d[:], ALU.add)

            dve.sem_inc(s_agread, NSB)
            dve.sem_inc(s_qfree, 1)

            def source_rows(i, s, turn):
                k = i * NSB + s
                hold(dve, "dve", (s_gb[s], turn * (16 * GB)))
                v.tensor_tensor(x1s[:, s], agg_ring[:, s],
                                xsd[:, k * GB:(k + 1) * GB, 0, :] if isinstance(k, int)
                                else xsd[:, bass.ds(k * GB, GB), 0, :], ALU.add).then_inc(s_agread, 1)
                v.drain()
                v.tensor_reduce(stat_b[:, s, 0, :], x1s[:, s], AX, ALU.add)
                v.drain()
                v.tensor_scalar(stat_b[:, s, 3, :], stat_b[:, s, 0, :], 1.0 / FEAT, None, ALU.mult)
                v.drain()
                v.tensor_tensor(c1s[:, s], x1s[:, s], spread(stat_b[:, s, 3, :], 2, [P, GB, FEAT]),
                                ALU.subtract).then_inc(s_bc, 1)

            source_rows(0, 0, 1)

            def scores(i, s, last):
                k = i * NSB + s
                if not last:
                    if s + 1 < NSB:
                        source_rows(i, s + 1, i + 1)
                    else:
                        source_rows(i + 1, 0, i + 2)
                dve.wait_ge(s_bq, k + 1)
                v.tensor_reduce(stat_b[:, s, 1, :], q1s[:, s], AX, ALU.add).then_inc(s_bv, 1)
                dve.wait_ge(s_bd, k + 1)
                v.reciprocal(stat_b[:, s, 3, :], stat_b[:, s, 2, :])
                v.drain()
                v.scalar_tensor_tensor(h1s[:, s], c1s[:, s], 0.0, spread(stat_b[:, s, 3, :], 2, [P, GB, FEAT]),
                                       ALU.max, ALU.mult).then_inc(s_bh, 1)
                v.drain()
                dve.wait_ge(s_q, k + 1)
                v.tensor_tensor(hprod, tens[s % 2][:, 0:GB * P].rearrange("p (t h f) -> p t h f", t=GB, h=HEADS),
                                spread(h1s[:, s], 2, [P, GB, HEADS, FEAT]), ALU.mult).then_inc(s_qfree, 1)
                v.drain()
                sc = score[:, :, k * GB:(k + 1) * GB] if isinstance(k, int) else score[:, :, bass.ds(k * GB, GB)]
                v.tensor_reduce(sc.rearrange("p h t -> p t h"), hprod, AX, ALU.add)

            with dve.Fori(0, ITB - 1) as i:
                for s in range(NSB):
                    scores(i, s, False)
            for s in range(NSB):
                scores(ITB - 1, s, s == NSB - 1)

            v.tensor_scalar(same_far[:], same[:], FAR, -FAR, ALU.mult, ALU.add)
            v.tensor_scalar(first_far, first_run[:], FAR, -FAR, ALU.mult, ALU.add)
            v.tensor_scalar(last_far, last_run[:], FAR, -FAR, ALU.mult, ALU.add)
            v.drain()
            for h in range(HEADS):
                v.tensor_tensor_scan(seg_f[:, h, :], same_far[:, 0:T], score[:, h, :], -FAR, ALU.add, ALU.max)
                v.tensor_tensor_scan(seg_b[:, h, ::-1], same_far[:, T:0:-1], score[:, h, ::-1], -FAR, ALU.add,
                                     ALU.max)
            v.drain()
            v.tensor_copy(ends[:, 0, 0:HEADS], seg_f[:, :, T - 1])
            v.tensor_copy(ends[:, 1, 0:HEADS], seg_b[:, :, 0])
            v.tensor_tensor(seg_m, seg_f, seg_b, ALU.max)
            cross(HEADS, 1, True)
            for a, at in ((0, first_far), (1, last_far)):
                v.tensor_tensor(seg_f, spread(at, 1, [P, HEADS, T]), spread(carry[:, a, 0:HEADS], 2, [P, HEADS, T]),
                                ALU.add)
                v.drain()
                v.tensor_tensor(seg_m, seg_m, seg_f, ALU.max)
                v.drain()
            v.tensor_tensor(seg_b, score, seg_m, ALU.subtract).then_inc(s_sm, 1)
            dve.wait_ge(s_e, 1)
            for h in range(HEADS):
                v.tensor_tensor_scan(seg_f[:, h, :], same[:, 0:T], seg_m[:, h, :], 0.0, ALU.mult, ALU.add)
                v.tensor_tensor_scan(seg_b[:, h, ::-1], same[:, T:0:-1], seg_m[:, h, ::-1], 0.0, ALU.mult, ALU.add)
            v.drain()
            v.tensor_copy(ends[:, 0, 0:HEADS], seg_f[:, :, T - 1])
            v.tensor_copy(ends[:, 1, 0:HEADS], seg_b[:, :, 0])
            v.drain()
            v.tensor_tensor(seg_b, seg_b, seg_m, ALU.subtract)
            v.drain()
            v.tensor_tensor(seg_b, seg_b, seg_f, ALU.add)
            cross(HEADS, 2, False)
            for a, at in ((0, first_run), (1, last_run)):
                v.tensor_tensor(seg_f, spread(at[:], 1, [P, HEADS, T]), spread(carry[:, a, 0:HEADS], 2, [P, HEADS, T]),
                                ALU.mult)
                v.drain()
                v.tensor_tensor(seg_b, seg_b, seg_f, ALU.add)
                v.drain()
            v.reciprocal(seg_f, seg_b)
            v.drain()
            v.tensor_tensor(score, seg_m, seg_f, ALU.mult)
            v.memset(yrun, 0.0)
            v.memset(yfirst, 0.0)
            v.drain()

            dve.sem_inc(s_vfree, 1)
            dve.sem_inc(s_vused, NSB)
            with dve.Fori(0, ITB) as i:
                for s in range(NSB):
                    k = i * NSB + s
                    hold(dve, "dve", (s_v, k + 1))
                    v.tensor_tensor(hprod, tens[s % 2][:, 0:GB * P].rearrange("p (t h f) -> p t h f", t=GB, h=HEADS),
                                    score[:, :, bass.ds(k * GB, GB)].rearrange("p h t -> p t h")[:, :, :, None]
                                    .to_broadcast([P, GB, HEADS, FEAT]), ALU.mult).then_inc(s_vfree, 1)
                    v.drain().then_inc(s_vused, 1)
                    v.tensor_reduce(yrow[:, s], hprod.rearrange("p t h f -> p t f h"), AX, ALU.add)
                    v.drain()
                    v.tensor_tensor(ytmp, yrow[:, s], spread(first_run[:, bass.ds(k * GB, GB)], 2, [P, GB, FEAT]),
                                    ALU.mult)
                    for t in range(GB):
                        before = yrun[:, s, t - 1, :] if t else yrun[:, (s - 1) % NSB, GB - 1, :]
                        v.scalar_tensor_tensor(yrun[:, s, t, :], before, same[:, bass.ds(k * GB + t, 1)],
                                               yrow[:, s, t, :], ALU.mult, ALU.add)
                        v.drain()
                    v.tensor_tensor(yfirst, yfirst, ytmp, ALU.add)
                    hold(dve, "dve", (s_ofree, k + 1))
                    v.tensor_tensor(out_ring[:, s], yrun[:, s], base[:, bass.ds(k * GB, GB), :],
                                    ALU.add).then_inc(s_orow, 1)
            v.drain()
            v.tensor_copy(ends[:, 0, :], yrun[:, NSB - 1, GB - 1, :])
            v.tensor_reduce(ends[:, 1, :], yfirst.rearrange("p t f -> p f t"), AX, ALU.add)
            v.drain()
            v.tensor_tensor(fixrow[:], base[:, 0, :], ends[:, 1, :], ALU.add)
            cross(FEAT, 3, False)
            v.tensor_tensor(fixrow[:], fixrow[:], carry[:, 0, :], ALU.add).then_inc(s_fix, 1)


_INS = ['x', 'src', 'dst', 'edge_attr_10', 'edge_attr_3', 'edge_weight', 'L0_gnn_W1', 'L0_gnn_W2',
        'L1_gnn_Wq', 'L1_gnn_Wk', 'L1_gnn_Wv', 'L1_gnn_Wout']


def kernel(**inputs):
    import numpy as _np
    import concourse.bacc as _bacc
    from concourse import mybir as _mybir
    from concourse.bass_utils import run_bass_kernel_spmd as _run

    nc = _bacc.Bacc("TRN2", target_bir_lowering=False, num_devices=1)
    arrays, args = {}, []
    for name in _INS:
        a = _np.ascontiguousarray(inputs[name])
        arrays[f"in_{name}"] = a
        args.append(nc.dram_tensor(f"in_{name}", a.shape, _mybir.dt.from_np(a.dtype), kind="ExternalInput").ap())
    shape = arrays["in_x"].shape
    args.append(nc.dram_tensor("out_dram", shape, _mybir.dt.float32, kind="ExternalOutput").ap())
    build_gnn(nc, *args)
    return _run(nc, [arrays], core_ids=[0]).results[0]["out_dram"]
```

```python
import numpy as np
import concourse.bass as bass
from concourse import mybir
from contextlib import ExitStack

F32 = mybir.dt.float32
I32 = mybir.dt.int32
BF16 = mybir.dt.bfloat16
ALU = mybir.AluOpType
ACT = mybir.ActivationFunctionType
AX = mybir.AxisListType.X

P = 128
FEAT = 32
EMB = 10
HID = 16
MOUT = 8
HEADS = 4
EPS = 1e-5
TANH_GAIN = 1.593
PW_S = 0.17677669529663687
PW_V = 0.25
BIG = float(1 << 20)
FAR = 1.0e30


def build_gnn(nc, x, src, dst, attr10, attr3, weight, W1, W2, Wq, Wk, Wv, Wout, out):
    N = x.shape[0]
    E = src.shape[0]
    T = -(-E // P)
    T = -(-T // 28) * 28
    TAIL = E - (P - 1) * T
    assert 0 < TAIL <= T and T % 28 == 0

    GA = 7
    NGA = T // GA
    ITA = NGA // 2
    GB = 4
    NSB = 7
    NGB = T // GB
    ITB = NGB // NSB
    SC = 4 * MOUT
    VU = 2 * MOUT
    OG = 3 * MOUT
    OUTS = 2 * OG
    RPP = N // P
    DR = -(-RPP // NGA)
    DLAST = RPP - (NGA - 1) * DR
    DREM = N - P * RPP
    assert 0 < DLAST < DR and DREM <= P and NGA % 2 == 0

    agg = nc.dram_tensor("agg_rows", [N, FEAT], F32, kind="Internal").ap()

    ctx = ExitStack()
    with ctx:
        def sb(name, shape, dt=F32):
            return ctx.enter_context(nc.sbuf_tensor(name, shape, dt))

        def pb(name, cols=512):
            return ctx.enter_context(nc.psum_tensor(name, [P, cols], F32))

        def sem(name):
            return ctx.enter_context(nc.semaphore(name))

        idx = sb("idx", [P, 2, T + 28], I32)
        sidx = sb("sidx", [P, T], I32)
        fixidx = sb("fixidx", [P, 1], I32)
        dst_i = sb("dst_i", [P, T], I32)
        edge_i = sb("edge_i", [P, 2], I32)
        edge_f = sb("edge_f", [P, 2])
        dstf = sb("dstf", [P, T])
        same = sb("same", [P, T + 1])
        first_run = sb("first_run", [P, T])
        last_run = sb("last_run", [P, T])
        crossing = sb("crossing", [P, 3, FEAT])
        xsd = sb("xsd", [P, T, 2, FEAT])
        msg = sb("msg", [P, T, FEAT])
        run = sb("run", [P, T + 1, FEAT])
        back = sb("back", [P, T, FEAT])
        x1d = xsd[:, :, 1, :]
        h1d = msg
        base = run
        h1sT = back[:, :, :].rearrange("p t f -> p (t f)").rearrange("p (k e) -> p k e", e=P)
        prod = back[:, :, :].rearrange("p t f -> p (t f)")[:, 0:GA * HID * OUTS].rearrange(
            "p (b j o) -> p b j o", b=2 * GA, o=OG)

        ident = sb("ident", [P, P])
        eps = sb("eps", [P, 1])
        wscale = sb("wscale", [P, 1])
        w1bd = sb("w1bd", [GA * EMB, GA * HID])
        w_s = sb("w2_scalar_stack", [4 * SC, 2, HID, OG], BF16)
        w_v = sb("w2_vector_stack", [6 * VU, HID, MOUT], BF16)
        identb = sb("identb", [P, P], BF16)
        gbd = sb("gbd", [P, GB, P])
        ubd = sb("ubd", [P, GB, P])

        area_a = sb("features_or_scores", [P, 4 * HEADS * T])
        taken_a = {0: 0, 1: 0}

        def in_a(layer, *dims):
            n, at = int(np.prod(dims)), taken_a[layer]
            taken_a[layer] += n
            assert taken_a[layer] <= 4 * HEADS * T
            v = area_a[:, at:at + n]
            names = "abc"[:len(dims)]
            return v.rearrange(f"p ({' '.join(names)}) -> p {' '.join(names)}", **dict(zip(names, dims))) \
                if len(dims) > 1 else v

        emb = in_a(0, T, EMB)
        unit = in_a(0, T, 3)
        wn = in_a(0, T)
        score = in_a(1, HEADS, T)
        seg_f = in_a(1, HEADS, T)
        seg_b = in_a(1, HEADS, T)
        seg_m = in_a(1, HEADS, T)

        AREA = 7832
        area_b = sb("working_buffers", [P, AREA])
        taken_b = {0: 0, 1: 0}

        def in_b(layer, *dims, parts=P):
            n, at = int(np.prod(dims)), taken_b[layer]
            taken_b[layer] += n
            assert taken_b[layer] <= AREA, taken_b
            v = area_b[0:parts, at:at + n]
            names = "abcd"[:len(dims)]
            return v.rearrange(f"p ({' '.join(names)}) -> p {' '.join(names)}", **dict(zip(names, dims))) \
                if len(dims) > 1 else v

        raw = in_b(0, 2, GA, 2, FEAT)
        cen = in_b(0, GA * 2, FEAT)
        sqr = in_b(0, GA * 2, FEAT)
        pos = in_b(0, GA, 2, FEAT)
        val_s = in_b(0, GA, SC)
        val_v = in_b(0, GA, 3, VU)
        stack_s = in_b(0, GA * 4 * SC // 2).bitcast(BF16).rearrange("p (t a c) -> p t a c", t=GA, a=4)
        stack_v = in_b(0, GA * 3 * 6 * VU // 2).bitcast(BF16).rearrange("p (t a c) -> p t a c", t=GA * 3, a=6)
        rest_s = sqr.rearrange("p n f -> p (n f)")[:, 0:GA * SC].rearrange("p (t c) -> p t c", c=SC)
        rest_v = cen.rearrange("p n f -> p (n f)")[:, 0:GA * 3 * VU].rearrange("p (t c) -> p t c", c=VU)
        vprod = pos.rearrange("p t s f -> p (t s f)")[:, 0:GA * 3 * VU].rearrange(
            "p (t u k) -> p t u k", t=GA, k=3)
        emb_blk = in_b(0, 2, GA * EMB)
        embT = in_b(0, P, parts=GA * EMB)
        hid = in_b(0, 2, GA, HID)
        stackT_s = in_b(0, GA * P // 2).bitcast(BF16).rearrange("c (t e) -> c t e", t=GA)
        stackT_v = in_b(0, GA * 3 * P // 2, parts=6 * VU).bitcast(BF16).rearrange("c (t k e) -> c t k e", t=GA, k=3)
        msgT = in_b(0, FEAT, GA + 1)
        runT = in_b(0, 2, FEAT, GA + 1)
        sameT = in_b(0, 2, FEAT, GA + 1)
        behind = back[:, :, :].rearrange("p t f -> p (t f)")[:, GA * HID * OUTS:]
        outs = behind[:, 0:GA * OUTS].rearrange("p (t o) -> p t o", t=GA)
        gate = behind[:, 336:336 + 4 * GA * MOUT].rearrange("p (a t o) -> p a t o", a=2, t=GA)
        vmix = behind[:, 560:560 + 3 * GA * MOUT].rearrange("p (t w k) -> p t w k", t=GA, w=MOUT)

        agg_ring = in_b(1, NSB, GB, FEAT)
        x1s = in_b(1, NSB, GB, FEAT)
        c1s = in_b(1, NSB, GB, FEAT)
        q1s = in_b(1, NSB, GB, FEAT)
        h1s = in_b(1, NSB, GB, FEAT)
        hprod = in_b(1, GB, HEADS, FEAT)
        h1d_blk = in_b(1, P)
        h1dT = in_b(1, P)
        ytmp = in_b(1, GB, FEAT)
        yfirst = in_b(1, GB, FEAT)
        first_far = in_b(1, T)
        last_far = in_b(1, T)
        out_ring = agg_ring
        h1sT_ring = q1s
        yrow = x1s
        yrun = c1s

        idx_ring = sb("idx_ring", [P, 2, 2, GA], I32)
        sidx_ring = sb("sidx_ring", [P, 2, GA], I32)
        idx_ring_b = sb("idx_ring_b", [P, NSB, GB], I32)
        sidx_ring_b = sb("sidx_ring_b", [P, NSB, GB], I32)
        row_ring = sb("row_ring", [P, 2, GA, FEAT])
        NST = 2 * GA + DR
        stat = sb("stat", [P, 4, NST])
        stat_b = sb("stat_b", [P, NSB, 4, GB])
        xin = sb("xin", [P, 2, DR, FEAT])
        dcen = sb("dcen", [P, DR, FEAT])
        dsqr = sb("dsqr", [P, DR, FEAT])
        fixrow = sb("fixrow", [P, FEAT])
        same_far = sb("same_far", [P, T + 1])

        flagT = sb("flagT", [FEAT, 3, P])
        keepT = sb("keepT", [FEAT, 2, P])
        farT = sb("farT", [FEAT, 4, P])
        ends = sb("ends", [P, 2, FEAT])
        endT = sb("endT", [FEAT, 2, P])
        carryT = sb("carryT", [FEAT, 2, P])
        carry = sb("carry", [P, 2, FEAT])

        back_flat = back[:, :, :].rearrange("p t f -> p (t f)")
        def in_back(at, parts, *dims):
            n = int(np.prod(dims))
            names = "abc"[:len(dims)]
            return back_flat[0:parts, at:at + n].rearrange(f"p ({' '.join(names)}) -> p {' '.join(names)}",
                                                           **dict(zip(names, dims)))

        w2s = in_back(0, SC, HID, OG)
        w2d = in_back(384, VU, HID, MOUT)
        w2e = in_back(512, VU, HID, MOUT)
        w2v = in_back(640, VU, HID, MOUT)
        w2s_rest = in_back(768, SC, HID, OG)
        w2v_rest = in_back(1152, VU, HID, MOUT)
        w2s_part = back_flat[0:SC, 1280:1280 + 576].bitcast(BF16).rearrange("p (a j o) -> p a j o", a=3, o=OG)
        w2v_part = back_flat[0:VU, 1856:1856 + 192].bitcast(BF16).rearrange("p (a j o) -> p a j o", a=3, o=MOUT)
        msg_flat = msg[:, :, :].rearrange("p t f -> p (t f)")
        ZR = 28
        zeros = xsd[:, T - ZR // 2:T, :, :].rearrange("p t s f -> p (t s f)")
        wtop = T * FEAT
        wqk = msg_flat[:, wtop - 96:wtop].rearrange("p (a f) -> p a f", a=3)
        wqkvT = msg_flat[0:FEAT, wtop - 512:wtop - 128].rearrange("p (a e) -> p a e", a=3)
        wout = msg_flat[0:FEAT, wtop - 128:wtop - 96]
        gu = msg_flat[0:FEAT, wtop - 768:wtop - 512].rearrange("p (a e) -> p a e", a=2)

        small = pb("small")
        turnA = pb("turnA")
        turnB = pb("turnB")
        tens = [pb("tens0", 1024), pb("tens1", 1024)]
        spare = pb("spare")

        s_pad = sem("pads_set")
        s_edges = sem("edges_loaded")
        s_feat = sem("edge_features_loaded")
        s_wz = sem("weight_buffers_zeroed")
        s_wl = sem("weights_loaded")
        s_w2p = sem("w2_parts_ready")
        s_w2 = sem("w2_stacks_loaded")
        s_wT = sem("attention_weights_turned")
        s_wTs = sem("turned_weights_on_sbuf")
        s_gps = sem("folded_weights_ready")
        s_gsb = sem("folded_weights_on_sbuf")
        s_gbd = sem("block_weights_loaded")
        s_flags = sem("partition_flags_ready")
        s_id0 = sem("identity_zeroed")
        s_id = sem("identity_ready")
        s_zset = sem("zeros_set")
        s_zfill = sem("agg_rows_zeroed")
        s_const = sem("act_constants_ready")
        s_vsq = sem("vector_norms_summed")
        s_vstd = sem("vector_norms_ready")
        s_cross = sem("crossing_flags_ready")
        s_crossT = sem("crossing_flags_turned")
        s_istg = sem("indices_staged")
        s_pool = sem("pool_steps")
        s_gath = [sem("rows_gathered0"), sem("rows_gathered1")]
        s_rawd = sem("raw_read_by_vector")
        s_rawa = sem("raw_read_by_scalar")
        s_cen = sem("centred")
        s_sq = sem("squared")
        s_var = sem("variance_summed")
        s_std = sem("deviation_ready")
        s_val = sem("channels_ready")
        s_part1 = sem("first_parts_ready")
        s_rest1 = sem("first_rests_ready")
        s_part2 = sem("second_parts_ready")
        s_chan = sem("stacks_ready")
        s_same = sem("segment_flags_spread")
        s_mfree = sem("messages_kept")
        s_embB = sem("emb_block_staged")
        s_embT = sem("emb_turned")
        s_embS = sem("emb_on_sbuf")
        s_hps = sem("hidden_product_ready")
        s_hid = sem("hidden_ready")
        s_turn = sem("channels_turned")
        s_turned = sem("turned_channels_on_sbuf")
        s_tens = sem("tensor_product_ready")
        s_tfree = sem("tensor_product_read")
        s_outs = sem("outputs_summed")
        s_tanh = sem("gates_ready")
        s_run = sem("running_sums_ready")
        s_rows = sem("scatter_rows_staged")
        s_rfree = sem("scatter_ring_free")
        s_scat = sem("agg_rows_scattered")
        s_xl = [sem("dense_rows_loaded0"), sem("dense_rows_loaded1")]
        s_ddone = sem("dense_rows_ready")
        s_dst = sem("dense_rows_stored")
        s_ends = sem("segment_ends_ready")
        s_endT = sem("segment_ends_turned")
        s_carT = sem("carries_scanned")
        s_car = sem("carries_ready")
        s_fix = sem("fix_rows_ready")
        s_fixd = sem("fix_rows_scattered")
        s_hdB = sem("dst_block_staged")
        s_hvB = sem("values_block_staged")
        s_hdT = sem("dst_rows_turned")
        s_hdS = sem("turned_dst_rows_on_sbuf")
        s_h1d = sem("dst_h_ready")
        s_dc = sem("dst_centred")
        s_dq = sem("dst_squared")
        s_dv = sem("dst_variance_summed")
        s_dd = sem("dst_deviation_ready")
        s_istgb = sem("src_indices_staged")
        s_gb = [sem(f"agg_gathered{s}") for s in range(NSB)]
        s_agread = sem("agg_ring_read")
        s_bc = sem("src_centred")
        s_bq = sem("src_squared")
        s_bv = sem("src_variance_summed")
        s_bd = sem("src_deviation_ready")
        s_bh = sem("src_h_ready")
        s_hsT = sem("src_rows_turned")
        s_hsS = sem("turned_src_rows_on_sbuf")
        s_q = sem("query_ready")
        s_qfree = sem("query_read")
        s_sm = sem("max_subtracted")
        s_e = sem("exponentials_ready")
        s_attn = sem("attention_ready")
        s_v = sem("values_ready")
        s_vfree = sem("values_read")
        s_vused = sem("value_blocks_used")
        s_orow = sem("output_rows_ready")
        s_sstg = sem("output_indices_staged")
        s_ofree = sem("output_ring_free")
        s_osc = [sem(f"output_rows_scattered{s}") for s in range(NSB)]
        s_last = sem("last_rows_scattered")
        s_hold = {e: sem(f"held_{e}") for e in ("act", "dve", "pe", "pool", "sp")}

        def hold(eng, name, *waits):
            for s, v in waits:
                eng.wait_ge(s, v)
            eng.sem_inc(s_hold[name], 1)

        def full(ap, dims):
            return ap.to_broadcast(dims)

        block = ctx.enter_context(nc.Block())

        def edge_loads(eng, dest, source, s):
            w = 1 if len(source.shape) == 1 else source.shape[1]
            flat = source if w == 1 else source.rearrange("e c -> (e c)")
            for a, b in ((0, 112), (112, P - 1)):
                v = flat[a * T * w:b * T * w].rearrange("(p n) -> p n", p=b - a)
                eng.dma_start(dest[a:b, 0:T * w], v).then_inc(s, 16)
            v = flat[(P - 1) * T * w:E * w].rearrange("(p n) -> p n", p=1)
            eng.dma_start(dest[P - 1:P, 0:TAIL * w], v).then_inc(s, 16)
            return 48

        ZC = N // (P * ZR)
        ZREST = (N - ZC * P * ZR) // P
        ZREM = N - ZC * P * ZR - P * ZREST
        N_LOADS = 2 * 3 + 2 + GA + 3 + 1

        @block.sync
        def _(sp):
            sp.wait_ge(s_pad, 1)
            edge_loads(sp, dst_i[:, :], dst, s_edges)
            edge_loads(sp, idx[:, 0, :], src, s_edges)
            border = dst[0:(P - 1) * T].rearrange("(p n) -> p n", n=T)[:, T - 1:T]
            sp.dma_start(edge_i[1:P, 0:1], border, allow_slow_non_contiguous=True).then_inc(s_edges, 16)
            border = dst[T:(P - 1) * T].rearrange("(p n) -> p n", n=T)[:, 0:1]
            sp.dma_start(edge_i[0:P - 2, 1:2], border, allow_slow_non_contiguous=True).then_inc(s_edges, 16)
            sp.dma_start(edge_i[P - 2:P - 1, 1:2],
                         dst[(P - 1) * T:(P - 1) * T + 1].rearrange("(p n) -> p n", n=1)).then_inc(s_edges, 16)
            edge_loads(sp, unit[:, :, :].rearrange("p t c -> p (t c)"), attr3, s_feat)
            edge_loads(sp, wn, weight, s_feat)
            edge_loads(sp, emb[:, :, :].rearrange("p t c -> p (t c)"), attr10, s_feat)
            xrows = x[0:P * RPP, :].rearrange("(p r) f -> p (r f)", p=P)
            orows = out[0:P * RPP, :].rearrange("(p r) f -> p (r f)", p=P)

            def chunk(ap, g, n):
                if isinstance(g, int):
                    return ap[:, g * DR * FEAT:(g * DR + n) * FEAT]
                return ap[:, bass.ds(g * (DR * FEAT), n * FEAT)]

            def slot(b, n):
                return xin[:, b, 0:n, :].rearrange("p r f -> p (r f)")

            for b in range(2):
                sp.dma_start(slot(b, DR), chunk(xrows, b, DR)).then_inc(s_xl[b], 16)
            sp.wait_ge(s_w2p, 1)
            for turn, parts in enumerate(((0, 0, 0, 1), (2, 1, 1))):
                for place, part in enumerate(parts):
                    sp.dma_start(w_s[place * SC:(place + 1) * SC, turn, :, :], w2s_part[:, part]).then_inc(s_w2, 16)
            for place, part in enumerate((0, 0, 1, 1, 2, 0)):
                sp.dma_start(w_v[place * VU:(place + 1) * VU, :, :], w2v_part[:, part]).then_inc(s_w2, 16)
            sp.wait_ge(s_zset, 1)
            sp.dma_start(agg[0:ZC * P * ZR, :].rearrange("(c p a) f -> p c (a f)", c=ZC, p=P),
                         zeros[:, None, :].to_broadcast([P, ZC, ZR * FEAT])).then_inc(s_zfill, 16)
            sp.dma_start(agg[ZC * P * ZR:ZC * P * ZR + P * ZREST, :].rearrange("(p a) f -> p (a f)", p=P),
                         zeros[:, 0:ZREST * FEAT]).then_inc(s_zfill, 16)
            sp.dma_start(agg[N - ZREM:N, :], zeros[0:ZREM, 0:FEAT]).then_inc(s_zfill, 16)

            def store(g, b, n):
                hold(sp, "sp", (s_ddone, g + 1))
                sp.dma_start(chunk(orows, g, n), slot(b, n)).then_inc(s_dst, 16)

            with sp.Fori(0, ITA - 2) as i:
                for b in range(2):
                    g = i * 2 + b
                    store(g, b, DR)
                    hold(sp, "sp", (s_dst, (g + 1) * 16))
                    sp.dma_start(slot(b, DR), chunk(xrows, g + 2, DR)).then_inc(s_xl[b], 16)
            store(NGA - 4, 0, DR)
            sp.wait_ge(s_dst, (NGA - 3) * 16)
            sp.dma_start(slot(0, DR), chunk(xrows, NGA - 2, DR)).then_inc(s_xl[0], 16)
            store(NGA - 3, 1, DR)
            sp.wait_ge(s_dst, (NGA - 2) * 16)
            sp.dma_start(slot(1, DLAST), chunk(xrows, NGA - 1, DLAST)).then_inc(s_xl[1], 16)
            sp.dma_start(xin[0:DREM, 1, DLAST, :], x[P * RPP:N, :]).then_inc(s_xl[1], 16)
            store(NGA - 2, 0, DR)
            store(NGA - 1, 1, DLAST)
            sp.dma_start(out[P * RPP:N, :], xin[0:DREM, 1, DLAST, :]).then_inc(s_dst, 16)
            sp.wait_ge(s_dst, (NGA + 1) * 16)

        @block.gpsimd
        def _(pool):
            nc.gpsimd.memset(ident[:], 0.0).then_inc(s_id0, 1)
            pool.wait_ge(s_id0, 1)
            nc.gpsimd.affine_select(out=ident[:], in_=ident[:], compare_op=ALU.not_equal, fill=1.0, base=0,
                                    pattern=[[-1, P]], channel_multiplier=1).then_inc(s_id, 1)
            pool.wait_ge(s_id, 1)
            nc.gpsimd.tensor_copy(identb[:], ident[:]).then_inc(s_id, 1)

            def gathers(g, b):
                hold(pool, "pool", (s_istg, g + 1), (s_rawd, g + 1), (s_rawa, g + 1))
                for t in range(GA):
                    for side in range(2):
                        nc.gpsimd.indirect_dma_start(
                            raw[:, b, t, side, :], None, x,
                            bass.IndirectOffsetOnAxis(ap=idx_ring[:, b, side, t:t + 1], axis=0)
                        ).then_inc(s_gath[b], 16)

            def scatters(g, b):
                hold(pool, "pool", (s_rows, g + 1))
                for t in range(GA):
                    nc.gpsimd.indirect_dma_start(
                        agg, bass.IndirectOffsetOnAxis(ap=sidx_ring[:, b, t:t + 1], axis=0),
                        row_ring[:, b, t, :], None, bounds_check=N - 1, oob_is_err=False
                    ).then_inc(s_scat, 16)

            def scattered(g):
                pool.wait_ge(s_scat, (g + 1) * (16 * GA))
                pool.sem_inc(s_rfree, 1)

            pool.sem_inc(s_rfree, 2)
            for g in range(4):
                gathers(g, g % 2)
            pool.wait_ge(s_zfill, 48)
            with pool.Fori(2, ITA) as i:
                for b in range(2):
                    g = i * 2 + b
                    gathers(g, b)
                    scatters(g - 4, b)
                    scattered(g - 4)
            for g in range(NGA - 4, NGA):
                scatters(g, g % 2)
                scattered(g)
            pool.wait_ge(s_fix, 1)
            nc.gpsimd.indirect_dma_start(agg, bass.IndirectOffsetOnAxis(ap=fixidx[:, 0:1], axis=0),
                                         fixrow[:], None, bounds_check=N - 1, oob_is_err=False
                                         ).then_inc(s_fixd, 16)
            pool.wait_ge(s_fixd, 16)

            with pool.Fori(0, ITB) as i:
                for s in range(NSB):
                    k = i * NSB + s
                    hold(pool, "pool", (s_istgb, k + 1), (s_agread, k + 1))
                    for t in range(GB):
                        nc.gpsimd.indirect_dma_start(
                            agg_ring[:, s, t, :], None, agg,
                            bass.IndirectOffsetOnAxis(ap=idx_ring_b[:, s, t:t + 1], axis=0)
                        ).then_inc(s_gb[s], 16)

            pool.wait_ge(s_dst, (NGA + 1) * 16)
            pool.sem_inc(s_ofree, NSB)

            def out_scatters(i, first):
                for s in range(NSB):
                    k = i * NSB + s
                    if not first:
                        pool.wait_ge(s_osc[s], i * (16 * GB))
                        pool.sem_inc(s_ofree, 1)
                    hold(pool, "pool", (s_orow, k + 1), (s_sstg, k + 1))
                    for t in range(GB):
                        nc.gpsimd.indirect_dma_start(
                            out, bass.IndirectOffsetOnAxis(ap=sidx_ring_b[:, s, t:t + 1], axis=0),
                            out_ring[:, s, t, :], None, bounds_check=N - 1, oob_is_err=False
                        ).then_inc(s_osc[s], 16)

            out_scatters(0, True)
            with pool.Fori(1, ITB) as i:
                out_scatters(i, False)
            pool.wait_ge(s_fix, 2)
            nc.gpsimd.indirect_dma_start(out, bass.IndirectOffsetOnAxis(ap=fixidx[:, 0:1], axis=0),
                                         fixrow[:], None, bounds_check=N - 1, oob_is_err=False
                                         ).then_inc(s_last, 16)
            for s in range(NSB):
                pool.wait_ge(s_osc[s], ITB * 16 * GB)
            pool.wait_ge(s_last, 16)

        @block.scalar
        def _(act):
            act.sem_inc(s_rawa, 2)
            act.sem_inc(s_mfree, 1)
            act.wait_ge(s_wz, 1)
            loads = []

            def load(dest, source):
                act.dma_start(dest, source).then_inc(s_wl, 16)
                loads.append(1)

            w2_rows = W2.rearrange("j (i u w) -> i u j w", i=7, w=MOUT)
            WA_S, WB_S, WA_G, WB_G, WC, WD, WE = range(7)
            load(w2d, w2_rows[WD])
            load(w2e, w2_rows[WE])
            for rows, plan in ((slice(0, VU), (WA_S, WA_G, WC)), (slice(VU, SC), (WB_S, WB_G, WE))):
                for col, which in enumerate(plan):
                    load(w2s[rows, :, col * MOUT:(col + 1) * MOUT], w2_rows[which])
            for t in range(GA):
                load(w1bd[t * EMB:(t + 1) * EMB, t * HID:(t + 1) * HID], W1)
            for a, w in enumerate((Wq, Wk, Wv)):
                load(wqk[:, a, :], w.rearrange("h f o -> (h f) o"))
            load(wout, Wout)
            assert len(loads) == N_LOADS

            def stage_indices(g, b):
                return nc.scalar.copy(idx_ring[:, b, :, :],
                                      idx[:, :, g * GA:(g + 1) * GA] if isinstance(g, int)
                                      else idx[:, :, bass.ds(g * GA, GA)]).then_inc(s_istg, 1)


            act.wait_ge(s_vsq, 1)
            nc.scalar.activation(same_far[:, 0:T], dstf[:, :], ACT.Sqrt).then_inc(s_vstd, 1)

            act.wait_ge(s_wT, 1)
            nc.scalar.copy(wqkvT, turnA[0:FEAT, 0:3 * P].rearrange("p (a e) -> p a e", a=3)).then_inc(s_wTs, 1)
            act.wait_ge(s_gps, 1)
            nc.scalar.activation(gu[:, 0, :], turnB[0:FEAT, 0:P], ACT.Copy, scale=float(FEAT) ** -0.5)
            nc.scalar.activation(gu[:, 1, :], turnB[0:FEAT, P:2 * P], ACT.Copy,
                                 scale=1.0 / HEADS).then_inc(s_gsb, 1)
            act.wait_ge(s_gsb, 1)
            for t in range(GB):
                act.dma_start(gbd[t * FEAT:(t + 1) * FEAT, t, :], gu[:, 0, :]).then_inc(s_gbd, 16)
                act.dma_start(ubd[t * FEAT:(t + 1) * FEAT, t, :], gu[:, 1, :]).then_inc(s_gbd, 16)

            def cols(ap, start, n, axis_len=None):
                return ap[:, start:start + n] if isinstance(start, int) else ap[:, bass.ds(start, n)]

            def take_rows(g, b, turn):
                nc.scalar.copy(emb_blk[:, b].rearrange("p (t c) -> p t c", c=EMB),
                               cols(emb, g * GA, GA)).then_inc(s_embB, 1)
                nc.scalar.copy(sameT[:, b, :, 1:], cols(same, g * GA, GA)[:, None, :].to_broadcast(
                    [P, FEAT, GA])).then_inc(s_same, 1)
                hold(act, "act", (s_gath[b], turn * (16 * 2 * GA)))
                nc.scalar.copy(cols(xsd, g * GA, GA), raw[:, b]).then_inc(s_rawa, 1)
                stage_indices(g + 2, b)

            def squares(n, gathered, dense):
                act.wait_ge(s_cen, n)
                if gathered:
                    nc.scalar.activation(pos, cen.rearrange("p (t s) f -> p t s f", s=2), ACT.Relu)
                    last = nc.scalar.activation(sqr, cen, ACT.Square)
                if dense:
                    last = nc.scalar.activation(dsqr[:], dcen[:], ACT.Square)
                last.then_inc(s_sq, 1)

            def deviation(n):
                act.wait_ge(s_var, n)
                nc.scalar.activation(stat[:, 2, :], stat[:, 1, :], ACT.Sqrt, bias=eps[:, 0:1],
                                     scale=1.0 / FEAT).then_inc(s_std, 1)

            def hidden(g, b):
                act.wait_ge(s_embT, g + 1)
                nc.scalar.copy(embT, small[0:GA * EMB, 0:P]).then_inc(s_embS, 1)
                act.wait_ge(s_hps, g + 1)
                nc.scalar.activation(hid[:, b].rearrange("p t j -> p (t j)"), small[:, P:P + GA * HID], ACT.Relu,
                                     scale=2.0 ** 0.5 / (4 * EMB ** 0.5)).then_inc(s_hid, 1)
                for pair in range(4):
                    n = 2 if pair < 3 else 1
                    bank = (turnA, turnB)[pair % 2][:, :].bitcast(BF16).rearrange("c (t a e) -> c t a e", t=2, a=4)
                    act.wait_ge(s_turn, g * 4 + pair + 1)
                    nc.scalar.copy(stackT_s[:, 2 * pair:2 * pair + n, :], bank[:, 0:n, 0, :])
                    nc.scalar.copy(stackT_v[:, 2 * pair:2 * pair + n], bank[0:6 * VU, 0:n, 1:4, :]).then_inc(s_turned, 1)

            def split(n):
                act.wait_ge(s_val, n)
                nc.scalar.copy(stack_s[:, :, 0:4:3, :], val_s[:, :, None, :].to_broadcast([P, GA, 2, SC]))
                nc.scalar.copy(stack_v[:, :, 0:6:2, :],
                               val_v.rearrange("p t k u -> p (t k) u")[:, :, None, :].to_broadcast(
                                   [P, GA * 3, 3, VU])).then_inc(s_part1, 1)
                act.wait_ge(s_rest1, n)
                nc.scalar.copy(stack_s[:, :, 1, :], rest_s)
                nc.scalar.copy(stack_v[:, :, 1:4:2, :],
                               rest_v[:, :, None, :].to_broadcast([P, GA * 3, 2, VU])).then_inc(s_part2, 1)

            def gates(g):
                act.wait_ge(s_outs, g + 1)
                nc.scalar.activation(gate[:, 0], outs[:, :, 0:2 * MOUT], ACT.Tanh).then_inc(s_tanh, 1)

            def stage_rows(g, b):
                hold(act, "act", (s_run, g + 1), (s_rfree, g + 1))
                sums = runT[:, b, :, 1:].rearrange("p f t -> p t f")
                nc.scalar.copy(cols(msg, g * GA, GA), msgT[:, :, 1:].rearrange("p f t -> p t f"))
                nc.scalar.copy(cols(run, g * GA + 1, GA), sums).then_inc(s_mfree, 1)
                nc.scalar.copy(row_ring[:, b], sums)
                nc.scalar.copy(sidx_ring[:, b], cols(sidx, g * GA, GA)).then_inc(s_rows, 1)

            take_rows(0, 0, 1)
            squares(1, True, False)
            deviation(1)
            split(1)
            hidden(0, 0)

            def layer0(i, b, last):
                g = i * 2 + b
                if not last:
                    take_rows(g + 1, 1 - b, i + 1 + b)
                squares(g + 2, not last, True)
                deviation(g + 2)
                if not last:
                    split(g + 2)
                    hidden(g + 1, 1 - b)
                gates(g)
                stage_rows(g, b)

            with act.Fori(0, ITA - 1) as i:
                for b in range(2):
                    layer0(i, b, False)
            layer0(ITA - 1, 0, False)
            layer0(ITA - 1, 1, True)

            act.wait_ge(s_dc, 1)
            nc.scalar.activation(back[:], msg[:], ACT.Square).then_inc(s_dq, 1)
            act.wait_ge(s_dv, 1)
            nc.scalar.activation(seg_f[:, 2, :], seg_f[:, 1, :], ACT.Sqrt, bias=eps[:, 0:1],
                                 scale=1.0 / FEAT).then_inc(s_dd, 1)

            def stage_src(k, s):
                return nc.scalar.copy(idx_ring_b[:, s, :],
                                      idx[:, 0, k * GB:(k + 1) * GB] if isinstance(k, int)
                                      else idx[:, 0, bass.ds(k * GB, GB)]).then_inc(s_istgb, 1)

            for s in range(NSB):
                stage_src(s, s)

            def sources(i, s, turn):
                k = i * NSB + s
                hold(act, "act", (s_gb[s], turn * (16 * GB)))
                stage_src(k + NSB, s)
                act.wait_ge(s_bc, k + 1)
                nc.scalar.activation(q1s[:, s], c1s[:, s], ACT.Square).then_inc(s_bq, 1)

            def stage_dst(k):
                return nc.scalar.copy(h1d_blk.rearrange("p (t f) -> p t f", f=FEAT),
                                      cols(h1d, k * GB, GB)).then_inc(s_hdB, 1)

            act.wait_ge(s_h1d, 1)
            stage_dst(0)
            sources(0, 0, 1)

            def layer1(i, s, last):
                k = i * NSB + s
                act.wait_ge(s_hdT, k + 1)
                nc.scalar.copy(h1dT, turnA[:, 0:P]).then_inc(s_hdS, 1)
                if not last:
                    stage_dst(k + 1)
                    if s + 1 < NSB:
                        sources(i, s + 1, i + 1)
                    else:
                        sources(i + 1, 0, i + 2)
                act.wait_ge(s_bv, k + 1)
                nc.scalar.activation(stat_b[:, s, 2, :], stat_b[:, s, 1, :], ACT.Sqrt, bias=eps[:, 0:1],
                                     scale=1.0 / FEAT).then_inc(s_bd, 1)
                hold(act, "act", (s_hsT, k + 1))
                nc.scalar.copy(h1sT[:, k, :] if isinstance(k, int) else h1sT[:, bass.ds(k, 1), :],
                               turnB[:, 0:P] if isinstance(k, int) else turnB[:, None, 0:P]).then_inc(s_hsS, 1)

            with act.Fori(0, ITB - 1) as i:
                for s in range(NSB):
                    layer1(i, s, False)
            for s in range(NSB):
                layer1(ITB - 1, s, s == NSB - 1)

            act.wait_ge(s_sm, 1)
            nc.scalar.activation(seg_m, seg_b, ACT.Exp).then_inc(s_e, 1)

            with act.Fori(0, ITB) as i:
                for s in range(NSB):
                    k = i * NSB + s
                    hold(act, "act", (s_vused, k + 1))
                    nc.scalar.copy(h1sT_ring[:, s:s + 1].rearrange("p s t f -> p s (t f)"),
                                   h1sT[:, bass.ds(k, 1), :]).then_inc(s_hvB, 1)
                    hold(act, "act", (s_ofree, k + 1))
                    nc.scalar.copy(sidx_ring_b[:, s, :], sidx[:, bass.ds(k * GB, GB)]).then_inc(s_sstg, 1)

        @block.tensor
        def _(pe):
            pe.wait_ge(s_id, 2)
            pe.wait_ge(s_wl, 16 * N_LOADS)
            for a in range(3):
                mm = nc.tensor.transpose(turnA[0:FEAT, a * P:(a + 1) * P], wqk[:, a, :], ident[:])
            mm.then_inc(s_wT, 1)
            pe.wait_ge(s_wTs, 1)
            for h in range(HEADS):
                w = slice(h * FEAT, (h + 1) * FEAT)
                nc.tensor.matmul(turnB[0:FEAT, w], wqkvT[:, 0, w], wqkvT[:, 1, w], start=True, stop=True)
                mm = nc.tensor.matmul(turnB[0:FEAT, P + h * FEAT:P + (h + 1) * FEAT], wqkvT[:, 2, w], wout,
                                      start=True, stop=True)
            mm.then_inc(s_gps, 1)
            pe.wait_ge(s_cross, 1)
            for a in range(3):
                mm = nc.tensor.transpose(small[0:FEAT, a * P:(a + 1) * P], crossing[:, a, :], ident[:])
            mm.then_inc(s_crossT, 1)
            pe.wait_ge(s_flags, 1)
            pe.wait_ge(s_gsb, 1)
            pe.wait_ge(s_feat, 16 * 9)
            pe.wait_ge(s_w2, 16 * 13)

            def prepare(g, b):
                if not (isinstance(g, int) and g == 0):
                    pe.wait_ge(s_hid, g)
                pe.wait_ge(s_embB, g + 1)
                nc.tensor.transpose(small[0:GA * EMB, 0:P], emb_blk[:, b], ident[:]).then_inc(s_embT, 1)
                pe.wait_ge(s_embS, g + 1)
                nc.tensor.matmul(small[:, P:P + GA * HID], embT, w1bd[:], start=True, stop=True).then_inc(s_hps, 1)
                pe.wait_ge(s_chan, g + 1)
                for t in range(GA):
                    pair = t // 2
                    bank = (turnA, turnB)[pair % 2][:, :].bitcast(BF16).rearrange("c (t a e) -> c t a e", t=2, a=4)
                    if t in (4, 6):
                        pe.wait_ge(s_turned, g * 4 + pair - 1)
                    nc.tensor.transpose(bank[:, t % 2, 0, :], stack_s[:, t].rearrange("p a c -> p (a c)"), identb[:])
                    for k in range(3):
                        mm = nc.tensor.transpose(bank[0:6 * VU, t % 2, 1 + k, :],
                                                 stack_v[:, 3 * t + k].rearrange("p a c -> p (a c)"), identb[:])
                    if t % 2 or t == GA - 1:
                        mm.then_inc(s_turn, 1)

            def products(g, b):
                for t in range(GA):
                    n = g * GA + t
                    if t % 2 == 0:
                        pe.wait_ge(s_turned, g * 4 + (t // 2 + 1))
                    pe.wait_ge(s_tfree, n + 1)
                    bank = tens[(b + t) % 2]
                    for turn in range(2):
                        nc.tensor.matmul(bank[:, 0:HID * OG], stackT_s[:, t, :],
                                         w_s[:, turn].rearrange("c j o -> c (j o)"), start=(turn == 0),
                                         stop=(turn == 1))
                    vec = bank[:, 512:512 + HID * OG].rearrange("p (j o) -> p j o", o=OG)
                    for k in range(3):
                        mm = nc.tensor.matmul(vec[:, :, k * MOUT:(k + 1) * MOUT], stackT_v[:, t, k, :], w_v[:],
                                              start=True, stop=True)
                    mm.then_inc(s_tens, 1)

            prepare(0, 0)
            with pe.Fori(0, ITA - 1) as i:
                for b in range(2):
                    products(i * 2 + b, b)
                    prepare(i * 2 + b + 1, 1 - b)
            products(NGA - 2, 0)
            prepare(NGA - 1, 1)
            products(NGA - 1, 1)

            def cross(n, done):
                pe.wait_ge(s_ends, done + 1)
                nc.tensor.transpose(small[0:n, 0:P], ends[:, 0, 0:n], ident[:])
                nc.tensor.transpose(small[0:n, P:2 * P], ends[:, 1, 0:n], ident[:]).then_inc(s_endT, 1)
                pe.wait_ge(s_carT, done + 1)
                nc.tensor.transpose(small[:, 2 * P:2 * P + n], carryT[0:n, 0, :], ident[0:n, 0:n])
                nc.tensor.transpose(small[:, 2 * P + FEAT:2 * P + FEAT + n], carryT[0:n, 1, :],
                                    ident[0:n, 0:n]).then_inc(s_car, 1)

            cross(FEAT, 0)

            pe.wait_ge(s_h1d, 1)
            pe.wait_ge(s_gbd, 16 * 2 * GB)
            pe.wait_ge(s_dd, 1)
            with pe.Fori(0, ITB) as i:
                for s in range(NSB):
                    k = i * NSB + s
                    hold(pe, "pe", (s_qfree, k + 1))
                    pe.wait_ge(s_hdB, k + 1)
                    nc.tensor.transpose(turnA[:, 0:P], h1d_blk, ident[:]).then_inc(s_hdT, 1)
                    pe.wait_ge(s_hdS, k + 1)
                    nc.tensor.matmul(tens[s % 2][:, 0:GB * P], h1dT, gbd[:, :, :].rearrange("p t e -> p (t e)"),
                                     start=True, stop=True).then_inc(s_q, 1)
                    pe.wait_ge(s_bh, k + 1)
                    nc.tensor.transpose(turnB[:, 0:P], h1s[:, s].rearrange("p t f -> p (t f)"),
                                        ident[:]).then_inc(s_hsT, 1)

            cross(HEADS, 1)
            cross(HEADS, 2)

            pe.wait_ge(s_hsS, NGB)
            with pe.Fori(0, ITB) as i:
                for s in range(NSB):
                    k = i * NSB + s
                    hold(pe, "pe", (s_vfree, k + 1), (s_hvB, k + 1))
                    nc.tensor.matmul(tens[s % 2][:, 0:GB * P], h1sT_ring[:, s].rearrange("p t f -> p (t f)"),
                                     ubd[:, :, :].rearrange("p t e -> p (t e)"),
                                     start=True, stop=True).then_inc(s_v, 1)
            cross(FEAT, 3)

        @block.vector
        def _(dve):
            v = nc.vector

            def cols(ap, start, n):
                return ap[:, start:start + n] if isinstance(start, int) else ap[:, bass.ds(start, n)]

            def spread(ap, axis, dims):
                full = [slice(None)] * (len(ap.shape) + 1)
                full[axis] = None
                return ap[tuple(full)].to_broadcast(dims)

            q = slice(96, P)
            v.memset(idx[:], 0)
            v.memset(edge_i[:], -1)
            v.memset(dst_i[q, TAIL:T], int(BIG))
            v.memset(unit[q, TAIL:T, :], 1.0)
            v.memset(wn[q, TAIL:T], 0.0)
            v.memset(emb[q, TAIL:T, :], 0.0).then_inc(s_pad, 1)
            v.memset(zeros, 0.0).then_inc(s_zset, 1)
            v.memset(w1bd[:], 0.0)
            v.memset(w_s[3 * SC:4 * SC, 1], 0.0)
            v.memset(gbd[:], 0.0)
            v.memset(ubd[:], 0.0).then_inc(s_wz, 1)
            v.memset(run[:, 0, :], 0.0)
            v.memset(eps[:], EPS)
            v.memset(same[:], 0.0)
            v.memset(stat[:], 1.0)
            v.memset(keepT[:], 0.0)
            v.memset(endT[:], 0.0)
            v.memset(runT, 0.0)
            v.memset(sameT, 0.0)
            v.memset(wscale[0:SC], 1.5 ** 0.5 * PW_V)
            v.drain()
            v.memset(wscale[0:VU], PW_V)

            dve.wait_ge(s_edges, 16 * 9)
            v.tensor_copy(dstf[:], dst_i[:])
            v.tensor_copy(edge_f[:], edge_i[:])
            v.drain()
            v.tensor_scalar(idx[:, 1, 0:T], dstf[:], float(N - 1), None, ALU.min)
            v.drain()
            for b in range(2):
                v.tensor_copy(idx_ring[:, b], idx[:, :, b * GA:(b + 1) * GA])
            v.drain().then_inc(s_istg, 2)

            v.tensor_tensor(same[:, 1:T], dstf[:, 1:T], dstf[:, 0:T - 1], ALU.is_equal)
            v.tensor_scalar(first_run[:], dstf[:], dstf[:, 0:1], None, ALU.is_equal)
            v.tensor_scalar(last_run[:], dstf[:], dstf[:, T - 1:T], None, ALU.is_equal)
            v.tensor_tensor(crossing[:, 0, 0:1], edge_f[:, 0:1], dstf[:, 0:1], ALU.is_equal)
            v.tensor_tensor(crossing[:, 1, 0:1], dstf[:, T - 1:T], edge_f[:, 1:2], ALU.is_equal)
            v.drain()
            v.tensor_copy(crossing[:, 2, :], first_run[:, T - 1:T].to_broadcast([P, FEAT]))
            v.tensor_copy(crossing[:, 0, 1:FEAT], crossing[:, 0, 0:1].to_broadcast([P, FEAT - 1]))
            v.tensor_copy(crossing[:, 1, 1:FEAT], crossing[:, 1, 0:1].to_broadcast([P, FEAT - 1])).then_inc(s_cross, 1)
            goes_on = same_far
            v.tensor_copy(goes_on[:, 0:T - 1], same[:, 1:T])
            v.drain()
            v.tensor_copy(goes_on[:, T - 1:T], crossing[:, 1, 0:1])
            v.drain()
            v.tensor_tensor(goes_on[:, 0:T], goes_on[:, 0:T], first_run[:], ALU.max)
            v.tensor_tensor(fixrow[:, 0:1], crossing[:, 1, 0:1], crossing[:, 2, 0:1], ALU.mult)
            v.drain()
            v.scalar_tensor_tensor(sidx[:], goes_on[:, 0:T], BIG, dstf[:], ALU.mult, ALU.add)
            v.scalar_tensor_tensor(fixidx[:], fixrow[:, 0:1], BIG, dstf[:, 0:1], ALU.mult, ALU.add)

            dve.wait_ge(s_feat, 16 * 9)
            v3 = msg_flat[:, 0:3 * T].rearrange("p (t c) -> p t c", c=3)
            v.tensor_tensor(v3, unit, unit, ALU.mult)
            v.tensor_scalar(wn, wn, TANH_GAIN, None, ALU.mult)
            v.drain()
            v.tensor_reduce(dstf[:], v3, AX, ALU.add).then_inc(s_vsq, 1)

            dve.wait_ge(s_crossT, 1)
            v.tensor_copy(flagT[:], small[0:FEAT, 0:3 * P].rearrange("p (a e) -> p a e", a=3))
            v.drain()
            v.tensor_tensor(keepT[:, 0, 1:P], flagT[:, 0, 1:P], flagT[:, 2, 0:P - 1], ALU.mult)
            v.tensor_tensor(keepT[:, 1, 0:P - 1], flagT[:, 1, 0:P - 1], flagT[:, 2, 1:P], ALU.mult)
            v.drain()
            for a in range(2):
                v.tensor_scalar(farT[:, a, :], flagT[:, a, :], FAR, -FAR, ALU.mult, ALU.add)
                v.tensor_scalar(farT[:, 2 + a, :], keepT[:, a, :], FAR, -FAR, ALU.mult, ALU.add)
            v.drain().then_inc(s_flags, 1)

            dve.wait_ge(s_vstd, 1)
            v.reciprocal(dstf[:], same_far[:, 0:T])
            v.drain()
            v.tensor_tensor(unit, unit, spread(dstf[:], 2, [P, T, 3]), ALU.mult)

            dve.wait_ge(s_wl, 16 * N_LOADS)
            v.tensor_scalar(w2s[:, :, 0:2 * MOUT], w2s[:, :, 0:2 * MOUT], PW_S, None, ALU.mult)
            v.tensor_scalar(w2s[:, :, 2 * MOUT:], w2s[:, :, 2 * MOUT:], wscale[0:SC, 0:1], None, ALU.mult)
            v.tensor_scalar(w2d, w2d, PW_V * 3.0 ** -0.5, None, ALU.mult)
            v.drain()
            v.scalar_tensor_tensor(w2v, w2e, -PW_V * 6.0 ** -0.5, w2d, ALU.mult, ALU.add)
            v.drain()
            for part in range(3):
                for whole, rest, parts in ((w2s, w2s_rest, w2s_part), (w2v, w2v_rest, w2v_part)):
                    v.tensor_copy(parts[:, part], whole if part == 0 else rest)
                v.drain()
                for whole, rest, parts in ((w2s, w2s_rest, w2s_part), (w2v, w2v_rest, w2v_part)):
                    if part < 2:
                        v.tensor_tensor(rest, whole if part == 0 else rest, parts[:, part], ALU.subtract)
                v.drain()
            v.drain().then_inc(s_w2p, 1)

            dve.sem_inc(s_tfree, 2)
            dve.sem_inc(s_rawd, 2)
            NG2 = 2 * GA

            def centre(b_next, turn, g, b, dense_wait):
                if b_next is not None:
                    hold(dve, "dve", (s_gath[b_next], turn * (16 * 2 * GA)))
                    rows = raw[:, b_next].rearrange("p t s f -> p (t s) f")
                    v.tensor_reduce(stat[:, 0, 0:NG2], rows, AX, ALU.add)
                if g is not None:
                    hold(dve, "dve", (s_xl[b], dense_wait))
                    v.tensor_reduce(stat[:, 0, NG2:NST], xin[:, b], AX, ALU.add)
                v.drain()
                v.tensor_scalar(stat[:, 3, :], stat[:, 0, :], 1.0 / FEAT, None, ALU.mult)
                v.drain()
                if b_next is not None:
                    last = v.tensor_tensor(cen, rows, spread(stat[:, 3, 0:NG2], 2, [P, NG2, FEAT]), ALU.subtract)
                    last.then_inc(s_rawd, 1)
                if g is not None:
                    last = v.tensor_tensor(dcen[:], xin[:, b], spread(stat[:, 3, NG2:NST], 2, [P, DR, FEAT]),
                                           ALU.subtract)
                v.drain().then_inc(s_cen, 1)

            def variance(n, gathered, dense):
                dve.wait_ge(s_sq, n)
                if gathered:
                    last = v.tensor_reduce(stat[:, 1, 0:NG2], sqr, AX, ALU.add)
                if dense:
                    last = v.tensor_reduce(stat[:, 1, NG2:NST], dsqr[:], AX, ALU.add)
                v.drain().then_inc(s_var, 1)

            def channels(g):
                scale = stat[:, 3, 0:NG2].rearrange("p (t s) -> p t s", s=2)
                v.tensor_tensor(val_s[:, :, 0:VU].rearrange("p t (s u) -> p t s u", s=2), pos[:, :, :, 0:MOUT],
                                spread(scale, 3, [P, GA, 2, MOUT]), ALU.mult)
                for side in range(2):
                    v.tensor_tensor(val_v[:, :, :, side * MOUT:(side + 1) * MOUT].rearrange("p t k u -> p t u k"),
                                    pos[:, :, side, MOUT:].rearrange("p t (u k) -> p t u k", k=3),
                                    scale[:, :, side:side + 1][:, :, :, None].to_broadcast([P, GA, MOUT, 3]), ALU.mult)
                v.drain()
                v.tensor_tensor(vprod, val_v.rearrange("p t k u -> p t u k"),
                                spread(cols(unit, g * GA, GA), 2, [P, GA, VU, 3]), ALU.mult)
                v.drain()
                v.tensor_reduce(val_s[:, :, VU:], vprod, AX, ALU.add).then_inc(s_val, 1)

            def first_rest(n):
                dve.wait_ge(s_part1, n)
                v.tensor_tensor(rest_s, val_s, stack_s[:, :, 0, :], ALU.subtract)
                v.tensor_tensor(rest_v, val_v.rearrange("p t k u -> p (t k) u"), stack_v[:, :, 0, :],
                                ALU.subtract).then_inc(s_rest1, 1)

            def third_part(n):
                dve.wait_ge(s_part2, n)
                v.tensor_tensor(stack_s[:, :, 2, :], rest_s, stack_s[:, :, 1, :], ALU.subtract)
                v.tensor_tensor(stack_v[:, :, 5, :], rest_v, stack_v[:, :, 1, :], ALU.subtract).then_inc(s_chan, 1)

            def multiply(g, b, t):
                dve.wait_ge(s_tens, g * GA + (t + 1))
                v.tensor_tensor(
                    prod[:, 2 * t:2 * t + 2],
                    tens[(b + t) % 2][:, :].rearrange("p (a c) -> p a c", a=2)[:, :, 0:HID * OG].rearrange(
                        "p a (j o) -> p a j o", o=OG),
                    hid[:, b, t, :][:, None, :, None].to_broadcast([P, 2, HID, OG]), ALU.mult).then_inc(s_tfree, 1)

            def messages(g, b):
                v.drain()
                v.tensor_reduce(outs.rearrange("p t (a o) -> p (t a) o", a=2), prod.rearrange("p b j o -> p b o j"),
                                AX, ALU.add).then_inc(s_outs, 1)
                v.tensor_copy(msgT[:, :, 0:1], runT[:, 1 - b, :, GA:])
                v.drain()
                v.tensor_tensor(vmix, spread(outs[:, :, 2 * MOUT:3 * MOUT], 3, [P, GA, MOUT, 3]),
                                spread(cols(unit, g * GA, GA), 2, [P, GA, MOUT, 3]), ALU.mult)
                v.drain()
                v.tensor_tensor(vmix, vmix, outs[:, :, 3 * MOUT:].rearrange("p t (k w) -> p t w k", k=3), ALU.add)
                hold(dve, "dve", (s_tanh, g + 1))
                v.tensor_tensor(gate[:, 1], gate[:, 0], spread(cols(wn, g * GA, GA), 2, [P, GA, 2 * MOUT]), ALU.mult)
                v.drain()
                hold(dve, "dve", (s_mfree, g + 1), (s_same, g + 1))
                v.tensor_copy(msgT[:, 0:MOUT, 1:].rearrange("p f t -> p t f"), gate[:, 1, :, 0:MOUT])
                v.tensor_tensor(msgT[:, MOUT:, 1:].rearrange("p (w k) t -> p t w k", k=3), vmix,
                                spread(gate[:, 1, :, MOUT:], 3, [P, GA, MOUT, 3]), ALU.mult)
                v.drain()
                v.tensor_tensor_scan(runT[:, b].rearrange("p f t -> p (f t)"),
                                     sameT[:, b].rearrange("p f t -> p (f t)"),
                                     msgT.rearrange("p f t -> p (f t)"), 0.0, ALU.mult, ALU.add).then_inc(s_run, 1)

            def invert(n):
                dve.wait_ge(s_std, n)
                v.reciprocal(stat[:, 3, :], stat[:, 2, :])
                v.drain()

            def layer0(i, b, last):
                g = i * 2 + b
                wait = (i + 1) * 16
                if last:
                    wait = (i + 2) * 16
                centre(None if last else 1 - b, i + 1 + b, g, b, wait)
                dve.wait_ge(s_hid, g + 1)
                for t in range(0, 3):
                    multiply(g, b, t)
                variance(g + 2, not last, True)
                for t in range(3, 5):
                    multiply(g, b, t)
                invert(g + 2)
                if not last:
                    channels(g + 1)
                multiply(g, b, 5)
                v.scalar_tensor_tensor(dcen[:], dcen[:], 0.0, spread(stat[:, 3, NG2:NST], 2, [P, DR, FEAT]),
                                       ALU.max, ALU.mult)
                if not last:
                    first_rest(g + 2)
                multiply(g, b, 6)
                v.drain()
                v.tensor_tensor(xin[:, b], xin[:, b], dcen[:], ALU.add).then_inc(s_ddone, 1)
                if not last:
                    third_part(g + 2)
                messages(g, b)

            centre(0, 1, None, None, None)
            dve.wait_ge(s_gbd, 16 * 2 * GB)
            variance(1, True, False)
            invert(1)
            channels(0)
            first_rest(1)
            third_part(1)
            with dve.Fori(0, ITA - 1) as i:
                for b in range(2):
                    layer0(i, b, False)
            layer0(ITA - 1, 0, False)
            layer0(ITA - 1, 1, True)

            dve.wait_ge(s_mfree, NGA + 1)
            v.drain()
            for f in range(FEAT):
                v.tensor_tensor_scan(back[:, ::-1, f], same[:, T:0:-1], msg[:, ::-1, f], 0.0, ALU.mult, ALU.add)

            def cross(n, done, far):
                v.drain().then_inc(s_ends, 1)
                dve.wait_ge(s_endT, done + 1)
                if far:
                    v.memset(endT[0:n, 0, 0:1], -FAR)
                    v.memset(endT[0:n, 1, P - 1:P], -FAR)
                f0, f1 = (farT[0:n, 0], farT[0:n, 1]) if far else (flagT[0:n, 0], flagT[0:n, 1])
                k0, k1 = (farT[0:n, 2], farT[0:n, 3]) if far else (keepT[0:n, 0], keepT[0:n, 1])
                op = ALU.add if far else ALU.mult
                v.tensor_tensor(endT[0:n, 0, 1:P], f0[:, 1:P], small[0:n, 0:P - 1], op)
                v.tensor_tensor(endT[0:n, 1, 0:P - 1], f1[:, 0:P - 1], small[0:n, P + 1:2 * P], op)
                v.drain()
                init = -FAR if far else 0.0
                op1 = ALU.max if far else ALU.add
                v.tensor_tensor_scan(carryT[0:n, 0, :], k0, endT[0:n, 0, :], init, op, op1)
                v.tensor_tensor_scan(carryT[0:n, 1, ::-1], k1[:, ::-1], endT[0:n, 1, ::-1], init, op, op1)
                v.drain().then_inc(s_carT, 1)
                dve.wait_ge(s_car, done + 1)
                v.tensor_copy(carry[:, :, 0:n], small[:, 2 * P:2 * P + 2 * FEAT].rearrange(
                    "p (a n) -> p a n", a=2)[:, :, 0:n])
                if far:
                    v.memset(endT[0:n, 0, 0:1], 0.0)
                    v.memset(endT[0:n, 1, P - 1:P], 0.0)
                v.drain()

            v.drain()
            v.tensor_copy(ends[:, 0, :], run[:, T, :])
            v.tensor_copy(ends[:, 1, :], back[:, 0, :])
            cross(FEAT, 0, False)
            v.tensor_tensor(fixrow[:], back[:, 0, :], carry[:, 0, :], ALU.add).then_inc(s_fix, 1)

            v.drain()
            v.tensor_tensor(back[:], back[:], msg[:], ALU.subtract)
            v.drain()
            v.tensor_tensor(back[:], back[:], run[:, 1:, :], ALU.add)
            for a, at in ((0, first_run), (1, last_run)):
                v.drain()
                v.tensor_tensor(msg[:], spread(at[:], 2, [P, T, FEAT]), spread(carry[:, a, :], 1, [P, T, FEAT]),
                                ALU.mult)
                v.drain()
                v.tensor_tensor(back[:], back[:], msg[:], ALU.add)
            v.drain()
            v.tensor_tensor(x1d, x1d, back[:], ALU.add)
            v.drain()

            s0, s1, s2, s3 = (seg_f[:, a, :] for a in range(4))
            v.tensor_reduce(s0, x1d, AX, ALU.add)
            v.drain()
            v.tensor_scalar(s3, s0, 1.0 / FEAT, None, ALU.mult)
            v.drain()
            v.tensor_tensor(msg[:], x1d, spread(s3, 2, [P, T, FEAT]), ALU.subtract).then_inc(s_dc, 1)
            dve.wait_ge(s_dq, 1)
            v.tensor_reduce(s1, back[:], AX, ALU.add).then_inc(s_dv, 1)
            dve.wait_ge(s_dd, 1)
            v.reciprocal(s3, s2)
            v.drain()
            v.scalar_tensor_tensor(h1d[:], msg[:], 0.0, spread(s3, 2, [P, T, FEAT]), ALU.max,
                                   ALU.mult).then_inc(s_h1d, 1)
            v.drain()
            v.tensor_tensor(base[:, 0:T, :], x1d, h1d[:], ALU.add)

            dve.sem_inc(s_agread, NSB)
            dve.sem_inc(s_qfree, 1)

            def source_rows(i, s, turn):
                k = i * NSB + s
                hold(dve, "dve", (s_gb[s], turn * (16 * GB)))
                v.tensor_tensor(x1s[:, s], agg_ring[:, s],
                                xsd[:, k * GB:(k + 1) * GB, 0, :] if isinstance(k, int)
                                else xsd[:, bass.ds(k * GB, GB), 0, :], ALU.add).then_inc(s_agread, 1)
                v.drain()
                v.tensor_reduce(stat_b[:, s, 0, :], x1s[:, s], AX, ALU.add)
                v.drain()
                v.tensor_scalar(stat_b[:, s, 3, :], stat_b[:, s, 0, :], 1.0 / FEAT, None, ALU.mult)
                v.drain()
                v.tensor_tensor(c1s[:, s], x1s[:, s], spread(stat_b[:, s, 3, :], 2, [P, GB, FEAT]),
                                ALU.subtract).then_inc(s_bc, 1)

            source_rows(0, 0, 1)

            def scores(i, s, last):
                k = i * NSB + s
                if not last:
                    if s + 1 < NSB:
                        source_rows(i, s + 1, i + 1)
                    else:
                        source_rows(i + 1, 0, i + 2)
                dve.wait_ge(s_bq, k + 1)
                v.tensor_reduce(stat_b[:, s, 1, :], q1s[:, s], AX, ALU.add).then_inc(s_bv, 1)
                dve.wait_ge(s_bd, k + 1)
                v.reciprocal(stat_b[:, s, 3, :], stat_b[:, s, 2, :])
                v.drain()
                v.scalar_tensor_tensor(h1s[:, s], c1s[:, s], 0.0, spread(stat_b[:, s, 3, :], 2, [P, GB, FEAT]),
                                       ALU.max, ALU.mult).then_inc(s_bh, 1)
                v.drain()
                dve.wait_ge(s_q, k + 1)
                v.tensor_tensor(hprod, tens[s % 2][:, 0:GB * P].rearrange("p (t h f) -> p t h f", t=GB, h=HEADS),
                                spread(h1s[:, s], 2, [P, GB, HEADS, FEAT]), ALU.mult).then_inc(s_qfree, 1)
                v.drain()
                sc = score[:, :, k * GB:(k + 1) * GB] if isinstance(k, int) else score[:, :, bass.ds(k * GB, GB)]
                v.tensor_reduce(sc.rearrange("p h t -> p t h"), hprod, AX, ALU.add)

            with dve.Fori(0, ITB - 1) as i:
                for s in range(NSB):
                    scores(i, s, False)
            for s in range(NSB):
                scores(ITB - 1, s, s == NSB - 1)

            v.tensor_scalar(same_far[:], same[:], FAR, -FAR, ALU.mult, ALU.add)
            v.tensor_scalar(first_far, first_run[:], FAR, -FAR, ALU.mult, ALU.add)
            v.tensor_scalar(last_far, last_run[:], FAR, -FAR, ALU.mult, ALU.add)
            v.drain()
            for h in range(HEADS):
                v.tensor_tensor_scan(seg_f[:, h, :], same_far[:, 0:T], score[:, h, :], -FAR, ALU.add, ALU.max)
                v.tensor_tensor_scan(seg_b[:, h, ::-1], same_far[:, T:0:-1], score[:, h, ::-1], -FAR, ALU.add,
                                     ALU.max)
            v.drain()
            v.tensor_copy(ends[:, 0, 0:HEADS], seg_f[:, :, T - 1])
            v.tensor_copy(ends[:, 1, 0:HEADS], seg_b[:, :, 0])
            v.tensor_tensor(seg_m, seg_f, seg_b, ALU.max)
            cross(HEADS, 1, True)
            for a, at in ((0, first_far), (1, last_far)):
                v.tensor_tensor(seg_f, spread(at, 1, [P, HEADS, T]), spread(carry[:, a, 0:HEADS], 2, [P, HEADS, T]),
                                ALU.add)
                v.drain()
                v.tensor_tensor(seg_m, seg_m, seg_f, ALU.max)
                v.drain()
            v.tensor_tensor(seg_b, score, seg_m, ALU.subtract).then_inc(s_sm, 1)
            dve.wait_ge(s_e, 1)
            for h in range(HEADS):
                v.tensor_tensor_scan(seg_f[:, h, :], same[:, 0:T], seg_m[:, h, :], 0.0, ALU.mult, ALU.add)
                v.tensor_tensor_scan(seg_b[:, h, ::-1], same[:, T:0:-1], seg_m[:, h, ::-1], 0.0, ALU.mult, ALU.add)
            v.drain()
            v.tensor_copy(ends[:, 0, 0:HEADS], seg_f[:, :, T - 1])
            v.tensor_copy(ends[:, 1, 0:HEADS], seg_b[:, :, 0])
            v.drain()
            v.tensor_tensor(seg_b, seg_b, seg_m, ALU.subtract)
            v.drain()
            v.tensor_tensor(seg_b, seg_b, seg_f, ALU.add)
            cross(HEADS, 2, False)
            for a, at in ((0, first_run), (1, last_run)):
                v.tensor_tensor(seg_f, spread(at[:], 1, [P, HEADS, T]), spread(carry[:, a, 0:HEADS], 2, [P, HEADS, T]),
                                ALU.mult)
                v.drain()
                v.tensor_tensor(seg_b, seg_b, seg_f, ALU.add)
                v.drain()
            v.reciprocal(seg_f, seg_b)
            v.drain()
            v.tensor_tensor(score, seg_m, seg_f, ALU.mult)
            v.memset(yrun, 0.0)
            v.memset(yfirst, 0.0)
            v.drain()

            dve.sem_inc(s_vfree, 1)
            dve.sem_inc(s_vused, NSB)
            with dve.Fori(0, ITB) as i:
                for s in range(NSB):
                    k = i * NSB + s
                    hold(dve, "dve", (s_v, k + 1))
                    v.tensor_tensor(hprod, tens[s % 2][:, 0:GB * P].rearrange("p (t h f) -> p t h f", t=GB, h=HEADS),
                                    score[:, :, bass.ds(k * GB, GB)].rearrange("p h t -> p t h")[:, :, :, None]
                                    .to_broadcast([P, GB, HEADS, FEAT]), ALU.mult).then_inc(s_vfree, 1)
                    v.drain().then_inc(s_vused, 1)
                    v.tensor_reduce(yrow[:, s], hprod.rearrange("p t h f -> p t f h"), AX, ALU.add)
                    v.drain()
                    v.tensor_tensor(ytmp, yrow[:, s], spread(first_run[:, bass.ds(k * GB, GB)], 2, [P, GB, FEAT]),
                                    ALU.mult)
                    for t in range(GB):
                        before = yrun[:, s, t - 1, :] if t else yrun[:, (s - 1) % NSB, GB - 1, :]
                        v.scalar_tensor_tensor(yrun[:, s, t, :], before, same[:, bass.ds(k * GB + t, 1)],
                                               yrow[:, s, t, :], ALU.mult, ALU.add)
                        v.drain()
                    v.tensor_tensor(yfirst, yfirst, ytmp, ALU.add)
                    hold(dve, "dve", (s_ofree, k + 1))
                    v.tensor_tensor(out_ring[:, s], yrun[:, s], base[:, bass.ds(k * GB, GB), :],
                                    ALU.add).then_inc(s_orow, 1)
            v.drain()
            v.tensor_copy(ends[:, 0, :], yrun[:, NSB - 1, GB - 1, :])
            v.tensor_reduce(ends[:, 1, :], yfirst.rearrange("p t f -> p f t"), AX, ALU.add)
            v.drain()
            v.tensor_tensor(fixrow[:], base[:, 0, :], ends[:, 1, :], ALU.add)
            cross(FEAT, 3, False)
            v.tensor_tensor(fixrow[:], fixrow[:], carry[:, 0, :], ALU.add).then_inc(s_fix, 1)


_INS = ['x', 'src', 'dst', 'edge_attr_10', 'edge_attr_3', 'edge_weight', 'L0_gnn_W1', 'L0_gnn_W2',
        'L1_gnn_Wq', 'L1_gnn_Wk', 'L1_gnn_Wv', 'L1_gnn_Wout']


def kernel(**inputs):
    import numpy as _np
    import concourse.bacc as _bacc
    from concourse import mybir as _mybir
    from concourse.bass_utils import run_bass_kernel_spmd as _run

    nc = _bacc.Bacc("TRN2", target_bir_lowering=False, num_devices=1)
    arrays, args = {}, []
    for name in _INS:
        a = _np.ascontiguousarray(inputs[name])
        arrays[f"in_{name}"] = a
        args.append(nc.dram_tensor(f"in_{name}", a.shape, _mybir.dt.from_np(a.dtype), kind="ExternalInput").ap())
    shape = arrays["in_x"].shape
    args.append(nc.dram_tensor("out_dram", shape, _mybir.dt.float32, kind="ExternalOutput").ap())
    build_gnn(nc, *args)
    return _run(nc, [arrays], core_ids=[0]).results[0]["out_dram"]
```

```python
import numpy as np
import concourse.bass as bass
from concourse import mybir
from contextlib import ExitStack

F32 = mybir.dt.float32
I32 = mybir.dt.int32
BF16 = mybir.dt.bfloat16
ALU = mybir.AluOpType
ACT = mybir.ActivationFunctionType
AX = mybir.AxisListType.X

P = 128
FEAT = 32
EMB = 10
HID = 16
MOUT = 8
HEADS = 4
EPS = 1e-5
TANH_GAIN = 1.593
PW_S = 0.17677669529663687
PW_V = 0.25
BIG = float(1 << 20)
FAR = 1.0e30


def build_gnn(nc, x, src, dst, attr10, attr3, weight, W1, W2, Wq, Wk, Wv, Wout, out):
    N = x.shape[0]
    E = src.shape[0]
    T = -(-E // P)
    T = -(-T // 98) * 98
    TAIL = E - (P - 1) * T

    GA = 7
    NGA = T // GA
    TPE = 4
    TACT = 3
    VT = GA - 1
    LAG = 3
    ITA = NGA // 2
    GB = 7
    BT = 4
    NSB = 14
    NGB = T // GB
    ITB = NGB // NSB
    HT = GB * NSB
    assert 0 < TAIL <= T and T % (2 * GA) == 0 and T % HT == 0
    SC = 4 * MOUT
    VU = 2 * MOUT
    OG = 3 * MOUT
    OUTS = 2 * OG
    RPP = N // P
    DR = -(-RPP // NGA)
    DLAST = RPP - (NGA - 1) * DR
    DREM = N - P * RPP
    assert 0 < DLAST < DR and DREM <= P and NGA % 2 == 0

    agg = nc.dram_tensor("agg_rows", [N, FEAT], F32, kind="Internal").ap()

    ctx = ExitStack()
    with ctx:
        def sb(name, shape, dt=F32):
            return ctx.enter_context(nc.sbuf_tensor(name, shape, dt))

        def pb(name, cols=512):
            return ctx.enter_context(nc.psum_tensor(name, [P, cols], F32))

        def sem(name):
            return ctx.enter_context(nc.semaphore(name))

        idx = sb("idx", [P, 2, T + HT], I32)
        sidx = sb("sidx", [P, T], I32)
        fixidx = sb("fixidx", [P, 1], I32)
        dst_i = sb("dst_i", [P, T], I32)
        edge_i = sb("edge_i", [P, 2], I32)
        edge_f = sb("edge_f", [P, 2])
        dstf = sb("dstf", [P, T])
        same = sb("same", [P, T + 1])
        first_run = sb("first_run", [P, T])
        last_run = sb("last_run", [P, T])
        crossing = sb("crossing", [P, 3, FEAT])
        xsd = sb("xsd", [P, T, 2, FEAT])
        msg = sb("msg", [P, T, FEAT])
        run = sb("run", [P, T + 1, FEAT])
        back = sb("back", [P, T, FEAT])
        x1d = xsd[:, :, 1, :]
        h1d = msg
        h1s_rows = back
        prod = back[:, :, :].rearrange("p t f -> p (t f)")[:, 0:GA * HID * OUTS].rearrange(
            "p (b j o) -> p b j o", b=2 * GA, o=OG)

        ident = sb("ident", [P, P])
        eps = sb("eps", [P, 1])
        wscale = sb("wscale", [P, 1])
        w1bd = sb("w1bd", [GA * EMB, GA * HID])
        w_s = sb("w2_scalar_stack", [4 * SC, 2, HID, OG], BF16)
        w_v = sb("w2_vector_stack", [6 * VU, HID, MOUT], BF16)
        identb = sb("identb", [P, P], BF16)
        gbd = sb("gbd", [P, BT, P])
        ubd = sb("ubd", [P, BT, P])

        area_a = sb("features_or_scores", [P, 4 * HEADS * T])
        taken_a = {0: 0, 1: 0}

        def in_a(layer, *dims):
            n, at = int(np.prod(dims)), taken_a[layer]
            taken_a[layer] += n
            assert taken_a[layer] <= 4 * HEADS * T
            v = area_a[:, at:at + n]
            names = "abc"[:len(dims)]
            return v.rearrange(f"p ({' '.join(names)}) -> p {' '.join(names)}", **dict(zip(names, dims))) \
                if len(dims) > 1 else v

        emb = in_a(0, T, EMB)
        unit = in_a(0, T, 3)
        wn = in_a(0, T)
        score = in_a(1, HEADS, T)
        seg_f = in_a(1, HEADS, T)
        seg_b = in_a(1, HEADS, T)
        seg_m = in_a(1, HEADS, T)

        AREA = 7832
        area_b = sb("working_buffers", [P, AREA])
        taken_b = {0: 0, 1: 0}

        def in_b(layer, *dims, parts=P):
            n, at = int(np.prod(dims)), taken_b[layer]
            taken_b[layer] += n
            assert taken_b[layer] <= AREA, taken_b
            v = area_b[0:parts, at:at + n]
            names = "abcd"[:len(dims)]
            return v.rearrange(f"p ({' '.join(names)}) -> p {' '.join(names)}", **dict(zip(names, dims))) \
                if len(dims) > 1 else v

        raw = in_b(0, 2, GA, 2, FEAT)
        cen = in_b(0, GA * 2, FEAT)
        sqr = in_b(0, GA * 2, FEAT)
        pos = in_b(0, GA, 2, FEAT)
        val_s = in_b(0, GA, SC)
        val_v = in_b(0, GA, 3, VU)
        stack_s = in_b(0, GA * 4 * SC // 2).bitcast(BF16).rearrange("p (t a c) -> p t a c", t=GA, a=4)
        stack_v = in_b(0, GA * 3 * 6 * VU // 2).bitcast(BF16).rearrange("p (t a c) -> p t a c", t=GA * 3, a=6)
        rest_s = sqr.rearrange("p n f -> p (n f)")[:, 0:GA * SC].rearrange("p (t c) -> p t c", c=SC)
        rest_v = cen.rearrange("p n f -> p (n f)")[:, 0:GA * 3 * VU].rearrange("p (t c) -> p t c", c=VU)
        vprod = pos.rearrange("p t s f -> p (t s f)")[:, 0:GA * 3 * VU].rearrange(
            "p (t u k) -> p t u k", t=GA, k=3)
        emb_blk = in_b(0, 2, GA * EMB)
        embT = in_b(0, P, parts=GA * EMB)
        hid = in_b(0, 2, GA, HID)
        stackT_s = in_b(0, GA * P // 2).bitcast(BF16).rearrange("c (t e) -> c t e", t=GA)
        stackT_v = in_b(0, GA * 3 * P // 2, parts=6 * VU).bitcast(BF16).rearrange("c (t k e) -> c t k e", t=GA, k=3)
        msgT = in_b(0, FEAT, GA + 1)
        runT = in_b(0, 2, FEAT, GA + 1)
        sameT = in_b(0, 2, FEAT, GA + 1)
        behind = back[:, :, :].rearrange("p t f -> p (t f)")[:, GA * HID * OUTS:]
        outs = behind[:, 0:GA * OUTS].rearrange("p (t o) -> p t o", t=GA)
        gate = behind[:, 336:336 + 4 * GA * MOUT].rearrange("p (a t o) -> p a t o", a=2, t=GA)
        vmix = behind[:, 560:560 + 3 * GA * MOUT].rearrange("p (t w k) -> p t w k", t=GA, w=MOUT)

        agg_ring = in_b(1, NSB, GB, FEAT)
        x1s = in_b(1, 2, GB, FEAT)
        c1s = in_b(1, 2, GB, FEAT)
        q1s = in_b(1, 2, GB, FEAT)
        h1s = in_b(1, 2, GB, FEAT)
        hprod = in_b(1, GB, HEADS, FEAT)
        rows_blk = in_b(1, 2, GB * FEAT)
        rowsT = in_b(1, 2, 2, P)
        ytmp = in_b(1, FEAT, GB)
        yfirst = in_b(1, FEAT, GB)
        first_far = in_b(1, T)
        last_far = in_b(1, T)
        out_ring = agg_ring
        assert 4 * 2 * GB * FEAT >= FEAT * (GB + 1) * 5 + 2 * GB * FEAT
        at = NSB * GB * FEAT

        def in_sources(*dims):
            nonlocal at
            n = int(np.prod(dims))
            at += n
            names = "abcd"[:len(dims)]
            return area_b[:, at - n:at].rearrange(f"p ({' '.join(names)}) -> p {' '.join(names)}",
                                                  **dict(zip(names, dims)))

        yrowT = in_sources(FEAT, GB + 1)
        yrunT = in_sources(2, FEAT, GB + 1)
        yflagT = in_sources(2, FEAT, GB + 1)
        ysum = in_sources(2, GB, FEAT)

        idx_ring = sb("idx_ring", [P, 2, 2, GA], I32)
        sidx_ring = sb("sidx_ring", [P, 2, GA], I32)
        idx_ring_b = sb("idx_ring_b", [P, NSB, GB], I32)
        sidx_ring_b = idx_ring_b
        row_ring = sb("row_ring", [P, 2, GA, FEAT])
        NST = 2 * GA + DR
        stat = sb("stat", [P, 4, NST])
        stat_b = sb("stat_b", [P, 2, 4, GB])
        xin = sb("xin", [P, 2, DR, FEAT])
        dcen = sb("dcen", [P, DR, FEAT])
        dsqr = sb("dsqr", [P, DR, FEAT])
        share = stat_b
        assert HEADS == 4
        fixrow = sb("fixrow", [P, FEAT])
        same_far = sb("same_far", [P, T + 1])

        flagT = sb("flagT", [FEAT, 3, P])
        keepT = sb("keepT", [FEAT, 2, P])
        farT = sb("farT", [FEAT, 4, P])
        ends = sb("ends", [P, 2, FEAT])
        endT = sb("endT", [FEAT, 2, P])
        carryT = sb("carryT", [FEAT, 2, P])
        carry = sb("carry", [P, 2, FEAT])

        back_flat = back[:, :, :].rearrange("p t f -> p (t f)")
        def in_back(at, parts, *dims):
            n = int(np.prod(dims))
            names = "abc"[:len(dims)]
            return back_flat[0:parts, at:at + n].rearrange(f"p ({' '.join(names)}) -> p {' '.join(names)}",
                                                           **dict(zip(names, dims)))

        w2s = in_back(0, SC, HID, OG)
        w2d = in_back(384, VU, HID, MOUT)
        w2e = in_back(512, VU, HID, MOUT)
        w2v = in_back(640, VU, HID, MOUT)
        w2s_rest = in_back(768, SC, HID, OG)
        w2v_rest = in_back(1152, VU, HID, MOUT)
        w2s_part = back_flat[0:SC, 1280:1280 + 576].bitcast(BF16).rearrange("p (a j o) -> p a j o", a=3, o=OG)
        w2v_part = back_flat[0:VU, 1856:1856 + 192].bitcast(BF16).rearrange("p (a j o) -> p a j o", a=3, o=MOUT)
        msg_flat = msg[:, :, :].rearrange("p t f -> p (t f)")
        v3 = msg_flat[:, 0:3 * T].rearrange("p (t c) -> p t c", c=3)
        length2 = msg_flat[:, 3 * T:4 * T]
        length = msg_flat[:, 4 * T:5 * T]
        ZR = 28
        zeros = xsd[:, T - ZR // 2:T, :, :].rearrange("p t s f -> p (t s f)")
        wtop = T * FEAT
        wqk = msg_flat[:, wtop - 96:wtop].rearrange("p (a f) -> p a f", a=3)
        wqkvT = msg_flat[0:FEAT, wtop - 512:wtop - 128].rearrange("p (a e) -> p a e", a=3)
        wout = msg_flat[0:FEAT, wtop - 128:wtop - 96]
        gu = msg_flat[0:FEAT, wtop - 768:wtop - 512].rearrange("p (a e) -> p a e", a=2)

        small = pb("small")
        turnA = pb("turnA")
        turnB = pb("turnB")
        tens = [pb("tens0", 1024), pb("tens1", 1024)]
        sums = pb("sums")

        s_pad = sem("edge_list_pads_set")
        s_padf = sem("feature_pads_set")
        s_edges = sem("edges_loaded")
        s_borders = sem("borders_loaded")
        s_feat = sem("edge_features_loaded")
        s_wz = sem("weight_buffers_zeroed")
        s_wl = sem("weights_loaded")
        s_w2p = sem("w2_parts_ready")
        s_w2 = sem("w2_stacks_loaded")
        s_wT = sem("attention_weights_turned")
        s_wTs = sem("turned_weights_on_sbuf")
        s_gps = sem("folded_weights_ready")
        s_gsb = sem("folded_weights_on_sbuf")
        s_gbd = sem("block_weights_loaded")
        s_flags = sem("partition_flags_ready")
        s_id0 = sem("identity_zeroed")
        s_id = sem("identity_ready")
        s_zset = sem("zeros_set")
        s_zfill = sem("agg_rows_zeroed")
        s_vsq = sem("vector_norms_summed")
        s_vstd = sem("vector_norms_ready")
        s_cross = sem("crossing_flags_ready")
        s_crossT = sem("crossing_flags_turned")
        s_istg = sem("indices_staged")
        s_gath = [sem("rows_gathered0"), sem("rows_gathered1")]
        s_rawd = sem("raw_read_by_vector")
        s_rawa = sem("raw_read_by_scalar")
        s_cen = sem("centred")
        s_sq = sem("squared")
        s_var = sem("variance_summed")
        s_std = sem("deviation_ready")
        s_val = sem("channels_ready")
        s_part1 = sem("first_parts_ready")
        s_rest1 = sem("first_rests_ready")
        s_part2 = sem("second_parts_ready")
        s_chan = sem("stacks_ready")
        s_same = sem("segment_flags_spread")
        s_mfree = sem("messages_kept")
        s_embB = sem("emb_block_staged")
        s_embT = sem("emb_turned")
        s_embS = sem("emb_on_sbuf")
        s_hps = sem("hidden_product_ready")
        s_hid = sem("hidden_ready")
        s_turn = sem("channels_turned")
        s_turned = sem("turned_channels_on_sbuf")
        s_tens = sem("tensor_product_ready")
        s_tfree = sem("tensor_product_read_by_vector")
        s_tact = sem("tensor_product_read_by_scalar")
        s_outs = sem("outputs_summed")
        s_psum = sem("first_tiles_outputs_summed")
        s_outc = sem("first_tiles_outputs_on_sbuf")
        s_tanh = sem("gates_ready")
        s_run = sem("running_sums_ready")
        s_rows = sem("scatter_rows_staged")
        s_rfree = sem("scatter_ring_free")
        s_scat = sem("agg_rows_scattered")
        s_xl = [sem("dense_rows_loaded0"), sem("dense_rows_loaded1")]
        s_ddone = sem("dense_rows_ready")
        s_dst = sem("dense_rows_stored")
        s_ends = sem("segment_ends_ready")
        s_endT = sem("segment_ends_turned")
        s_carT = sem("carries_scanned")
        s_car = sem("carries_ready")
        s_fix = sem("fix_rows_ready")
        s_fixd = sem("fix_rows_scattered")
        s_hdB = sem("dst_block_staged")
        s_hvB = sem("values_block_staged")
        s_hdT = sem("dst_rows_turned")
        s_hdS = sem("turned_dst_rows_on_sbuf")
        s_hvT = sem("src_rows_turned")
        s_hvS = sem("turned_src_rows_on_sbuf")
        s_first = sem("first_carries_spread")
        s_carried = sem("carries_on_sbuf")
        s_saved = sem("src_h_kept")
        s_h1d = sem("dst_h_ready")
        s_dc = sem("dst_centred")
        s_dq = sem("dst_squared")
        s_dv = sem("dst_variance_summed")
        s_dd = sem("dst_deviation_ready")
        s_istgb = sem("src_indices_staged")
        s_gb = [sem(f"agg_gathered{s}") for s in range(NSB)]
        s_agread = sem("agg_ring_read")
        s_bc = sem("src_centred")
        s_bq = sem("src_squared")
        s_bv = sem("src_variance_summed")
        s_bd = sem("src_deviation_ready")
        s_bh = sem("src_h_ready")
        s_q = sem("query_ready")
        s_qfree = sem("query_read")
        s_sm = sem("max_subtracted")
        s_e = sem("exponentials_ready")
        s_v = sem("values_ready")
        s_vfree = sem("values_read")
        s_yflag = sem("output_flags_spread")
        s_yfree = sem("output_flags_used")
        s_orow = sem("output_rows_ready")
        s_sstg = sem("output_indices_staged")
        s_ofree = sem("output_ring_free")
        s_osc = [sem(f"output_rows_scattered{s}") for s in range(NSB)]
        s_last = sem("last_rows_scattered")
        s_hold = {e: sem(f"held_{e}") for e in ("act", "dve", "pe", "pool", "sp")}

        def hold(eng, name, *waits):
            for s, v in waits:
                eng.wait_ge(s, v)
            eng.sem_inc(s_hold[name], 1)

        block = ctx.enter_context(nc.Block())

        def edge_loads(eng, dest, source, s):
            w = 1 if len(source.shape) == 1 else source.shape[1]
            flat = source if w == 1 else source.rearrange("e c -> (e c)")
            for a, b in ((0, 112), (112, P - 1)):
                v = flat[a * T * w:b * T * w].rearrange("(p n) -> p n", p=b - a)
                eng.dma_start(dest[a:b, 0:T * w], v).then_inc(s, 16)
            v = flat[(P - 1) * T * w:E * w].rearrange("(p n) -> p n", p=1)
            eng.dma_start(dest[P - 1:P, 0:TAIL * w], v).then_inc(s, 16)
            return 48

        ZC = N // (P * ZR)
        ZREST = (N - ZC * P * ZR) // P
        ZREM = N - ZC * P * ZR - P * ZREST
        ZPIECE = 4
        ZEARLY = 2
        N_ZERO = -(-ZC // ZPIECE) + 2
        N_LOADS = 2 * 3 + 2 + GA + 3 + 1

        @block.sync
        def _(sp):
            sp.wait_ge(s_pad, 1)
            edge_loads(sp, dst_i[:, :], dst, s_edges)
            edge_loads(sp, idx[:, 0, :], src, s_edges)
            sp.wait_ge(s_padf, 1)
            edge_loads(sp, unit[:, :, :].rearrange("p t c -> p (t c)"), attr3, s_feat)
            edge_loads(sp, wn, weight, s_feat)
            edge_loads(sp, emb[:, :, :].rearrange("p t c -> p (t c)"), attr10, s_feat)
            border = dst[0:(P - 1) * T].rearrange("(p n) -> p n", n=T)[:, T - 1:T]
            sp.dma_start(edge_i[1:P, 0:1], border, allow_slow_non_contiguous=True).then_inc(s_borders, 16)
            border = dst[T:(P - 1) * T].rearrange("(p n) -> p n", n=T)[:, 0:1]
            sp.dma_start(edge_i[0:P - 2, 1:2], border, allow_slow_non_contiguous=True).then_inc(s_borders, 16)
            sp.dma_start(edge_i[P - 2:P - 1, 1:2],
                         dst[(P - 1) * T:(P - 1) * T + 1].rearrange("(p n) -> p n", n=1)).then_inc(s_borders, 16)
            xrows = x[0:P * RPP, :].rearrange("(p r) f -> p (r f)", p=P)
            orows = out[0:P * RPP, :].rearrange("(p r) f -> p (r f)", p=P)

            def chunk(ap, g, n):
                if isinstance(g, int):
                    return ap[:, g * DR * FEAT:(g * DR + n) * FEAT]
                return ap[:, bass.ds(g * (DR * FEAT), n * FEAT)]

            def slot(b, n):
                return xin[:, b, 0:n, :].rearrange("p r f -> p (r f)")

            for b in range(2):
                sp.dma_start(slot(b, DR), chunk(xrows, b, DR)).then_inc(s_xl[b], 16)
            sp.wait_ge(s_zset, 1)
            pieces = 0
            for c in range(0, ZC, ZPIECE):
                n = min(ZPIECE, ZC - c)
                if pieces == ZEARLY:
                    sp.wait_ge(s_w2p, 1)
                    for turn, parts in enumerate(((0, 0, 0, 1), (2, 1, 1))):
                        for place, part in enumerate(parts):
                            sp.dma_start(w_s[place * SC:(place + 1) * SC, turn, :, :],
                                         w2s_part[:, part]).then_inc(s_w2, 16)
                    for place, part in enumerate((0, 0, 1, 1, 2, 0)):
                        sp.dma_start(w_v[place * VU:(place + 1) * VU, :, :], w2v_part[:, part]).then_inc(s_w2, 16)
                sp.dma_start(agg[c * P * ZR:(c + n) * P * ZR, :].rearrange("(c p a) f -> p c (a f)", c=n, p=P),
                             zeros[:, None, :].to_broadcast([P, n, ZR * FEAT])).then_inc(s_zfill, 16)
                pieces += 1
                sp.wait_ge(s_zfill, 16 * pieces)
            sp.dma_start(agg[ZC * P * ZR:ZC * P * ZR + P * ZREST, :].rearrange("(p a) f -> p (a f)", p=P),
                         zeros[:, 0:ZREST * FEAT]).then_inc(s_zfill, 16)
            sp.dma_start(agg[N - ZREM:N, :], zeros[0:ZREM, 0:FEAT]).then_inc(s_zfill, 16)

            def store(g, b, n):
                hold(sp, "sp", (s_ddone, g + 1))
                sp.dma_start(chunk(orows, g, n), slot(b, n)).then_inc(s_dst, 16)

            with sp.Fori(0, ITA - 2) as i:
                for b in range(2):
                    g = i * 2 + b
                    store(g, b, DR)
                    hold(sp, "sp", (s_dst, (g + 1) * 16))
                    sp.dma_start(slot(b, DR), chunk(xrows, g + 2, DR)).then_inc(s_xl[b], 16)
            store(NGA - 4, 0, DR)
            sp.wait_ge(s_dst, (NGA - 3) * 16)
            sp.dma_start(slot(0, DR), chunk(xrows, NGA - 2, DR)).then_inc(s_xl[0], 16)
            store(NGA - 3, 1, DR)
            sp.wait_ge(s_dst, (NGA - 2) * 16)
            sp.dma_start(slot(1, DLAST), chunk(xrows, NGA - 1, DLAST)).then_inc(s_xl[1], 16)
            sp.dma_start(xin[0:DREM, 1, DLAST, :], x[P * RPP:N, :]).then_inc(s_xl[1], 16)
            store(NGA - 2, 0, DR)
            store(NGA - 1, 1, DLAST)
            sp.dma_start(out[P * RPP:N, :], xin[0:DREM, 1, DLAST, :]).then_inc(s_dst, 16)
            sp.wait_ge(s_dst, (NGA + 1) * 16)

        @block.gpsimd
        def _(pool):
            nc.gpsimd.memset(ident[:], 0.0).then_inc(s_id0, 1)
            pool.wait_ge(s_id0, 1)
            nc.gpsimd.affine_select(out=ident[:], in_=ident[:], compare_op=ALU.not_equal, fill=1.0, base=0,
                                    pattern=[[-1, P]], channel_multiplier=1).then_inc(s_id, 1)
            pool.wait_ge(s_id, 1)
            nc.gpsimd.tensor_copy(identb[:], ident[:]).then_inc(s_id, 1)

            def gathers(g, b):
                hold(pool, "pool", (s_istg, g + 1), (s_rawd, g + 1), (s_rawa, g + 1))
                for t in range(GA):
                    for side in range(2):
                        nc.gpsimd.indirect_dma_start(
                            raw[:, b, t, side, :], None, x,
                            bass.IndirectOffsetOnAxis(ap=idx_ring[:, b, side, t:t + 1], axis=0)
                        ).then_inc(s_gath[b], 16)

            def scatters(g, b):
                hold(pool, "pool", (s_rows, g + 1))
                for t in range(GA):
                    nc.gpsimd.indirect_dma_start(
                        agg, bass.IndirectOffsetOnAxis(ap=sidx_ring[:, b, t:t + 1], axis=0),
                        row_ring[:, b, t, :], None, bounds_check=N - 1, oob_is_err=False
                    ).then_inc(s_scat, 16)

            def scattered(g):
                pool.wait_ge(s_scat, (g + 1) * (16 * GA))
                pool.sem_inc(s_rfree, 1)

            pool.sem_inc(s_rfree, 2)
            for g in range(4):
                gathers(g, g % 2)
            pool.wait_ge(s_zfill, 16 * N_ZERO)
            scatters(0, 0)
            with pool.Fori(2, ITA - 1) as i:
                for b in range(2):
                    g = i * 2 + b
                    gathers(g, b)
                    scattered(g - LAG - 1)
                    scatters(g - LAG, (b + LAG) % 2)
            gathers(NGA - 2, 0)
            scattered(NGA - 3 - LAG)
            gathers(NGA - 1, 1)
            for g in range(NGA - 2 - LAG, NGA):
                scatters(g, g % 2)
                scattered(g)
            pool.wait_ge(s_fix, 1)
            nc.gpsimd.indirect_dma_start(agg, bass.IndirectOffsetOnAxis(ap=fixidx[:, 0:1], axis=0),
                                         fixrow[:], None, bounds_check=N - 1, oob_is_err=False
                                         ).then_inc(s_fixd, 16)
            pool.wait_ge(s_fixd, 16)

            with pool.Fori(0, ITB) as i:
                for s in range(NSB):
                    k = i * NSB + s
                    hold(pool, "pool", (s_istgb, k + 1), (s_agread, k + 1))
                    for t in range(GB):
                        nc.gpsimd.indirect_dma_start(
                            agg_ring[:, s, t, :], None, agg,
                            bass.IndirectOffsetOnAxis(ap=idx_ring_b[:, s, t:t + 1], axis=0)
                        ).then_inc(s_gb[s], 16)

            pool.wait_ge(s_dst, (NGA + 1) * 16)
            pool.sem_inc(s_ofree, NSB)

            def out_scatters(i, first):
                for s in range(NSB):
                    k = i * NSB + s
                    if not first:
                        pool.wait_ge(s_osc[s], i * (16 * GB))
                        pool.sem_inc(s_ofree, 1)
                    hold(pool, "pool", (s_orow, k + 1), (s_sstg, k + 1))
                    for t in range(GB):
                        nc.gpsimd.indirect_dma_start(
                            out, bass.IndirectOffsetOnAxis(ap=sidx_ring_b[:, s, t:t + 1], axis=0),
                            out_ring[:, s, t, :], None, bounds_check=N - 1, oob_is_err=False
                        ).then_inc(s_osc[s], 16)

            out_scatters(0, True)
            with pool.Fori(1, ITB) as i:
                out_scatters(i, False)
            pool.wait_ge(s_fix, 2)
            nc.gpsimd.indirect_dma_start(out, bass.IndirectOffsetOnAxis(ap=fixidx[:, 0:1], axis=0),
                                         fixrow[:], None, bounds_check=N - 1, oob_is_err=False
                                         ).then_inc(s_last, 16)
            for s in range(NSB):
                pool.wait_ge(s_osc[s], ITB * 16 * GB)
            pool.wait_ge(s_last, 16)

        @block.scalar
        def _(act):
            act.sem_inc(s_rawa, 2)
            act.sem_inc(s_mfree, 1)
            act.wait_ge(s_wz, 1)
            loads = []

            def load(dest, source):
                act.dma_start(dest, source).then_inc(s_wl, 16)
                loads.append(1)

            w2_rows = W2.rearrange("j (i u w) -> i u j w", i=7, w=MOUT)
            WA_S, WB_S, WA_G, WB_G, WC, WD, WE = range(7)
            load(w2d, w2_rows[WD])
            load(w2e, w2_rows[WE])
            for rows, plan in ((slice(0, VU), (WA_S, WA_G, WC)), (slice(VU, SC), (WB_S, WB_G, WE))):
                for col, which in enumerate(plan):
                    load(w2s[rows, :, col * MOUT:(col + 1) * MOUT], w2_rows[which])
            for t in range(GA):
                load(w1bd[t * EMB:(t + 1) * EMB, t * HID:(t + 1) * HID], W1)
            for a, w in enumerate((Wq, Wk, Wv)):
                load(wqk[:, a, :], w.rearrange("h f o -> (h f) o"))
            load(wout, Wout)
            assert len(loads) == N_LOADS

            def stage_indices(g, b):
                return nc.scalar.copy(idx_ring[:, b, :, :],
                                      idx[:, :, g * GA:(g + 1) * GA] if isinstance(g, int)
                                      else idx[:, :, bass.ds(g * GA, GA)]).then_inc(s_istg, 1)


            act.wait_ge(s_vsq, 1)
            nc.scalar.activation(length, length2, ACT.Sqrt).then_inc(s_vstd, 1)

            act.wait_ge(s_wT, 1)
            nc.scalar.copy(wqkvT, turnA[0:FEAT, 0:3 * P].rearrange("p (a e) -> p a e", a=3)).then_inc(s_wTs, 1)
            act.wait_ge(s_gps, 1)
            nc.scalar.activation(gu[:, 0, :], turnB[0:FEAT, 0:P], ACT.Copy, scale=float(FEAT) ** -0.5)
            nc.scalar.activation(gu[:, 1, :], turnB[0:FEAT, P:2 * P], ACT.Copy,
                                 scale=1.0 / HEADS).then_inc(s_gsb, 1)
            act.wait_ge(s_gsb, 1)
            for t in range(BT):
                act.dma_start(gbd[t * FEAT:(t + 1) * FEAT, t, :], gu[:, 0, :]).then_inc(s_gbd, 16)
                act.dma_start(ubd[t * FEAT:(t + 1) * FEAT, t, :], gu[:, 1, :]).then_inc(s_gbd, 16)

            def cols(ap, start, n, axis_len=None):
                return ap[:, start:start + n] if isinstance(start, int) else ap[:, bass.ds(start, n)]

            def stage_emb(g, b):
                nc.scalar.copy(emb_blk[:, b].rearrange("p (t c) -> p t c", c=EMB),
                               cols(emb, g * GA, GA)).then_inc(s_embB, 1)

            def take_rows(g, b, turn):
                nc.scalar.copy(sameT[:, b, :, 1:], cols(same, g * GA, GA)[:, None, :].to_broadcast(
                    [P, FEAT, GA])).then_inc(s_same, 1)
                hold(act, "act", (s_gath[b], turn * (16 * 2 * GA)))
                nc.scalar.copy(cols(xsd, g * GA, GA), raw[:, b]).then_inc(s_rawa, 1)
                stage_indices(g + 2, b)

            def squares(n, gathered, dense):
                act.wait_ge(s_cen, n)
                if gathered:
                    nc.scalar.activation(pos, cen.rearrange("p (t s) f -> p t s f", s=2), ACT.Relu)
                    last = nc.scalar.activation(sqr, cen, ACT.Square)
                if dense:
                    last = nc.scalar.activation(dsqr[:], dcen[:], ACT.Square)
                last.then_inc(s_sq, 1)

            def deviation(n):
                act.wait_ge(s_var, n)
                nc.scalar.activation(stat[:, 2, :], stat[:, 1, :], ACT.Sqrt, bias=eps[:, 0:1],
                                     scale=1.0 / FEAT).then_inc(s_std, 1)

            def take_emb(g):
                act.wait_ge(s_embT, g + 1)
                nc.scalar.copy(embT, small[0:GA * EMB, 0:P]).then_inc(s_embS, 1)

            def hidden(g, b):
                act.wait_ge(s_hps, g + 1)
                nc.scalar.activation(hid[:, b].rearrange("p t j -> p (t j)"), small[:, P:P + GA * HID], ACT.Relu,
                                     scale=2.0 ** 0.5 / (4 * EMB ** 0.5)).then_inc(s_hid, 1)

            def turned(g, pairs):
                for pair in pairs:
                    n = 2 if pair < 3 else 1
                    bank = (turnA, turnB)[pair % 2][:, :].bitcast(BF16).rearrange("c (t a e) -> c t a e", t=2, a=4)
                    act.wait_ge(s_turn, g * 4 + pair + 1)
                    nc.scalar.copy(stackT_s[:, 2 * pair:2 * pair + n, :], bank[:, 0:n, 0, :])
                    nc.scalar.copy(stackT_v[:, 2 * pair:2 * pair + n],
                                   bank[0:6 * VU, 0:n, 1:4, :]).then_inc(s_turned, 1)

            def multiply(g, b):
                act.wait_ge(s_tens, g * GA + (TACT + 1))
                bank = tens[(b + TACT) % 2][:, :].rearrange("p (a c) -> p a c", a=2)
                for j in range(HID):
                    last = nc.scalar.activation(prod[:, 2 * TACT:2 * TACT + 2, j, :], bank[:, :, j * OG:(j + 1) * OG],
                                                ACT.Copy, scale=hid[:, b, TACT, j:j + 1])
                last.then_inc(s_tact, 1)

            def split_first(n):
                act.wait_ge(s_val, n)
                nc.scalar.copy(stack_s[:, :, 0:4:3, :], val_s[:, :, None, :].to_broadcast([P, GA, 2, SC]))
                nc.scalar.copy(stack_v[:, :, 0:6:2, :],
                               val_v.rearrange("p t k u -> p (t k) u")[:, :, None, :].to_broadcast(
                                   [P, GA * 3, 3, VU])).then_inc(s_part1, 1)

            def split_second(n):
                act.wait_ge(s_rest1, n)
                nc.scalar.copy(stack_s[:, :, 1, :], rest_s)
                nc.scalar.copy(stack_v[:, :, 1:4:2, :],
                               rest_v[:, :, None, :].to_broadcast([P, GA * 3, 2, VU])).then_inc(s_part2, 1)

            def first_outputs(g):
                act.wait_ge(s_psum, g + 1)
                nc.scalar.copy(outs[:, 0:TPE], sums[:, 0:TPE * OUTS].rearrange("p (t o) -> p t o", t=TPE)
                               ).then_inc(s_outc, 1)

            def gates(g):
                act.wait_ge(s_outc, g + 2)
                act.wait_ge(s_outs, g + 1)
                nc.scalar.activation(gate[:, 0], outs[:, :, 0:2 * MOUT], ACT.Tanh).then_inc(s_tanh, 1)

            def stage_rows(g, b):
                hold(act, "act", (s_run, g + 1), (s_rfree, g + 1))
                sums = runT[:, b, :, 1:].rearrange("p f t -> p t f")
                nc.scalar.copy(cols(msg, g * GA, GA), msgT[:, :, 1:].rearrange("p f t -> p t f"))
                nc.scalar.copy(cols(run, g * GA + 1, GA), sums).then_inc(s_mfree, 1)
                nc.scalar.copy(row_ring[:, b], sums)
                nc.scalar.copy(sidx_ring[:, b], cols(sidx, g * GA, GA)).then_inc(s_rows, 1)

            stage_emb(0, 0)
            take_rows(0, 0, 1)
            squares(1, True, False)
            deviation(1)
            split_first(1)
            split_second(1)
            take_emb(0)
            hidden(0, 0)
            turned(0, range(4))
            squares(2, True, True)

            def layer0(i, b, last, squared):
                g = i * 2 + b
                if not last:
                    deviation(g + 2)
                    stage_emb(g + 1, 1 - b)
                multiply(g, b)
                if not last:
                    take_emb(g + 1)
                    split_first(g + 2)
                    take_rows(g + 1, 1 - b, i + 1 + b)
                    split_second(g + 2)
                    hidden(g + 1, 1 - b)
                first_outputs(g)
                gates(g)
                if not last:
                    turned(g + 1, range(4))
                if squared:
                    squares(g + 3, True, True)
                stage_rows(g, b)

            with act.Fori(0, ITA - 1) as i:
                for b in range(2):
                    layer0(i, b, False, True)
            layer0(ITA - 1, 0, False, False)
            layer0(ITA - 1, 1, True, False)

            def stage_src(k, s):
                return nc.scalar.copy(idx_ring_b[:, s, :], cols(idx[:, 0, :], k * GB, GB)).then_inc(s_istgb, 1)

            for s in range(NSB):
                stage_src(s, s)

            act.wait_ge(s_carried, 1)
            for f in range(FEAT):
                last = nc.scalar.activation(msg[:, :, f], first_run[:], ACT.Copy, scale=carry[:, 0, f:f + 1])
            last.then_inc(s_first, 1)

            squares(NGA + 1, False, True)
            deviation(NGA + 1)

            def square(k, s):
                act.wait_ge(s_bc, k + 1)
                nc.scalar.activation(q1s[:, s % 2], c1s[:, s % 2], ACT.Square).then_inc(s_bq, 1)

            def stage_rows_of(k, s, rows, staged):
                nc.scalar.copy(rows_blk[:, s % 2].rearrange("p (t f) -> p t f", f=FEAT),
                               cols(rows, k * GB, GB)).then_inc(staged, 1)

            def take_turned(k, s, turned, taken):
                act.wait_ge(turned, k + 1)
                nc.scalar.copy(rowsT[:, s % 2, 0, :], turnA[:, 0:P])
                nc.scalar.copy(rowsT[0:(GB - BT) * FEAT, s % 2, 1, :],
                               turnA[0:(GB - BT) * FEAT, P:2 * P]).then_inc(taken, 1)

            act.sem_inc(s_saved, 2)
            with act.Fori(0, ITB) as i:
                hold(act, "act", (s_dc, i + 1))
                nc.scalar.activation(cols(back, i * HT, HT), cols(msg, i * HT, HT), ACT.Square).then_inc(s_dq, 1)
                act.wait_ge(s_dv, i + 1)
                nc.scalar.activation(seg_f[:, 2, 0:HT], seg_f[:, 1, 0:HT], ACT.Sqrt, bias=eps[:, 0:1],
                                     scale=1.0 / FEAT).then_inc(s_dd, 1)
                square(i * NSB, 0)
                hold(act, "act", (s_h1d, i + 1))
                for s in range(2):
                    stage_rows_of(i * NSB + s, s, h1d, s_hdB)
                take_turned(i * NSB, 0, s_hdT, s_hdS)
                for s in range(NSB):
                    k = i * NSB + s
                    if s + 1 < NSB:
                        take_turned(k + 1, s + 1, s_hdT, s_hdS)
                    if s + 2 < NSB:
                        stage_rows_of(k + 2, s, h1d, s_hdB)
                    act.wait_ge(s_bv, k + 1)
                    nc.scalar.activation(stat_b[:, s % 2, 2, :], stat_b[:, s % 2, 1, :], ACT.Sqrt, bias=eps[:, 0:1],
                                         scale=1.0 / FEAT).then_inc(s_bd, 1)
                    if s + 1 < NSB:
                        square(k + 1, s + 1)
                    hold(act, "act", (s_gb[s], (i + 1) * (16 * GB)))
                    stage_src(k + NSB, s)
                    hold(act, "act", (s_bh, k + 1))
                    nc.scalar.copy(cols(h1s_rows, k * GB, GB), h1s[:, s % 2]).then_inc(s_saved, 1)

            act.wait_ge(s_sm, 1)
            nc.scalar.activation(seg_m, seg_b, ACT.Exp).then_inc(s_e, 1)

            act.wait_ge(s_hdT, NGB)
            act.wait_ge(s_saved, NGB + 2)
            with act.Fori(0, ITB) as i:
                for s in range(2):
                    stage_rows_of(i * NSB + s, s, h1s_rows, s_hvB)
                take_turned(i * NSB, 0, s_hvT, s_hvS)
                for s in range(NSB):
                    k = i * NSB + s
                    if s + 1 < NSB:
                        take_turned(k + 1, s + 1, s_hvT, s_hvS)
                    if s + 2 < NSB:
                        stage_rows_of(k + 2, s, h1s_rows, s_hvB)
                    hold(act, "act", (s_ofree, k + 1))
                    nc.scalar.copy(sidx_ring_b[:, s, :], cols(sidx, k * GB, GB)).then_inc(s_sstg, 1)
                    hold(act, "act", (s_yfree, k + 1))
                    nc.scalar.copy(yflagT[:, s % 2, :, 1:], cols(same, k * GB, GB)[:, None, :].to_broadcast(
                        [P, FEAT, GB])).then_inc(s_yflag, 1)

        @block.tensor
        def _(pe):
            pe.wait_ge(s_id, 2)
            pe.wait_ge(s_cross, 1)
            for a in range(3):
                mm = nc.tensor.transpose(small[0:FEAT, a * P:(a + 1) * P], crossing[:, a, :], ident[:])
            mm.then_inc(s_crossT, 1)
            pe.wait_ge(s_wl, 16 * N_LOADS)
            for a in range(3):
                mm = nc.tensor.transpose(turnA[0:FEAT, a * P:(a + 1) * P], wqk[:, a, :], ident[:])
            mm.then_inc(s_wT, 1)
            pe.wait_ge(s_wTs, 1)
            for h in range(HEADS):
                w = slice(h * FEAT, (h + 1) * FEAT)
                nc.tensor.matmul(turnB[0:FEAT, w], wqkvT[:, 0, w], wqkvT[:, 1, w], start=True, stop=True)
                mm = nc.tensor.matmul(turnB[0:FEAT, P + h * FEAT:P + (h + 1) * FEAT], wqkvT[:, 2, w], wout,
                                      start=True, stop=True)
            mm.then_inc(s_gps, 1)
            pe.wait_ge(s_flags, 1)
            pe.wait_ge(s_gsb, 1)
            pe.wait_ge(s_feat, 16 * 9)
            pe.wait_ge(s_w2, 16 * 13)

            def turn_emb(g, b):
                if not (isinstance(g, int) and g == 0):
                    pe.wait_ge(s_hid, g)
                pe.wait_ge(s_embB, g + 1)
                nc.tensor.transpose(small[0:GA * EMB, 0:P], emb_blk[:, b], ident[:]).then_inc(s_embT, 1)

            def hidden_product(g):
                pe.wait_ge(s_embS, g + 1)
                nc.tensor.matmul(small[:, P:P + GA * HID], embT, w1bd[:], start=True, stop=True).then_inc(s_hps, 1)

            def turn_channels(g):
                pe.wait_ge(s_chan, g + 1)
                for t in range(GA):
                    pair = t // 2
                    bank = (turnA, turnB)[pair % 2][:, :].bitcast(BF16).rearrange("c (t a e) -> c t a e", t=2, a=4)
                    if t in (4, 6):
                        pe.wait_ge(s_turned, g * 4 + pair - 1)
                    nc.tensor.transpose(bank[:, t % 2, 0, :], stack_s[:, t].rearrange("p a c -> p (a c)"), identb[:])
                    for k in range(3):
                        mm = nc.tensor.transpose(bank[0:6 * VU, t % 2, 1 + k, :],
                                                 stack_v[:, 3 * t + k].rearrange("p a c -> p (a c)"), identb[:])
                    if t % 2 or t == GA - 1:
                        mm.then_inc(s_turn, 1)

            def sum_part(g, part):
                if part == 0:
                    pe.wait_ge(s_tfree, g * VT + (TPE + 1))
                    pe.wait_ge(s_tact, g + 1)
                    pe.wait_ge(s_outc, g + 1)
                for j in range(part * HID // 4, (part + 1) * HID // 4):
                    mm = nc.tensor.matmul(sums[:, 0:TPE * OUTS].rearrange("p (c o) -> p c o", o=OG), ident[:],
                                          prod[:, 0:2 * TPE, j, :], start=(j == 0), stop=(j == HID - 1))
                if part == 3:
                    mm.then_inc(s_psum, 1)

            def products(g, b, more):
                for t in range(GA):
                    n = g * GA + t
                    if t % 2 == 0:
                        pe.wait_ge(s_turned, g * 4 + (t // 2 + 1))
                    if t == TACT + 2:
                        pe.wait_ge(s_tact, g + 1)
                    else:
                        pe.wait_ge(s_tfree, g * VT + (t + 1 if t < TACT + 2 else t))
                    bank = tens[(b + t) % 2]
                    for turn in range(2):
                        nc.tensor.matmul(bank[:, 0:HID * OG], stackT_s[:, t, :],
                                         w_s[:, turn].rearrange("c j o -> c (j o)"), start=(turn == 0),
                                         stop=(turn == 1))
                    vec = bank[:, 512:512 + HID * OG].rearrange("p (j o) -> p j o", o=OG)
                    for k in range(3):
                        mm = nc.tensor.matmul(vec[:, :, k * MOUT:(k + 1) * MOUT], stackT_v[:, t, k, :], w_v[:],
                                              start=True, stop=True)
                    mm.then_inc(s_tens, 1)
                    for part in {5: (0,), 6: (1, 2, 3)}.get(t, ()):
                        sum_part(g, part)
                    if more and t == TACT:
                        turn_emb(g + 1, 1 - b)
                    if more and t == TACT + 2:
                        hidden_product(g + 1)

            pe.sem_inc(s_outc, 1)
            turn_emb(0, 0)
            hidden_product(0)
            turn_channels(0)
            with pe.Fori(0, ITA - 1) as i:
                for b in range(2):
                    products(i * 2 + b, b, True)
                    turn_channels(i * 2 + b + 1)
            products(NGA - 2, 0, True)
            turn_channels(NGA - 1)
            products(NGA - 1, 1, False)

            def cross(n, done):
                pe.wait_ge(s_ends, done + 1)
                nc.tensor.transpose(small[0:n, 0:P], ends[:, 0, 0:n], ident[:])
                nc.tensor.transpose(small[0:n, P:2 * P], ends[:, 1, 0:n], ident[:]).then_inc(s_endT, 1)
                pe.wait_ge(s_carT, done + 1)
                nc.tensor.transpose(small[:, 2 * P:2 * P + n], carryT[0:n, 0, :], ident[0:n, 0:n])
                nc.tensor.transpose(small[:, 2 * P + FEAT:2 * P + FEAT + n], carryT[0:n, 1, :],
                                    ident[0:n, 0:n]).then_inc(s_car, 1)

            cross(FEAT, 0)

            def turn_rows(k, s, staged, turned):
                pe.wait_ge(staged, k + 1)
                nc.tensor.transpose(turnA[:, 0:P], rows_blk[:, s % 2, 0:BT * FEAT], ident[:])
                nc.tensor.transpose(turnA[0:(GB - BT) * FEAT, P:2 * P], rows_blk[:, s % 2, BT * FEAT:],
                                    ident[:]).then_inc(turned, 1)

            def head_products(weights, staged, turned, taken, free, ready):
                rest = (GB - BT) * FEAT
                with pe.Fori(0, ITB) as i:
                    turn_rows(i * NSB, 0, staged, turned)
                    for s in range(NSB):
                        k = i * NSB + s
                        pe.wait_ge(taken, k + 1)
                        if s + 1 < NSB:
                            turn_rows(k + 1, s + 1, staged, turned)
                        pe.wait_ge(free, k + 1)
                        nc.tensor.matmul(tens[s % 2][:, 0:BT * P], rowsT[:, s % 2, 0, :],
                                         weights[:, :, :].rearrange("p t e -> p (t e)"), start=True, stop=True)
                        nc.tensor.matmul(tens[s % 2][:, BT * P:GB * P], rowsT[0:rest, s % 2, 1, :],
                                         weights[0:rest, 0:GB - BT, :].rearrange("p t e -> p (t e)"),
                                         start=True, stop=True).then_inc(ready, 1)

            pe.wait_ge(s_gbd, 16 * 2 * BT)
            head_products(gbd, s_hdB, s_hdT, s_hdS, s_qfree, s_q)
            cross(HEADS, 1)
            cross(HEADS, 2)
            head_products(ubd, s_hvB, s_hvT, s_hvS, s_vfree, s_v)
            cross(FEAT, 3)

        @block.vector
        def _(dve):
            v = nc.vector

            def cols(ap, start, n):
                return ap[:, start:start + n] if isinstance(start, int) else ap[:, bass.ds(start, n)]

            def spread(ap, axis, dims):
                full = [slice(None)] * (len(ap.shape) + 1)
                full[axis] = None
                return ap[tuple(full)].to_broadcast(dims)

            dve.sem_inc(s_rawd, 2)
            q = slice(96, P)
            v.memset(idx[q, 0, TAIL:T], 0)
            v.memset(dst_i[q, TAIL:T], int(BIG)).then_inc(s_pad, 1)
            v.memset(idx[:, :, T:], 0)
            v.memset(edge_i[:], -1)
            v.memset(unit[q, TAIL:T, :], 1.0)
            v.memset(wn[q, TAIL:T], 0.0)
            v.memset(emb[q, TAIL:T, :], 0.0).then_inc(s_padf, 1)
            v.memset(zeros, 0.0).then_inc(s_zset, 1)
            v.memset(w1bd[:], 0.0)
            v.memset(w_s[3 * SC:4 * SC, 1], 0.0)
            v.memset(gbd[:], 0.0)
            v.memset(ubd[:], 0.0).then_inc(s_wz, 1)

            dve.wait_ge(s_edges, 16 * 6)
            v.tensor_copy(dstf[:], dst_i[:])
            v.drain()
            v.tensor_scalar(idx[:, 1, 0:T], dstf[:], float(N - 1), None, ALU.min)
            v.drain()
            for b in range(2):
                v.tensor_copy(idx_ring[:, b], idx[:, :, b * GA:(b + 1) * GA])
            v.drain().then_inc(s_istg, 2)

            v.memset(run[:, 0, :], 0.0)
            v.memset(eps[:], EPS * FEAT * FEAT)
            v.memset(same[:], 0.0)
            v.memset(stat[:], 1.0)
            v.memset(keepT[:], 0.0)
            v.memset(endT[:], 0.0)
            v.memset(runT, 0.0)
            v.memset(sameT, 0.0)
            v.memset(wscale[0:SC], 1.5 ** 0.5 * PW_V)
            v.drain()
            v.memset(wscale[0:VU], PW_V)

            dve.wait_ge(s_feat, 16 * 9)
            v.tensor_tensor(v3, unit, unit, ALU.mult)
            v.tensor_scalar(wn, wn, TANH_GAIN, None, ALU.mult)
            v.drain()
            v.tensor_reduce(length2, v3, AX, ALU.add).then_inc(s_vsq, 1)

            v.tensor_tensor(same[:, 1:T], dstf[:, 1:T], dstf[:, 0:T - 1], ALU.is_equal)
            v.tensor_scalar(first_run[:], dstf[:], dstf[:, 0:1], None, ALU.is_equal)
            v.tensor_scalar(last_run[:], dstf[:], dstf[:, T - 1:T], None, ALU.is_equal)
            dve.wait_ge(s_borders, 16 * 3)
            v.tensor_copy(edge_f[:], edge_i[:])
            v.drain()
            v.tensor_tensor(crossing[:, 0, 0:1], edge_f[:, 0:1], dstf[:, 0:1], ALU.is_equal)
            v.tensor_tensor(crossing[:, 1, 0:1], dstf[:, T - 1:T], edge_f[:, 1:2], ALU.is_equal)
            v.drain()
            v.tensor_copy(crossing[:, 2, :], first_run[:, T - 1:T].to_broadcast([P, FEAT]))
            v.tensor_copy(crossing[:, 0, 1:FEAT], crossing[:, 0, 0:1].to_broadcast([P, FEAT - 1]))
            v.tensor_copy(crossing[:, 1, 1:FEAT], crossing[:, 1, 0:1].to_broadcast([P, FEAT - 1])).then_inc(s_cross, 1)
            goes_on = same_far
            v.tensor_copy(goes_on[:, 0:T - 1], same[:, 1:T])
            v.drain()
            v.tensor_copy(goes_on[:, T - 1:T], crossing[:, 1, 0:1])
            v.drain()
            v.tensor_tensor(goes_on[:, 0:T], goes_on[:, 0:T], first_run[:], ALU.max)
            v.tensor_tensor(fixrow[:, 0:1], crossing[:, 1, 0:1], crossing[:, 2, 0:1], ALU.mult)
            v.drain()
            v.scalar_tensor_tensor(sidx[:], goes_on[:, 0:T], BIG, dstf[:], ALU.mult, ALU.add)
            v.scalar_tensor_tensor(fixidx[:], fixrow[:, 0:1], BIG, dstf[:, 0:1], ALU.mult, ALU.add)

            dve.wait_ge(s_crossT, 1)
            v.tensor_copy(flagT[:], small[0:FEAT, 0:3 * P].rearrange("p (a e) -> p a e", a=3))
            v.drain()
            v.tensor_tensor(keepT[:, 0, 1:P], flagT[:, 0, 1:P], flagT[:, 2, 0:P - 1], ALU.mult)
            v.tensor_tensor(keepT[:, 1, 0:P - 1], flagT[:, 1, 0:P - 1], flagT[:, 2, 1:P], ALU.mult)
            v.drain()
            for a in range(2):
                v.tensor_scalar(farT[:, a, :], flagT[:, a, :], FAR, -FAR, ALU.mult, ALU.add)
                v.tensor_scalar(farT[:, 2 + a, :], keepT[:, a, :], FAR, -FAR, ALU.mult, ALU.add)
            v.drain().then_inc(s_flags, 1)

            dve.wait_ge(s_vstd, 1)
            v.reciprocal(length2, length)
            v.drain()
            v.tensor_tensor(unit, unit, spread(length2, 2, [P, T, 3]), ALU.mult)

            dve.wait_ge(s_wl, 16 * N_LOADS)
            v.tensor_scalar(w2s[:, :, 0:2 * MOUT], w2s[:, :, 0:2 * MOUT], PW_S, None, ALU.mult)
            v.tensor_scalar(w2s[:, :, 2 * MOUT:], w2s[:, :, 2 * MOUT:], wscale[0:SC, 0:1], None, ALU.mult)
            v.tensor_scalar(w2d, w2d, PW_V * 3.0 ** -0.5, None, ALU.mult)
            v.drain()
            v.scalar_tensor_tensor(w2v, w2e, -PW_V * 6.0 ** -0.5, w2d, ALU.mult, ALU.add)
            v.drain()
            for part in range(3):
                for whole, rest, parts in ((w2s, w2s_rest, w2s_part), (w2v, w2v_rest, w2v_part)):
                    v.tensor_copy(parts[:, part], whole if part == 0 else rest)
                v.drain()
                for whole, rest, parts in ((w2s, w2s_rest, w2s_part), (w2v, w2v_rest, w2v_part)):
                    if part < 2:
                        v.tensor_tensor(rest, whole if part == 0 else rest, parts[:, part], ALU.subtract)
                v.drain()
            v.drain().then_inc(s_w2p, 1)

            dve.sem_inc(s_tfree, 2)
            NG2 = 2 * GA

            def rows_of(b_next):
                return raw[:, b_next].rearrange("p t s f -> p (t s) f")

            def row_sums(b_next, turn, b, dense_wait):
                if b_next is not None:
                    hold(dve, "dve", (s_gath[b_next], turn * (16 * 2 * GA)))
                    v.tensor_reduce(stat[:, 0, 0:NG2], rows_of(b_next), AX, ALU.add)
                if b is not None:
                    hold(dve, "dve", (s_xl[b], dense_wait))
                    v.tensor_reduce(stat[:, 0, NG2:NST], xin[:, b], AX, ALU.add)

            def centre(b_next, turn, b, dense_wait):
                if b_next is not None:
                    v.scalar_tensor_tensor(cen, rows_of(b_next), float(FEAT),
                                           spread(stat[:, 0, 0:NG2], 2, [P, NG2, FEAT]),
                                           ALU.mult, ALU.subtract).then_inc(s_rawd, 1)
                if b is not None:
                    v.scalar_tensor_tensor(dcen[:], xin[:, b], float(FEAT),
                                           spread(stat[:, 0, NG2:NST], 2, [P, DR, FEAT]), ALU.mult, ALU.subtract)
                v.drain().then_inc(s_cen, 1)

            def variance(n, gathered, dense):
                dve.wait_ge(s_sq, n)
                if gathered:
                    last = v.tensor_reduce(stat[:, 1, 0:NG2], sqr, AX, ALU.add)
                if dense:
                    last = v.tensor_reduce(stat[:, 1, NG2:NST], dsqr[:], AX, ALU.add)
                v.drain().then_inc(s_var, 1)

            def channels(g):
                scale = stat[:, 3, 0:NG2].rearrange("p (t s) -> p t s", s=2)
                v.tensor_tensor(val_s[:, :, 0:VU].rearrange("p t (s u) -> p t s u", s=2), pos[:, :, :, 0:MOUT],
                                spread(scale, 3, [P, GA, 2, MOUT]), ALU.mult)
                for side in range(2):
                    v.tensor_tensor(val_v[:, :, :, side * MOUT:(side + 1) * MOUT].rearrange("p t k u -> p t u k"),
                                    pos[:, :, side, MOUT:].rearrange("p t (u k) -> p t u k", k=3),
                                    scale[:, :, side:side + 1][:, :, :, None].to_broadcast([P, GA, MOUT, 3]), ALU.mult)
                v.drain()
                v.tensor_tensor(vprod, val_v.rearrange("p t k u -> p t u k"),
                                spread(cols(unit, g * GA, GA), 2, [P, GA, VU, 3]), ALU.mult)
                v.drain()
                v.tensor_reduce(val_s[:, :, VU:], vprod, AX, ALU.add).then_inc(s_val, 1)

            def first_rest(n):
                dve.wait_ge(s_part1, n)
                v.tensor_tensor(rest_s, val_s, stack_s[:, :, 0, :], ALU.subtract)
                v.tensor_tensor(rest_v, val_v.rearrange("p t k u -> p (t k) u"), stack_v[:, :, 0, :],
                                ALU.subtract).then_inc(s_rest1, 1)

            def third_part(n):
                dve.wait_ge(s_part2, n)
                v.tensor_tensor(stack_s[:, :, 2, :], rest_s, stack_s[:, :, 1, :], ALU.subtract)
                v.tensor_tensor(stack_v[:, :, 5, :], rest_v, stack_v[:, :, 1, :], ALU.subtract).then_inc(s_chan, 1)

            def multiply(g, b, t):
                dve.wait_ge(s_tens, g * GA + (t + 1))
                v.tensor_tensor(
                    prod[:, 2 * t:2 * t + 2],
                    tens[(b + t) % 2][:, :].rearrange("p (a c) -> p a c", a=2)[:, :, 0:HID * OG].rearrange(
                        "p a (j o) -> p a j o", o=OG),
                    hid[:, b, t, :][:, None, :, None].to_broadcast([P, 2, HID, OG]), ALU.mult).then_inc(s_tfree, 1)

            def messages(g, b, following):
                v.drain()
                v.tensor_reduce(outs[:, TPE:].rearrange("p t (a o) -> p (t a) o", a=2),
                                prod[:, 2 * TPE:].rearrange("p b j o -> p b o j"), AX, ALU.add).then_inc(s_outs, 1)
                v.tensor_copy(msgT[:, :, 0:1], runT[:, 1 - b, :, GA:])
                v.drain()
                dve.wait_ge(s_outc, g + 2)
                v.tensor_tensor(vmix, spread(outs[:, :, 2 * MOUT:3 * MOUT], 3, [P, GA, MOUT, 3]),
                                spread(cols(unit, g * GA, GA), 2, [P, GA, MOUT, 3]), ALU.mult)
                if following:
                    row_sums(*following)
                v.drain()
                v.tensor_tensor(vmix, vmix, outs[:, :, 3 * MOUT:].rearrange("p t (k w) -> p t w k", k=3), ALU.add)
                hold(dve, "dve", (s_tanh, g + 1))
                v.tensor_tensor(gate[:, 1], gate[:, 0], spread(cols(wn, g * GA, GA), 2, [P, GA, 2 * MOUT]), ALU.mult)
                if following:
                    centre(*following)
                else:
                    v.drain()
                hold(dve, "dve", (s_mfree, g + 1), (s_same, g + 1))
                v.tensor_copy(msgT[:, 0:MOUT, 1:].rearrange("p f t -> p t f"), gate[:, 1, :, 0:MOUT])
                v.tensor_tensor(msgT[:, MOUT:, 1:].rearrange("p (w k) t -> p t w k", k=3), vmix,
                                spread(gate[:, 1, :, MOUT:], 3, [P, GA, MOUT, 3]), ALU.mult)
                v.drain()
                v.tensor_tensor_scan(runT[:, b].rearrange("p f t -> p (f t)"),
                                     sameT[:, b].rearrange("p f t -> p (f t)"),
                                     msgT.rearrange("p f t -> p (f t)"), 0.0, ALU.mult, ALU.add).then_inc(s_run, 1)

            def invert(n):
                dve.wait_ge(s_std, n)
                v.reciprocal(stat[:, 3, :], stat[:, 2, :])
                v.drain()

            def dense_scale():
                v.scalar_tensor_tensor(dcen[:], dcen[:], 0.0, spread(stat[:, 3, NG2:NST], 2, [P, DR, FEAT]),
                                       ALU.max, ALU.mult)

            def dense_add(b):
                v.tensor_tensor(xin[:, b], xin[:, b], dcen[:], ALU.add).then_inc(s_ddone, 1)

            def layer0(i, b, last, following):
                g = i * 2 + b
                dve.wait_ge(s_hid, g + 1)
                for t in range(0, 2):
                    multiply(g, b, t)
                if not last:
                    variance(g + 2, True, True)
                multiply(g, b, 2)
                if not last:
                    invert(g + 2)
                    channels(g + 1)
                multiply(g, b, 4)
                if not last:
                    dense_scale()
                multiply(g, b, 5)
                if not last:
                    first_rest(g + 2)
                if not last:
                    v.drain()
                    dense_add(b)
                multiply(g, b, 6)
                if not last:
                    third_part(g + 2)
                messages(g, b, following)

            def round_of(i, b):
                return 1 - b, i + 1 + b, b, (i + 1) * 16

            row_sums(0, 1, None, None)
            v.drain()
            centre(0, 1, None, None)
            dve.wait_ge(s_gbd, 16 * 2 * BT)
            variance(1, True, False)
            invert(1)
            channels(0)
            first_rest(1)
            third_part(1)
            row_sums(*round_of(0, 0))
            v.drain()
            centre(*round_of(0, 0))
            with dve.Fori(0, ITA - 1) as i:
                layer0(i, 0, False, round_of(i, 1))
                layer0(i, 1, False, round_of(i + 1, 0))
            layer0(ITA - 1, 0, False, None)
            layer0(ITA - 1, 1, True, None)

            dve.wait_ge(s_mfree, NGA + 1)
            v.drain()
            v.memset(back[:, T - 1, :], 0.0)
            for f in range(FEAT):
                v.tensor_tensor_scan(back[:, T - 2::-1, f], msg[:, T - 1:0:-1, f], same[:, T - 1:0:-1], 0.0,
                                     ALU.add, ALU.mult)

            def cross(n, done, far):
                v.drain().then_inc(s_ends, 1)
                dve.wait_ge(s_endT, done + 1)
                if far:
                    v.memset(endT[0:n, 0, 0:1], -FAR)
                    v.memset(endT[0:n, 1, P - 1:P], -FAR)
                f0, f1 = (farT[0:n, 0], farT[0:n, 1]) if far else (flagT[0:n, 0], flagT[0:n, 1])
                k0, k1 = (farT[0:n, 2], farT[0:n, 3]) if far else (keepT[0:n, 0], keepT[0:n, 1])
                op = ALU.add if far else ALU.mult
                v.tensor_tensor(endT[0:n, 0, 1:P], f0[:, 1:P], small[0:n, 0:P - 1], op)
                v.tensor_tensor(endT[0:n, 1, 0:P - 1], f1[:, 0:P - 1], small[0:n, P + 1:2 * P], op)
                v.drain()
                init = -FAR if far else 0.0
                op1 = ALU.max if far else ALU.add
                v.tensor_tensor_scan(carryT[0:n, 0, :], k0, endT[0:n, 0, :], init, op, op1)
                v.tensor_tensor_scan(carryT[0:n, 1, ::-1], k1[:, ::-1], endT[0:n, 1, ::-1], init, op, op1)
                v.drain().then_inc(s_carT, 1)
                dve.wait_ge(s_car, done + 1)
                v.tensor_copy(carry[:, :, 0:n], small[:, 2 * P:2 * P + 2 * FEAT].rearrange(
                    "p (a n) -> p a n", a=2)[:, :, 0:n])
                if far:
                    v.memset(endT[0:n, 0, 0:1], 0.0)
                    v.memset(endT[0:n, 1, P - 1:P], 0.0)
                v.drain()

            v.drain()
            v.tensor_copy(ends[:, 0, :], run[:, T, :])
            v.tensor_tensor(ends[:, 1, :], back[:, 0, :], msg[:, 0, :], ALU.add)
            cross(FEAT, 0, False)
            v.tensor_tensor(fixrow[:], ends[:, 1, :], carry[:, 0, :], ALU.add).then_inc(s_fix, 1)
            dve.sem_inc(s_carried, 1)
            dve.sem_inc(s_agread, NSB)

            for f in range(FEAT):
                v.scalar_tensor_tensor(back[:, :, f], last_run[:], carry[:, 1, f:f + 1], back[:, :, f], ALU.mult,
                                       ALU.add)
            v.drain()

            row_sums(None, None, 1, (ITA + 1) * 16)
            v.drain()
            centre(None, None, 1, None)
            variance(NGA + 1, False, True)
            invert(NGA + 1)
            dense_scale()
            v.drain()
            dense_add(1)

            dve.sem_inc(s_qfree, 2)
            s0, s1, s2, s3 = (seg_f[:, a, 0:HT] for a in range(4))
            dve.wait_ge(s_rows, NGA)
            v.tensor_scalar(same_far[:], same[:], FAR, -FAR, ALU.mult, ALU.add)
            v.tensor_scalar(first_far, first_run[:], FAR, -FAR, ALU.mult, ALU.add)
            v.tensor_scalar(last_far, last_run[:], FAR, -FAR, ALU.mult, ALU.add)
            v.memset(yfirst, 0.0)

            def source_rows(i, s):
                k = i * NSB + s
                hold(dve, "dve", (s_gb[s], (i + 1) * (16 * GB)))
                v.tensor_tensor(x1s[:, s % 2], agg_ring[:, s], xsd[:, bass.ds(k * GB, GB), 0, :],
                                ALU.add).then_inc(s_agread, 1)
                v.drain()
                v.tensor_reduce(stat_b[:, s % 2, 0, :], x1s[:, s % 2], AX, ALU.add)
                v.drain()
                v.scalar_tensor_tensor(c1s[:, s % 2], x1s[:, s % 2], float(FEAT),
                                       spread(stat_b[:, s % 2, 0, :], 2, [P, GB, FEAT]), ALU.mult,
                                       ALU.subtract).then_inc(s_bc, 1)

            def destination_rows(i):
                x1 = xsd[:, bass.ds(i * HT, HT), 1, :]
                v.tensor_tensor(x1, x1, run[:, bass.ds(i * HT + 1, HT), :], ALU.add)
                v.drain()
                v.tensor_tensor(x1, x1, cols(back, i * HT, HT), ALU.add)
                v.drain()
                dve.wait_ge(s_first, 1)
                v.tensor_tensor(x1, x1, cols(msg, i * HT, HT), ALU.add)
                v.drain()
                v.tensor_reduce(s0, x1, AX, ALU.add)
                v.drain()
                v.scalar_tensor_tensor(cols(msg, i * HT, HT), x1, float(FEAT), spread(s0, 2, [P, HT, FEAT]),
                                       ALU.mult, ALU.subtract).then_inc(s_dc, 1)
                source_rows(i, 0)
                hold(dve, "dve", (s_dq, i + 1))
                v.tensor_reduce(s1, cols(back, i * HT, HT), AX, ALU.add).then_inc(s_dv, 1)
                dve.wait_ge(s_dd, i + 1)
                v.reciprocal(s3, s2)
                v.drain()
                v.scalar_tensor_tensor(cols(h1d, i * HT, HT), cols(msg, i * HT, HT), 0.0,
                                       spread(s3, 2, [P, HT, FEAT]), ALU.max, ALU.mult).then_inc(s_h1d, 1)

            with dve.Fori(0, ITB) as i:
                destination_rows(i)
                for s in range(NSB):
                    k = i * NSB + s
                    dve.wait_ge(s_bq, k + 1)
                    v.tensor_reduce(stat_b[:, s % 2, 1, :], q1s[:, s % 2], AX, ALU.add).then_inc(s_bv, 1)
                    if s + 1 < NSB:
                        source_rows(i, s + 1)
                    dve.wait_ge(s_bd, k + 1)
                    v.reciprocal(stat_b[:, s % 2, 3, :], stat_b[:, s % 2, 2, :])
                    v.drain()
                    dve.wait_ge(s_saved, k + 1)
                    v.scalar_tensor_tensor(h1s[:, s % 2], c1s[:, s % 2], 0.0,
                                           spread(stat_b[:, s % 2, 3, :], 2, [P, GB, FEAT]), ALU.max,
                                           ALU.mult).then_inc(s_bh, 1)
                    v.drain()
                    dve.wait_ge(s_q, k + 1)
                    v.tensor_tensor(hprod, tens[s % 2][:, 0:GB * P].rearrange("p (t h f) -> p t h f", t=GB, h=HEADS),
                                    spread(h1s[:, s % 2], 2, [P, GB, HEADS, FEAT]), ALU.mult).then_inc(s_qfree, 1)
                    v.drain()
                    v.tensor_reduce(score[:, :, bass.ds(k * GB, GB)].rearrange("p h t -> p t h"), hprod, AX, ALU.add)

            v.drain()
            for h in range(HEADS):
                v.tensor_tensor_scan(seg_f[:, h, :], same_far[:, 0:T], score[:, h, :], -FAR, ALU.add, ALU.max)
                v.tensor_tensor_scan(seg_b[:, h, ::-1], same_far[:, T:0:-1], score[:, h, ::-1], -FAR, ALU.add,
                                     ALU.max)
            v.drain()
            v.tensor_copy(ends[:, 0, 0:HEADS], seg_f[:, :, T - 1])
            v.tensor_copy(ends[:, 1, 0:HEADS], seg_b[:, :, 0])
            v.tensor_tensor(seg_m, seg_f, seg_b, ALU.max)
            cross(HEADS, 1, True)
            for a, at in ((0, first_far), (1, last_far)):
                for h in range(HEADS):
                    v.scalar_tensor_tensor(seg_m[:, h, :], at, carry[:, a, h:h + 1], seg_m[:, h, :], ALU.add, ALU.max)
                v.drain()
            v.tensor_tensor(seg_b, score, seg_m, ALU.subtract).then_inc(s_sm, 1)
            dve.wait_ge(s_saved, NGB + 2)
            v.memset(yrunT, 0.0)
            v.memset(yflagT, 0.0)
            v.drain().then_inc(s_yfree, 2)
            dve.wait_ge(s_e, 1)
            v.memset(seg_b[:, :, T - 1:T], 0.0)
            for h in range(HEADS):
                v.tensor_tensor_scan(seg_f[:, h, :], same[:, 0:T], seg_m[:, h, :], 0.0, ALU.mult, ALU.add)
                v.tensor_tensor_scan(seg_b[:, h, T - 2::-1], seg_m[:, h, T - 1:0:-1], same[:, T - 1:0:-1], 0.0,
                                     ALU.add, ALU.mult)
            v.drain()
            v.tensor_copy(ends[:, 0, 0:HEADS], seg_f[:, :, T - 1])
            v.tensor_tensor(ends[:, 1, 0:HEADS], seg_b[:, :, 0], seg_m[:, :, 0], ALU.add)
            v.drain()
            v.tensor_tensor(seg_b, seg_b, seg_f, ALU.add)
            cross(HEADS, 2, False)
            for a, at in ((0, first_run), (1, last_run)):
                for h in range(HEADS):
                    v.scalar_tensor_tensor(seg_b[:, h, :], at[:], carry[:, a, h:h + 1], seg_b[:, h, :], ALU.mult,
                                           ALU.add)
                v.drain()
            v.drain()

            dve.sem_inc(s_vfree, 2)
            with dve.Fori(0, ITB) as i:
                for s in range(NSB):
                    k = i * NSB + s
                    b = s % 2
                    v.reciprocal(share[:, b], seg_b[:, :, bass.ds(k * GB, GB)])
                    v.drain()
                    v.tensor_tensor(share[:, b], share[:, b], seg_m[:, :, bass.ds(k * GB, GB)], ALU.mult)
                    v.drain()
                    dve.wait_ge(s_v, k + 1)
                    v.tensor_tensor(hprod, tens[b][:, 0:GB * P].rearrange("p (t h f) -> p t h f", t=GB, h=HEADS),
                                    share[:, b].rearrange("p h t -> p t h")[:, :, :, None]
                                    .to_broadcast([P, GB, HEADS, FEAT]), ALU.mult).then_inc(s_vfree, 1)
                    v.tensor_tensor(ysum[:, b], xsd[:, bass.ds(k * GB, GB), 1, :], cols(h1d, k * GB, GB), ALU.add)
                    v.drain()
                    v.tensor_reduce(yrowT[:, :, 1:].rearrange("p f t -> p t f"), hprod.rearrange("p t h f -> p t f h"),
                                    AX, ALU.add)
                    v.tensor_copy(yrowT[:, :, 0:1], yrunT[:, 1 - b, :, GB:])
                    v.drain()
                    dve.wait_ge(s_yflag, k + 1)
                    v.tensor_tensor_scan(yrunT[:, b].rearrange("p f t -> p (f t)"),
                                         yflagT[:, b].rearrange("p f t -> p (f t)"),
                                         yrowT.rearrange("p f t -> p (f t)"), 0.0, ALU.mult, ALU.add)
                    v.tensor_tensor(ytmp, yrowT[:, :, 1:], spread(first_run[:, bass.ds(k * GB, GB)], 1,
                                                                  [P, FEAT, GB]), ALU.mult)
                    v.drain().then_inc(s_yfree, 1)
                    v.tensor_tensor(yfirst, yfirst, ytmp, ALU.add)
                    hold(dve, "dve", (s_ofree, k + 1))
                    v.tensor_tensor(out_ring[:, s], yrunT[:, b, :, 1:].rearrange("p f t -> p t f"), ysum[:, b],
                                    ALU.add).then_inc(s_orow, 1)
            v.drain()
            v.tensor_copy(ends[:, 0, :], yrunT[:, (NSB - 1) % 2, :, GB])
            v.tensor_reduce(ends[:, 1, :], yfirst, AX, ALU.add)
            v.drain()
            v.tensor_tensor(fixrow[:], x1d[:, 0, :], ends[:, 1, :], ALU.add)
            v.drain()
            v.tensor_tensor(fixrow[:], fixrow[:], h1d[:, 0, :], ALU.add)
            cross(FEAT, 3, False)
            v.tensor_tensor(fixrow[:], fixrow[:], carry[:, 0, :], ALU.add).then_inc(s_fix, 1)


_INS = ['x', 'src', 'dst', 'edge_attr_10', 'edge_attr_3', 'edge_weight', 'L0_gnn_W1', 'L0_gnn_W2',
        'L1_gnn_Wq', 'L1_gnn_Wk', 'L1_gnn_Wv', 'L1_gnn_Wout']


def kernel(**inputs):
    import numpy as _np
    import concourse.bacc as _bacc
    from concourse import mybir as _mybir
    from concourse.bass_utils import run_bass_kernel_spmd as _run

    nc = _bacc.Bacc("TRN2", target_bir_lowering=False, num_devices=1)
    arrays, args = {}, []
    for name in _INS:
        a = _np.ascontiguousarray(inputs[name])
        arrays[f"in_{name}"] = a
        args.append(nc.dram_tensor(f"in_{name}", a.shape, _mybir.dt.from_np(a.dtype), kind="ExternalInput").ap())
    shape = arrays["in_x"].shape
    args.append(nc.dram_tensor("out_dram", shape, _mybir.dt.float32, kind="ExternalOutput").ap())
    build_gnn(nc, *args)
    return _run(nc, [arrays], core_ids=[0]).results[0]["out_dram"]
```
